# Optimizing a Trainium2 kernel written in Bass

```python
import numpy as np
import jax
import jax.numpy as jnp

def _softmax(x, axis=-1):
    return jax.nn.softmax(x, axis=axis)
def _gelu(x):
    return jax.nn.gelu(x, approximate=True)
def _silu(x):
    return jax.nn.silu(x)
def _sigmoid(x):
    return jax.nn.sigmoid(x)
def _layernorm(x, axis=-1, eps=1e-5):
    m = jnp.mean(x, axis=axis, keepdims=True)
    v = jnp.var(x, axis=axis, keepdims=True)
    return (x - m) / jnp.sqrt(v + eps)
def _scatter_add(tgt, idx, src, axis=0):
    return tgt.at[idx].add(src)
def _segment_sum(src, seg, n):
    return jax.ops.segment_sum(src, seg, n)

kernel_name = 'mk_adj_ffn_d1_adj_256_64fb1c'

def setup_inputs(seed: int = 0):
    np.random.seed(seed)
    _w = jnp.asarray
    def _rec_inputs():
        import jax
        import jax.numpy as jnp
        _gk = jax.random.key(seed)
        x = -0.0005146 + 1 * jax.random.normal(jax.random.fold_in(_gk, 1), (8, 2048, 256), jnp.float32)
        _a = jax.random.bernoulli(jax.random.fold_in(_gk, 2), 0.015625, (8, 2048, 2048))
        _a = jnp.logical_or(_a, jnp.swapaxes(_a, -1, -2))
        _a = jnp.logical_or(_a, jnp.eye(2048, dtype=bool))
        adj = _a.astype(jnp.int32)
        return x, adj
    x, adj = _rec_inputs()
    def _L0_gnn_setup():
        import jax, jax.numpy as jnp
        import numpy as np
        B, N, C, OUT, S = (4, 2048, 256, 256, 25)
        DENSITY = 0.008
        key = jax.random.key(seed)
        kA, kX, kW = jax.random.split(key, 3)
        A = jax.random.bernoulli(kA, DENSITY, (B, N, N)).astype(jnp.int32)
        X = jax.random.normal(kX, (B, N, C), dtype=jnp.float32)
        W = jax.random.normal(kW, (2 * C, OUT), dtype=jnp.float32) * np.float32(1.0 / np.sqrt(2 * C))
        b = jnp.zeros((OUT,), dtype=jnp.float32)
        return {'A': A, 'X': X, 'W': W, 'b': b}
    _L0_gnn_all = _L0_gnn_setup()
    _L0_gnn_in = {k: v for k, v in _L0_gnn_all.items() if k in ('W', 'b', )}
    del _L0_gnn_all

    def _L0_ffn_setup():
        import jax, jax.numpy as jnp
        import numpy as np
        H, P, G, NS, K = (8, 64, 64, 64, 3)
        D_INNER = H * P
        CONV_DIM = D_INNER + 2 * NS
        D_IN_PROJ = 2 * D_INNER + 2 * NS + 2 * H

        def _hydra(u, in_w, conv_w, conv_b, dt_bias, A_log, Dp, fcD_w, norm_w, out_w):
            Bt, L, _ = u.shape
            zxbcdt = u @ in_w.T
            z = zxbcdt[..., :D_INNER]
            xBC = zxbcdt[..., D_INNER:D_INNER + CONV_DIM]
            dt = zxbcdt[..., -2 * H:]
            dt = jnp.concatenate([dt[..., :H], jnp.flip(dt[..., H:], axis=1)], axis=0)
            dt = jax.nn.softplus(dt + dt_bias)
            xp = jnp.pad(xBC, ((0, 0), (K - 1, 0), (0, 0)))
            xBC = sum((xp[:, k:k + L, :] * conv_w[:, k] for k in range(K))) + conv_b
            xBC = jax.nn.silu(xBC)
            x = xBC[..., :D_INNER]
            Bm = xBC[..., D_INNER:D_INNER + NS]
            Cm = xBC[..., D_INNER + NS:]
            x_og = x
            x2 = jnp.concatenate([x, jnp.flip(x, 1)], 0).reshape(2 * Bt, L, H, P)
            B2 = jnp.concatenate([Bm, jnp.flip(Bm, 1)], 0)
            C2 = jnp.concatenate([Cm, jnp.flip(Cm, 1)], 0)
            dA = jnp.exp(dt * -jnp.exp(A_log))
            dBx = jnp.einsum('blh,bln,blhp->blhpn', dt, B2, x2)

            def step(h, inp):
                dA_t, dBx_t, C_t = inp
                h = h * dA_t[:, :, None, None] + dBx_t
                return (h, jnp.einsum('bhpn,bn->bhp', h, C_t))
            h0 = jnp.zeros((2 * Bt, H, P, NS), u.dtype)
            _, ys = jax.lax.scan(step, h0, (dA.transpose(1, 0, 2), dBx.transpose(1, 0, 2, 3, 4), C2.transpose(1, 0, 2)))
            y = ys.transpose(1, 0, 2, 3).reshape(2 * Bt, L, D_INNER)
            y_fw, y_bw = (y[:Bt], jnp.flip(y[Bt:], 1))
            y = jnp.pad(y_fw[:, :-1], ((0, 0), (1, 0), (0, 0))) + jnp.pad(y_bw[:, 1:], ((0, 0), (0, 1), (0, 0)))
            y = y + x_og * jnp.repeat(x_og @ fcD_w.T + Dp, P, axis=-1)
            yg = y * jax.nn.silu(z)
            yg = yg * jax.lax.rsqrt(jnp.mean(jnp.square(yg), -1, keepdims=True) + 1e-05) * norm_w
            return yg @ out_w.T
        key = jax.random.key(seed)
        ks = jax.random.split(key, 10)
        dim, Bsz, N = (256, 4, 8192)
        s = 0.02
        return {'x': jax.random.normal(ks[0], (Bsz, N, dim), jnp.float32), 'W_fx': jax.random.normal(ks[1], (D_INNER, dim), jnp.float32) * s, 'b_fx': jnp.zeros((D_INNER,), jnp.float32), 'W_x': jax.random.normal(ks[2], (D_INNER, dim), jnp.float32) * s, 'b_x': jnp.zeros((D_INNER,), jnp.float32), 'W_slice': jax.random.normal(ks[3], (G, P), jnp.float32) * s, 'b_slice': jnp.zeros((G,), jnp.float32), 'temperature': jnp.full((1, H, 1, 1), 0.5, jnp.float32), 'hy_in_w': jax.random.normal(ks[4], (D_IN_PROJ, D_INNER), jnp.float32) * s, 'hy_conv_w': jax.random.normal(ks[5], (CONV_DIM, K), jnp.float32) * s, 'hy_conv_b': jnp.zeros((CONV_DIM,), jnp.float32), 'hy_dt_bias': jnp.log(jnp.expm1(jnp.full((H,), 0.01, jnp.float32))), 'hy_A_log': jnp.log(jnp.linspace(1.0, 16.0, H)).astype(jnp.float32), 'hy_D': jnp.ones((H,), jnp.float32), 'hy_fcD_w': jax.random.normal(ks[6], (H, D_INNER), jnp.float32) * s, 'hy_norm_w': jnp.ones((D_INNER,), jnp.float32), 'hy_out_w': jax.random.normal(ks[7], (D_INNER, D_INNER), jnp.float32) * s, 'out_w': jax.random.normal(ks[8], (dim, D_INNER), jnp.float32) * s, 'out_b': jnp.zeros((dim,), jnp.float32)}
    _L0_ffn_all = _L0_ffn_setup()
    _L0_ffn_in = {k: v for k, v in _L0_ffn_all.items() if k in ('W_fx', 'b_fx', 'W_x', 'b_x', 'W_slice', 'b_slice', 'temperature', 'hy_in_w', 'hy_conv_w', 'hy_conv_b', 'hy_dt_bias', 'hy_A_log', 'hy_D', 'hy_fcD_w', 'hy_norm_w', 'hy_out_w', 'out_w', 'out_b', )}
    del _L0_ffn_all

    return {
        "x": x,
        "adj": adj,
        "L0_gnn_W": _L0_gnn_in["W"],
        "L0_gnn_b": _L0_gnn_in["b"],
        "L0_ffn_W_fx": _L0_ffn_in["W_fx"],
        "L0_ffn_b_fx": _L0_ffn_in["b_fx"],
        "L0_ffn_W_x": _L0_ffn_in["W_x"],
        "L0_ffn_b_x": _L0_ffn_in["b_x"],
        "L0_ffn_W_slice": _L0_ffn_in["W_slice"],
        "L0_ffn_b_slice": _L0_ffn_in["b_slice"],
        "L0_ffn_temperature": _L0_ffn_in["temperature"],
        "L0_ffn_hy_in_w": _L0_ffn_in["hy_in_w"],
        "L0_ffn_hy_conv_w": _L0_ffn_in["hy_conv_w"],
        "L0_ffn_hy_conv_b": _L0_ffn_in["hy_conv_b"],
        "L0_ffn_hy_dt_bias": _L0_ffn_in["hy_dt_bias"],
        "L0_ffn_hy_A_log": _L0_ffn_in["hy_A_log"],
        "L0_ffn_hy_D": _L0_ffn_in["hy_D"],
        "L0_ffn_hy_fcD_w": _L0_ffn_in["hy_fcD_w"],
        "L0_ffn_hy_norm_w": _L0_ffn_in["hy_norm_w"],
        "L0_ffn_hy_out_w": _L0_ffn_in["hy_out_w"],
        "L0_ffn_out_w": _L0_ffn_in["out_w"],
        "L0_ffn_out_b": _L0_ffn_in["out_b"],
    }

def reference(x, adj, L0_gnn_W, L0_gnn_b, L0_ffn_W_fx, L0_ffn_b_fx, L0_ffn_W_x, L0_ffn_b_x, L0_ffn_W_slice, L0_ffn_b_slice, L0_ffn_temperature, L0_ffn_hy_in_w, L0_ffn_hy_conv_w, L0_ffn_hy_conv_b, L0_ffn_hy_dt_bias, L0_ffn_hy_A_log, L0_ffn_hy_D, L0_ffn_hy_fcD_w, L0_ffn_hy_norm_w, L0_ffn_hy_out_w, L0_ffn_out_w, L0_ffn_out_b):
    import jax
    import jax.numpy as jnp
    def _L0_gnn_ref(A, X, W, b):
        import jax, jax.numpy as jnp
        import numpy as np
        B, N, C, OUT, S = (4, 2048, 256, 256, 25)
        DENSITY = 0.008
        mask = A != 0
        neg_inf = jnp.float32(-jnp.inf)
        pri = -jnp.arange(N, dtype=jnp.float32)
        scores = jnp.where(mask, pri, neg_inf)
        vals, idx = jax.lax.top_k(scores, S)
        valid = vals > neg_inf
        feats = jax.vmap(lambda x, i: x[i])(X, idx)
        feats = jnp.where(valid[..., None], feats, neg_inf)
        agg = feats.max(axis=2)
        degree = mask.sum(axis=-1)
        agg = jnp.where((degree <= S)[..., None], jnp.maximum(agg, 0.0), agg)
        h = jnp.concatenate([X, agg], axis=-1)
        out = jax.nn.relu(jnp.einsum('bnf,fo->bno', h, W) + b)
        return out

    def _L0_ffn_ref(x, W_fx, b_fx, W_x, b_x, W_slice, b_slice, temperature, hy_in_w, hy_conv_w, hy_conv_b, hy_dt_bias, hy_A_log, hy_D, hy_fcD_w, hy_norm_w, hy_out_w, out_w, out_b):
        import jax, jax.numpy as jnp
        import numpy as np
        H, P, G, NS, K = (8, 64, 64, 64, 3)
        D_INNER = H * P
        CONV_DIM = D_INNER + 2 * NS
        D_IN_PROJ = 2 * D_INNER + 2 * NS + 2 * H

        def _hydra(u, in_w, conv_w, conv_b, dt_bias, A_log, Dp, fcD_w, norm_w, out_w):
            Bt, L, _ = u.shape
            zxbcdt = u @ in_w.T
            z = zxbcdt[..., :D_INNER]
            xBC = zxbcdt[..., D_INNER:D_INNER + CONV_DIM]
            dt = zxbcdt[..., -2 * H:]
            dt = jnp.concatenate([dt[..., :H], jnp.flip(dt[..., H:], axis=1)], axis=0)
            dt = jax.nn.softplus(dt + dt_bias)
            xp = jnp.pad(xBC, ((0, 0), (K - 1, 0), (0, 0)))
            xBC = sum((xp[:, k:k + L, :] * conv_w[:, k] for k in range(K))) + conv_b
            xBC = jax.nn.silu(xBC)
            x = xBC[..., :D_INNER]
            Bm = xBC[..., D_INNER:D_INNER + NS]
            Cm = xBC[..., D_INNER + NS:]
            x_og = x
            x2 = jnp.concatenate([x, jnp.flip(x, 1)], 0).reshape(2 * Bt, L, H, P)
            B2 = jnp.concatenate([Bm, jnp.flip(Bm, 1)], 0)
            C2 = jnp.concatenate([Cm, jnp.flip(Cm, 1)], 0)
            dA = jnp.exp(dt * -jnp.exp(A_log))
            dBx = jnp.einsum('blh,bln,blhp->blhpn', dt, B2, x2)

            def step(h, inp):
                dA_t, dBx_t, C_t = inp
                h = h * dA_t[:, :, None, None] + dBx_t
                return (h, jnp.einsum('bhpn,bn->bhp', h, C_t))
            h0 = jnp.zeros((2 * Bt, H, P, NS), u.dtype)
            _, ys = jax.lax.scan(step, h0, (dA.transpose(1, 0, 2), dBx.transpose(1, 0, 2, 3, 4), C2.transpose(1, 0, 2)))
            y = ys.transpose(1, 0, 2, 3).reshape(2 * Bt, L, D_INNER)
            y_fw, y_bw = (y[:Bt], jnp.flip(y[Bt:], 1))
            y = jnp.pad(y_fw[:, :-1], ((0, 0), (1, 0), (0, 0))) + jnp.pad(y_bw[:, 1:], ((0, 0), (0, 1), (0, 0)))
            y = y + x_og * jnp.repeat(x_og @ fcD_w.T + Dp, P, axis=-1)
            yg = y * jax.nn.silu(z)
            yg = yg * jax.lax.rsqrt(jnp.mean(jnp.square(yg), -1, keepdims=True) + 1e-05) * norm_w
            return yg @ out_w.T
        B, N, _ = x.shape
        fx = (x @ W_fx.T + b_fx).reshape(B, N, H, P).transpose(0, 2, 1, 3)
        xm = (x @ W_x.T + b_x).reshape(B, N, H, P).transpose(0, 2, 1, 3)
        temp = jnp.maximum(temperature, 1e-06)
        sw = jax.nn.softmax((xm @ W_slice.T + b_slice) / temp, axis=-1)
        snorm = sw.sum(2)
        st = jnp.einsum('bhnc,bhng->bhgc', fx, sw) / (snorm + 1e-05)[..., None]
        st = st.transpose(0, 2, 1, 3).reshape(B, G, D_INNER)
        ot = _hydra(st, hy_in_w, hy_conv_w, hy_conv_b, hy_dt_bias, hy_A_log, hy_D, hy_fcD_w, hy_norm_w, hy_out_w)
        ot = ot.reshape(B, G, H, P).transpose(0, 2, 1, 3)
        out = jnp.einsum('bhgc,bhng->bhnc', ot, sw).transpose(0, 2, 1, 3).reshape(B, N, D_INNER)
        return out @ out_w.T + out_b

    x = x + _L0_gnn_ref(adj, _layernorm(x, axis=-1), L0_gnn_W, L0_gnn_b)
    x = x + _L0_ffn_ref(_layernorm(x, axis=-1), L0_ffn_W_fx, L0_ffn_b_fx, L0_ffn_W_x, L0_ffn_b_x, L0_ffn_W_slice, L0_ffn_b_slice, L0_ffn_temperature, L0_ffn_hy_in_w, L0_ffn_hy_conv_w, L0_ffn_hy_conv_b, L0_ffn_hy_dt_bias, L0_ffn_hy_A_log, L0_ffn_hy_D, L0_ffn_hy_fcD_w, L0_ffn_hy_norm_w, L0_ffn_hy_out_w, L0_ffn_out_w, L0_ffn_out_b)
    return x


_drawn_inputs = setup_inputs


def setup_inputs(seed=0):
    import zlib

    import numpy as np

    out = dict(_drawn_inputs(seed))
    spreads = {'L0_gnn_b': (0.0, 0.1),
     'L0_ffn_b_fx': (0.0, 0.1),
     'L0_ffn_b_x': (0.0, 0.8),
     'L0_ffn_b_slice': (0.0, 0.8),
     'L0_ffn_temperature': (0.5, 0.6),
     'L0_ffn_hy_conv_b': (0.0, 0.1),
     'L0_ffn_hy_dt_bias': (-4.600166320800781, 0.6),
     'L0_ffn_hy_D': (1.0, 0.6),
     'L0_ffn_hy_norm_w': (1.0, 0.6),
     'L0_ffn_out_b': (0.0, 0.1)}
    factors = {'L0_ffn_W_x': 8.0,
     'L0_ffn_W_slice': 8.0,
     'L0_ffn_hy_conv_w': 8.0,
     'L0_ffn_hy_A_log': 64.0,
     'L0_ffn_hy_fcD_w': 36.675}
    for name, (base, spread) in spreads.items():
        noise = np.random.default_rng([zlib.crc32(name.encode()), seed]).standard_normal(out[name].shape)
        drawn = base * np.exp(spread * noise) if base else spread * noise
        out[name] = jnp.asarray(drawn.astype(out[name].dtype))
    for name, factor in factors.items():
        out[name] = (out[name] * factor).astype(out[name].dtype)
    return out
```

```python
from contextlib import ExitStack

import concourse.bass as bass
from concourse import mybir

F32 = mybir.dt.float32
BF16 = mybir.dt.bfloat16
I32 = mybir.dt.int32
U32 = mybir.dt.uint32
ALU = mybir.AluOpType
ACT = mybir.ActivationFunctionType
AX_X = mybir.AxisListType.X

P = 128
B, N, C = 8, 2048, 256
H, HP, G = 8, 64, 64
DI = H * HP
NS = 64
CONV = DI + 2 * NS
K3 = 3
S = 25
TILES = N // P
PAIRS = TILES // 2
SEG = 8
NSEG = N // SEG
CAND = S + 1
TOP = 32
ROWS = N + 1
LN_EPS = 1e-5
BIG = 3.0e38


def adj_ffn(nc, x, adj, gnn_w, gnn_b, wfx_t, b_fx, w_x, b_x, wslice_t, b_slice, temperature,
            in_w_t, conv_w, conv_b, dt_bias, a_log, d_skip, fcd_t, norm_w, hyout_t, out_w_t, out_b, out):
    x_rows = x.rearrange("b n c -> (b n) c")
    out_rows = out.rearrange("b n c -> (b n) c")
    adj_rows = adj.rearrange("b n m -> (b n) m")
    tables = [nc.dram_tensor(f"normed_table{j}", (ROWS, C), F32, kind="Internal").ap() for j in range(2)]
    turned = nc.dram_tensor("turned_weights", (B * N, DI), F32, kind="Internal").ap()

    with ExitStack() as ctx:
        def sb(name, shape, dt=F32):
            return ctx.enter_context(nc.sbuf_tensor("sb_" + name, shape, dt))

        def sem(name):
            return ctx.enter_context(nc.semaphore(name))

        bank = [ctx.enter_context(nc.psum_tensor(f"bank{i}", [P, 512], F32)) for i in range(8)]

        ident = sb("ident", [P, P])
        ones = sb("ones", [1, P])
        ones_col = sb("ones_col", [P, 1])
        eps_col = sb("eps_col", [P, 1])
        zeros = sb("zeros", [1, C])
        bit_weight = sb("bit_weight", [P, SEG], BF16)
        bit_mask = sb("bit_mask", [P, SEG], I32)
        bit_index = sb("bit_index", [P, SEG])
        seg_base = sb("seg_base", [P, NSEG])
        shift = sb("shift", [G, K3, P])
        head_sel = sb("head_sel", [G, H, P])
        head_of_row = sb("head_of_row", [G, H])
        delta = sb("delta", [P, H, G])

        wg = sb("gnn_w", [P, 4, C])
        wg_b = sb("gnn_b", [1, C])
        wfx = sb("wfx", [P, 2, DI])
        bfx = sb("bfx", [1, DI])
        wlog = sb("wlog", [P, 2, DI])
        blog = sb("blog", [1, DI])
        rtemp = sb("rtemp", [P, H])
        slice_pair = sb("slice_pair", [P, P])
        b_slice2 = sb("b_slice2", [1, P])
        bx_col = sb("bx_col", [P, 4])
        w_in = sb("w_in", [P, 4, 2 * DI + 2 * NS])
        w_dt = sb("w_dt", [P, 4, G])
        conv_bc = sb("conv_bc", [G, CONV * K3])
        convb = sb("convb", [1, CONV])
        dt_b = sb("dt_b", [G, 1])
        neg_a = sb("neg_a", [G, 1])
        dskip = sb("dskip", [1, H])
        fcd = sb("fcd", [P, 4, H])
        normw = sb("normw", [P, 4])
        w_hyout = sb("w_hyout", [P, 4, DI])
        w_out = sb("w_out", [P, 4, C])
        bout = sb("bout", [1, C])

        adj_t = sb("adj_t", [P, N], I32)
        keys = sb("keys", [P, NSEG])
        packed = sb("packed", [P, NSEG])
        top_keys = sb("top_keys", [P, TOP])
        top_int = sb("top_int", [P, TOP], I32)
        top_base = sb("top_base", [P, TOP], I32)
        cand_bit = sb("cand_bit", [P, CAND, SEG], I32)
        cand = sb("cand", [P, CAND, SEG])
        first = sb("first", [P, TOP])
        indices = sb("indices", [P, 2, TOP], U32)
        floor = sb("floor", [P, 2])
        gathered = sb("gathered", [P, 2, S * C])
        agg = sb("agg", [P, C])
        agg_f = sb("agg_f", [P, C])
        x_t = sb("x_t", [P, 2, C])
        xn_t = sb("xn_t", [P, 2, C])
        h_t = sb("h_t", [P, 4, P])
        x2 = sb("x2", [P, TILES, C])
        stats2 = sb("stats2", [P, 6])
        mv2 = sb("mv2", [P, 2])
        rstd2 = sb("rstd2", [P, 2])
        xn2 = sb("xn2", [P, C])
        xn2_t = sb("xn2_t", [P, 2, P])
        head_max = sb("head_max", [P, H])
        head_sum = sb("head_sum", [P, H])
        head_rec = sb("head_rec", [P, H])
        expo = sb("expo", [P, DI])
        sw = sb("sw", [P, DI])
        swt_out = sb("swt_out", [P, 2, DI])
        sw_cur = sb("sw_cur", [P, 2, DI])
        out_t = sb("out_t", [P, 2, C])
        ln_x = sb("ln_x", [P, 2, C])
        ln_out = sb("ln_out", [P, 2, C])
        stats1 = sb("stats1", [P, 6])
        mv1 = sb("mv1", [P, 2])
        rstd1 = sb("rstd1", [P, 2])

        tok_sum = sb("tok_sum", [P, 2, DI])
        snorm = sb("snorm", [1, DI])
        den = sb("den", [G, H])
        rden = sb("rden", [G, H])
        u = sb("u", [G, DI])
        u_t = sb("u_t", [P, 4, G])
        v3 = sb("v3", [G, K3, CONV])
        dt_y = sb("dt_y", [G, G])
        dt_a = sb("dt_a", [G, G])
        dt_l = sb("dt_l", [G, G])
        dt_v = sb("dt_v", [G, G])
        dt_blocks = sb("dt_blocks", [G, P])
        log_decay = sb("log_decay", [G, G])
        decay = sb("decay", [G, G])
        xbc = sb("xbc", [P, CONV])
        gram = sb("gram", [P, G])
        w_mix = sb("w_mix", [P, H, G])
        z_e = expo[0:G, :]
        z_r = sw[0:G, :]
        prod = h_t[:, :, :].rearrange("p m c -> p (m c)")
        bc_t = xn2[0:G, :]
        xs_t = xn2_t[:, :, :].rearrange("p k (j g) -> p (k j) g", g=G)
        y1 = u
        yg = z_e
        ysq = z_r
        ss = sb("ss", [G, 1])
        rs = sb("rs", [G, 2])
        yg_t = u_t
        ot_pair = sb("ot_pair", [P, 4, P])
        mix = sb("mix", [P, 4, C])

        bits = tok_sum[:, :, :].rearrange("p k c -> p (k c)").bitcast(BF16)
        w_x_raw = x2[:, 0:4, :]

        adj_landed = sem("adj_landed")
        swt_stored = [sem(f"swt_stored{s}") for s in range(2)]
        swcur_landed = [sem(f"swcur_landed{s}") for s in range(2)]
        x_landed = [sem(f"x_landed{s}") for s in range(2)]
        xn_landed = [sem(f"xn_landed{s}") for s in range(2)]
        lnx_landed = [sem(f"lnx_landed{s}") for s in range(2)]
        table_stored = [sem(f"table_stored{s}") for s in range(2)]
        zero_rows_stored = sem("zero_rows_stored")
        rows_gathered = [sem(f"rows_gathered{s}") for s in range(2)]
        out_stored = [sem(f"out_stored{s}") for s in range(2)]
        weights_landed = sem("weights_landed")
        slices_landed = sem("slices_landed")
        consts_ready = sem("consts_ready")
        const_step = sem("const_step")
        dve_consts = sem("dve_consts")
        setup_psum = sem("setup_psum")
        setup_done = sem("setup_done")
        a_log_capped = sem("a_log_capped")
        neg_a_ready = sem("neg_a_ready")
        adj_used = sem("adj_used")
        indices_ready = sem("indices_ready")
        gather_free = sem("gather_free")
        gathers_begun = sem("gathers_begun")
        agg_ready = sem("agg_ready")
        ln1_var_ready = sem("ln1_var_ready")
        ln1_rstd_ready = sem("ln1_rstd_ready")
        normed_ready = sem("normed_ready")
        h_psum = sem("h_psum")
        h_ready = sem("h_ready")
        gnn_psum = sem("gnn_psum")
        xn_free = sem("xn_free")
        x_free = sem("x_free")
        ln2_var_ready = sem("ln2_var_ready")
        ln2_rstd_ready = sem("ln2_rstd_ready")
        xn2_ready = sem("xn2_ready")
        xn2t_psum = sem("xn2t_psum")
        xn2t_ready = sem("xn2t_ready")
        logits_psum = sem("logits_psum")
        shifted_ready = sem("shifted_ready")
        exp_ready = sem("exp_ready")
        sw_ready = sem("sw_ready")
        swt_psum = sem("swt_psum")
        swt_kept = sem("swt_kept")
        swcur_free = sem("swcur_free")
        final_psum = sem("final_psum")
        out_ready = sem("out_ready")
        sums_psum = sem("sums_psum")
        sums_copied = sem("sums_copied")
        slices_psum = sem("slices_psum")
        u_ready = sem("u_ready")
        ut_psum = sem("ut_psum")
        ut_ready = sem("ut_ready")
        v_psum = sem("v_psum")
        zdt_psum = sem("zdt_psum")
        v3_ready = sem("v3_ready")
        softplus_parts = sem("softplus_parts")
        log_decay_ready = sem("log_decay_ready")
        decay_ready = sem("decay_ready")
        conv_psum = sem("conv_psum")
        conv_exp = sem("conv_exp")
        xbc_ready = sem("xbc_ready")
        spread_psum = sem("spread_psum")
        spread_copied = sem("spread_copied")
        gram_psum = sem("gram_psum")
        wmix_ready = sem("wmix_ready")
        y_psum = sem("y_psum")
        ss_ready = sem("ss_ready")
        rs_ready = sem("rs_ready")
        yg_ready = sem("yg_ready")
        ygt_psum = sem("ygt_psum")
        ygt_ready = sem("ygt_ready")
        ot_psum = sem("ot_psum")
        ot_ready = sem("ot_ready")
        mix_psum = sem("mix_psum")
        mix_ready = sem("mix_ready")

        N_WEIGHTS = 20
        N_SLICE_LOADS = 7

        block = ctx.enter_context(nc.Block())

        def over_batches(eng, pair, mixer):
            with eng.Fori(0, PAIRS) as i:
                pair(0, i, False, True, True)
            mixer(0)
            with eng.Fori(1, B - 1) as b:
                with eng.Fori(0, PAIRS) as i:
                    pair(b, i, True, True, True)
                mixer(b)
            with eng.Fori(0, PAIRS - 1) as i:
                pair(B - 1, i, True, False, True)
            pair(B - 1, PAIRS - 1, True, False, False)
            mixer(B - 1)

        def over_batches_by_table(eng, pair):
            with eng.Fori(0, PAIRS) as i:
                pair(0, i, False, True, True, 0)
            with eng.Fori(0, (B - 2) // 2) as j:
                for own in (1, 0):
                    with eng.Fori(0, PAIRS) as i:
                        pair(2 * j + 2 - own, i, True, True, True, own)
            with eng.Fori(0, PAIRS - 1) as i:
                pair(B - 1, i, True, False, True, 1)
            pair(B - 1, PAIRS - 1, True, False, False, 1)

        @block.sync
        def _(sp):
            for s in range(2):
                sp.dma_start(ln_x[:, s, :], x_rows[s * P:(s + 1) * P, :]).then_inc(lnx_landed[s], 16)
            sp.dma_start(adj_t[:, :], adj_rows[0:P, :]).then_inc(adj_landed, 16)

            with sp.Fori(0, PAIRS - 1) as i:
                for s in range(2):
                    m = 2 * i + s
                    sp.wait_ge(normed_ready, m + 1)
                    sp.dma_start(tables[0][bass.ds(m * P, P), :], ln_out[:, s, :]).then_inc(table_stored[s], 16)
                    sp.dma_start(ln_x[:, s, :], x_rows[bass.ds((m + 2) * P, P), :]).then_inc(lnx_landed[s], 16)
            for s in range(2):
                m = TILES - 2 + s
                sp.wait_ge(normed_ready, m + 1)
                sp.dma_start(tables[0][m * P:(m + 1) * P, :], ln_out[:, s, :]).then_inc(table_stored[s], 16)
            sp.dma_start(x_t[:, 0, :], x_rows[0:P, :]).then_inc(x_landed[0], 16)

            sp.wait_ge(adj_used, 1)
            sp.dma_start(adj_t[:, :], adj_rows[P:2 * P, :]).then_inc(adj_landed, 16)

            sp.wait_ge(dve_consts, 1)
            for j in range(2):
                sp.dma_start(tables[j][N:ROWS, :], zeros[:, :]).then_inc(zero_rows_stored, 16)
            sp.dma_start(slice_pair[0:G, 0:G], wslice_t).then_inc(slices_landed, 16)
            sp.dma_start(slice_pair[G:P, G:P], wslice_t).then_inc(slices_landed, 16)
            sp.dma_start(w_x_raw, w_x.rearrange("(m p) c -> p m c", p=P)).then_inc(slices_landed, 16)
            sp.dma_start(rtemp[:, :], temperature.partition_broadcast(P)).then_inc(slices_landed, 16)
            for j in range(2):
                sp.dma_start(b_slice2[0:1, j * G:(j + 1) * G], b_slice).then_inc(slices_landed, 16)
            sp.dma_start(bx_col[:, :], b_x).then_inc(slices_landed, 16)
            chunks = "(m p) c -> p m c"
            for dst, src in (
                (wg[:, :, :], gnn_w.rearrange(chunks, p=P)),
                (wg_b[:, :], gnn_b),
                (wfx[:, :, :], wfx_t.rearrange(chunks, p=P)),
                (bfx[:, :], b_fx),
                (w_in[:, :, :], in_w_t[:, 0:DI + CONV].rearrange(chunks, p=P)),
                (w_dt[:, :, 0:H], in_w_t[:, DI + CONV:DI + CONV + H].rearrange(chunks, p=P)),
                (w_dt[:, :, 32:32 + H], in_w_t[:, DI + CONV + H:].rearrange(chunks, p=P)),
                (conv_bc[:, :], conv_w.partition_broadcast(G)),
                (convb[:, :], conv_b),
                (dt_b[0:H, :], dt_bias),
                (dt_b[32:32 + H, :], dt_bias),
                (neg_a[0:H, :], a_log),
                (neg_a[32:32 + H, :], a_log),
                (dskip[:, :], d_skip),
                (fcd[:, :, :], fcd_t.rearrange(chunks, p=P)),
                (normw[:, :], norm_w),
                (w_hyout[:, 0:2, :], hyout_t[0:2 * P].rearrange(chunks, p=P)),
                (w_hyout[:, 2:4, :], hyout_t[2 * P:].rearrange(chunks, p=P)),
                (w_out[:, :, :], out_w_t.rearrange(chunks, p=P)),
                (bout[:, :], out_b),
            ):
                sp.dma_start(dst, src).then_inc(weights_landed, 16)

            def pair(b, i, finish, prepare, ahead, own):
                p = b * PAIRS + i
                for s in range(2):
                    n = 2 * p + s
                    sp.wait_ge(table_stored[s], 16 * (p + 2))
                    sp.wait_ge(xn_free, n + 1)
                    sp.dma_start(xn_t[:, s, :], tables[own][bass.ds((2 * i + s) * P, P), :]).then_inc(xn_landed[s], 16)
                    if finish:
                        sp.wait_ge(swcur_free, n - TILES + 1)
                        sp.wait_ge(swt_stored[s], 16 * (p - PAIRS + 2))
                        sp.dma_start(sw_cur[:, s, :], turned[bass.ds((n - TILES) * P, P), :]
                                     ).then_inc(swcur_landed[s], 16)
                    if ahead:
                        sp.wait_ge(adj_used, n + 2)
                        sp.dma_start(adj_t[:, :], adj_rows[bass.ds((n + 2) * P, P), :]).then_inc(adj_landed, 16)
                    if prepare:
                        sp.wait_ge(normed_ready, n + TILES - 1)
                        sp.dma_start(ln_x[:, s, :], x_rows[bass.ds((n + TILES) * P, P), :]).then_inc(lnx_landed[s], 16)
                    if ahead or s == 0:
                        sp.wait_ge(x_free, n + 1)
                        sp.dma_start(x_t[:, 1 - s, :], x_rows[bass.ds((n + 1) * P, P), :]
                                     ).then_inc(x_landed[1 - s], 16)
                    if prepare:
                        sp.wait_ge(normed_ready, n + TILES + 1)
                        sp.dma_start(tables[1 - own][bass.ds((2 * i + s) * P, P), :], ln_out[:, s, :]
                                     ).then_inc(table_stored[s], 16)
                    sp.wait_ge(swt_kept, n + 2)
                    sp.dma_start(turned[bass.ds(n * P, P), :], swt_out[:, s, :]).then_inc(swt_stored[s], 16)
                    if finish:
                        sp.wait_ge(out_ready, n - TILES + 2)
                        sp.dma_start(out_rows[bass.ds((n - TILES) * P, P), :], out_t[:, s, :]
                                     ).then_inc(out_stored[s], 16)

            over_batches_by_table(sp, pair)
            with sp.Fori(0, PAIRS) as i:
                for s in range(2):
                    m = (B - 1) * TILES + 2 * i + s
                    sp.wait_ge(swcur_free, m + 1)
                    sp.wait_ge(swt_stored[s], 16 * ((B - 1) * PAIRS + i + 2))
                    sp.dma_start(sw_cur[:, s, :], turned[bass.ds(m * P, P), :]).then_inc(swcur_landed[s], 16)
                for s in range(2):
                    m = (B - 1) * TILES + 2 * i + s
                    sp.wait_ge(out_ready, m + 2)
                    sp.dma_start(out_rows[bass.ds(m * P, P), :], out_t[:, s, :]).then_inc(out_stored[s], 16)
            for s in range(2):
                sp.wait_ge(out_stored[s], 16 * (B * PAIRS + 1))
                sp.wait_ge(table_stored[s], 16 * (B * PAIRS + 1))
                sp.wait_ge(swt_stored[s], 16 * (B * PAIRS + 1))
            sp.wait_ge(zero_rows_stored, 32)

        @block.gpsimd
        def _(pool):
            steps = [0]

            def stepped(ins):
                steps[0] += 1
                ins.then_inc(const_step, 1)

            def wait_steps():
                pool.wait_ge(const_step, steps[0])

            stepped(pool.memset(ident[:, :], 0.0))
            stepped(pool.memset(shift[:, :, :], 0.0))
            stepped(pool.memset(head_sel[:, :, :], 0.0))
            stepped(pool.memset(head_of_row[:, :], 0.0))
            stepped(pool.memset(ones[:, :], 1.0))
            stepped(pool.memset(ones_col[:, :], 1.0))
            stepped(pool.memset(eps_col[:, :], LN_EPS))
            stepped(pool.memset(dt_blocks[:, :], 0.0))
            stepped(pool.memset(ot_pair[:, :, :], 0.0))
            stepped(pool.memset(w_mix[:, :, :], 0.0))
            stepped(pool.iota(seg_base[:, :], pattern=[[-256, NSEG]], base=256 * NSEG, channel_multiplier=0,
                              allow_small_or_imprecise_dtypes=True))
            stepped(pool.iota(bit_index[:, :], pattern=[[1, SEG]], base=0, channel_multiplier=0,
                              allow_small_or_imprecise_dtypes=True))
            for e in range(SEG):
                stepped(pool.memset(bit_weight[:, e:e + 1], float(1 << (SEG - 1 - e))))
                stepped(pool.memset(bit_mask[:, e:e + 1], 1 << (SEG - 1 - e)))
            wait_steps()

            def diagonal(view, base, pattern, rows=1):
                stepped(pool.affine_select(out=view, in_=view, compare_op=ALU.not_equal, fill=1.0, base=base,
                                           pattern=pattern, channel_multiplier=rows))

            diagonal(ident[:, :], 0, [[-1, P]])
            for k in range(K3):
                diagonal(shift[:, k, 0:G], 2 - k, [[-1, G]])
                diagonal(shift[:, k, G:P], -(G - 3) - k, [[1, G]])
            diagonal(head_sel[0:32, :, 0:G], 0, [[-1, H], [0, G]])
            diagonal(head_of_row[0:32, :], 0, [[-1, H]])
            wait_steps()
            diagonal(head_sel[32:64, :, G:P], 0, [[-1, H], [0, G]])
            diagonal(head_of_row[32:64, :], 0, [[-1, H]])
            wait_steps()
            for h in range(H):
                stepped(pool.tensor_tensor(delta[:, h, :], ident[:, 0:G], ident[:, G:P], ALU.add))
            wait_steps()
            pool.sem_inc(consts_ready, 1)
            pool.wait_ge(zero_rows_stored, 32)

            def pair(b, i, finish, prepare, ahead, own):
                p = b * PAIRS + i
                for s in range(2):
                    n = 2 * p + s
                    pool.wait_ge(table_stored[0], 16 * (PAIRS * (b + 1) + 1))
                    pool.wait_ge(table_stored[1], 16 * (PAIRS * (b + 1) + 1))
                    pool.wait_ge(gather_free, n + 1)
                    pool.wait_ge(indices_ready, n + 1)
                    pool.sem_inc(gathers_begun, 1)
                    for k in range(S):
                        pool.indirect_dma_start(
                            out=gathered[:, s, k * C:(k + 1) * C], out_offset=None, in_=tables[own],
                            in_offset=bass.IndirectOffsetOnAxis(ap=indices[:, s, k:k + 1], axis=0),
                        ).then_inc(rows_gathered[s], 16)

            over_batches_by_table(pool, pair)

        @block.vector
        def _(v):
            def ln1_stats(m, s, loads):
                v.wait_ge(lnx_landed[s], 16 * loads)
                v.bn_stats(stats1[:, :], ln_x[:, s, :])
                v.drain()
                v.bn_aggr(mv1[:, :], stats1[:, :]).then_inc(ln1_var_ready, 1)

            def ln1_apply(m, s, stores):
                v.wait_ge(table_stored[s], 16 * (stores + 1))
                v.wait_ge(ln1_rstd_ready, m + 1)
                v.tensor_scalar(ln_out[:, s, :], ln_x[:, s, :], mv1[:, 0:1], rstd1[:, 1:2],
                                ALU.subtract, ALU.mult).then_inc(normed_ready, 1)

            def pack_bits(loads):
                v.wait_ge(adj_landed, 16 * loads)
                v.scalar_tensor_tensor(
                    out=bits.rearrange("p (s e) -> p s e", e=SEG),
                    in0=adj_t[:, :].rearrange("p (s e) -> p s e", e=SEG), scalar=0.0,
                    in1=bit_weight[:, :].unsqueeze(1).to_broadcast([P, NSEG, SEG]),
                    op0=ALU.not_equal, op1=ALU.mult).then_inc(adj_used, 1)
                v.drain()
                v.tensor_reduce(packed[:, :], bits.rearrange("p (s e) -> p s e", e=SEG), AX_X, ALU.add)
                v.drain()
                v.scalar_tensor_tensor(out=keys[:, :], in0=packed[:, :], scalar=0.0, in1=seg_base[:, :],
                                       op0=ALU.is_gt, op1=ALU.mult)
                v.drain()
                v.tensor_tensor(keys[:, :], keys[:, :], packed[:, :], ALU.add)

            def top32(best, values):
                for r in range(TOP // 8):
                    v.drain()
                    v.max(best[:, 8 * r:8 * r + 8], values)
                    if r < TOP // 8 - 1:
                        v.drain()
                        v.match_replace(values, best[:, 8 * r:8 * r + 8], values, 0.0)

            def unpack_segments():
                v.drain()
                v.tensor_copy(top_int[:, :], top_keys[:, :])
                v.drain()
                v.tensor_scalar(top_base[:, :], top_int[:, :], 5, 0xFFF8, ALU.logical_shift_right, ALU.bitwise_and)
                v.tensor_tensor(cand_bit[:, :, :], top_int[:, 0:CAND].unsqueeze(2).to_broadcast([P, CAND, SEG]),
                                bit_mask[:, :].unsqueeze(1).to_broadcast([P, CAND, SEG]), ALU.bitwise_and)
                v.drain()
                v.tensor_tensor(cand[:, :, :], top_base[:, 0:CAND].unsqueeze(2).to_broadcast([P, CAND, SEG]),
                                bit_index[:, :].unsqueeze(1).to_broadcast([P, CAND, SEG]), ALU.subtract)
                v.drain()
                v.scalar_tensor_tensor(out=cand[:, :, :].rearrange("p s e -> p (s e)"),
                                       in0=cand_bit[:, :, :].rearrange("p s e -> p (s e)"), scalar=0.0,
                                       in1=cand[:, :, :].rearrange("p s e -> p (s e)"),
                                       op0=ALU.is_gt, op1=ALU.mult)

            def table_indices(s):
                v.drain()
                v.tensor_scalar(floor[:, s:s + 1], first[:, S:S + 1], 0.0, -BIG, ALU.is_gt, ALU.mult)
                v.tensor_scalar(indices[:, s, 0:S], first[:, 0:S], -1.0, float(N), ALU.mult, ALU.add
                                ).then_inc(indices_ready, 1)

            v.wait_ge(consts_ready, 1)
            v.memset(zeros[:, :], 0.0)
            v.memset(slice_pair[:, :], 0.0)
            v.memset(w_dt[:, :, :], 0.0)
            v.memset(dt_b[:, :], 0.0)
            v.memset(neg_a[:, :], 0.0)
            v.drain()
            v.sem_inc(dve_consts, 1)
            v.sem_inc(gather_free, 2)
            v.sem_inc(x_free, 1)
            v.sem_inc(swt_kept, 1)
            v.sem_inc(out_ready, 1)
            for s in range(2):
                v.sem_inc(table_stored[s], 16)
                v.sem_inc(swt_stored[s], 16)
                v.sem_inc(out_stored[s], 16)
            with v.Fori(0, PAIRS) as i:
                for s in range(2):
                    ln1_stats(2 * i + s, s, i + 1)
                    ln1_apply(2 * i + s, s, i)
            for s in range(2):
                pack_bits(s + 1)
                top32(top_keys[:, :], keys[:, :])
                unpack_segments()
                top32(first[:, :], cand[:, :, :].rearrange("p s e -> p (s e)"))
                table_indices(s)

            v.wait_ge(slices_landed, 16 * N_SLICE_LOADS)
            v.tensor_scalar(rtemp[:, :], rtemp[:, :], 1e-6, None, ALU.max)
            v.drain()
            v.reciprocal(rtemp[:, :], rtemp[:, :])
            v.drain()
            for k in range(2):
                v.wait_ge(setup_psum, k + 1)
                v.tensor_tensor(wlog[:, k, :].rearrange("p (h g) -> p h g", h=H),
                                bank[3 + k][:, :].rearrange("p (h g) -> p h g", h=H),
                                rtemp[:, :].unsqueeze(2).to_broadcast([P, H, G]), ALU.mult)
            v.wait_ge(setup_psum, 3)
            v.tensor_tensor(blog[:, :].rearrange("p (h g) -> p h g", h=H),
                            bank[5][0:1, :].rearrange("p (h g) -> p h g", h=H),
                            rtemp[0:1, :].unsqueeze(2).to_broadcast([1, H, G]), ALU.mult)
            v.wait_ge(weights_landed, 16 * N_WEIGHTS)
            v.tensor_scalar(neg_a[:, :], neg_a[:, :], 88.0, None, ALU.min).then_inc(a_log_capped, 1)
            for k in range(4):
                v.tensor_scalar(w_hyout[:, k, :], w_hyout[:, k, :], normw[:, k:k + 1], None, ALU.mult)
            v.wait_ge(neg_a_ready, 1)
            v.tensor_scalar(neg_a[:, :], neg_a[:, :], -1.0, None, ALU.mult)
            v.drain()
            v.sem_inc(setup_done, 1)

            def finish_tile(m, s, i, stores):
                v.wait_ge(final_psum, m + 1)
                v.wait_ge(out_stored[s], 16 * (stores + 1))
                v.tensor_tensor(out_t[:, s, :], x2[:, 2 * i + s, :], bank[7][:, 0:C], ALU.add
                                ).then_inc(out_ready, 1)

            def pair(b, i, finish, prepare, ahead):
                p = b * PAIRS + i
                for s in range(2):
                    n = 2 * p + s
                    v.wait_ge(rows_gathered[s], 16 * S * (p + 1))
                    v.tensor_reduce(agg[:, :], gathered[:, s, :].rearrange("p (k c) -> p c k", k=S), AX_X, ALU.max
                                    ).then_inc(gather_free, 1)
                    v.drain()
                    v.tensor_scalar(agg_f[:, :], agg[:, :], floor[:, s:s + 1], None, ALU.max).then_inc(agg_ready, 1)
                    if prepare:
                        ln1_stats(n + TILES, s, p + PAIRS + 1)
                    if ahead:
                        pack_bits(n + 3)
                    if prepare:
                        ln1_apply(n + TILES, s, p + PAIRS)
                    if finish:
                        finish_tile(n - TILES, s, i, p - PAIRS)
                        v.drain()
                    xt = x2[:, bass.ds(2 * i + s, 1), :].rearrange("p o c -> p (o c)")
                    v.wait_ge(x_landed[s], 16 * (p + 1))
                    v.wait_ge(gnn_psum, n + 1)
                    v.scalar_tensor_tensor(out=xt, in0=bank[4][:, 0:C], scalar=0.0, in1=x_t[:, s, :],
                                           op0=ALU.max, op1=ALU.add).then_inc(x_free, 1)
                    v.drain()
                    v.bn_stats(stats2[:, :], xt)
                    v.drain()
                    v.bn_aggr(mv2[:, :], stats2[:, :]).then_inc(ln2_var_ready, 1)
                    if ahead:
                        top32(top_keys[:, :], keys[:, :])
                    v.wait_ge(ln2_rstd_ready, n + 1)
                    v.tensor_scalar(xn2[:, :], xt, mv2[:, 0:1], rstd2[:, 1:2], ALU.subtract, ALU.mult
                                    ).then_inc(xn2_ready, 1)
                    if ahead:
                        unpack_segments()
                    v.wait_ge(logits_psum, n + 1)
                    logits = bank[5][:, :].rearrange("p (h g) -> p h g", h=H)
                    v.tensor_reduce(head_max[:, :], logits, AX_X, ALU.max)
                    v.drain()
                    v.tensor_tensor(expo[:, :].rearrange("p (h g) -> p h g", h=H), logits,
                                    head_max[:, :].unsqueeze(2).to_broadcast([P, H, G]), ALU.subtract
                                    ).then_inc(shifted_ready, 1)
                    if ahead:
                        top32(first[:, :], cand[:, :, :].rearrange("p s e -> p (s e)"))
                        table_indices(s)
                    v.wait_ge(exp_ready, n + 1)
                    v.tensor_reduce(head_sum[:, :], expo[:, :].rearrange("p (h g) -> p h g", h=H), AX_X, ALU.add)
                    v.drain()
                    v.reciprocal(head_rec[:, :], head_sum[:, :])
                    v.drain()
                    v.tensor_tensor(sw[:, :].rearrange("p (h g) -> p h g", h=H),
                                    expo[:, :].rearrange("p (h g) -> p h g", h=H),
                                    head_rec[:, :].unsqueeze(2).to_broadcast([P, H, G]), ALU.mult
                                    ).then_inc(sw_ready, 1)

            def mixer(b):
                done = b + 1
                v.wait_ge(sums_psum, done)
                v.tensor_copy(tok_sum[:, 1, :], bank[1][:, :])
                v.tensor_copy(snorm[:, :], bank[2][0:1, :]).then_inc(sums_copied, 1)
                v.wait_ge(slices_psum, done)
                v.tensor_scalar(den[:, :], bank[4][0:G, 0:H], 1e-5, None, ALU.add)
                v.drain()
                v.reciprocal(rden[:, :], den[:, :])
                v.drain()
                v.tensor_tensor(u[:, :].rearrange("p (h c) -> p h c", h=H),
                                bank[3][0:G, :].rearrange("p (h c) -> p h c", h=H),
                                rden[:, :].unsqueeze(2).to_broadcast([G, H, HP]), ALU.mult).then_inc(u_ready, 1)
                v.wait_ge(v_psum, done)
                taps = conv_bc[:, :].rearrange("p (c k) -> p k c", k=K3)
                for k in range(K3):
                    v.tensor_tensor(v3[:, k, 0:DI], bank[3][0:G, :], taps[:, k, 0:DI], ALU.mult)
                    last = v.tensor_tensor(v3[:, k, DI:CONV], bank[4][0:G, 0:2 * NS], taps[:, k, DI:CONV], ALU.mult)
                last.then_inc(v3_ready, 1)
                v.wait_ge(softplus_parts, done)
                v.scalar_tensor_tensor(out=dt_v[:, :], in0=dt_y[:, :], scalar=0.0, in1=dt_l[:, :],
                                       op0=ALU.max, op1=ALU.add)
                v.drain()
                v.tensor_copy(dt_blocks[0:32, 0:G], dt_v[0:32, :])
                v.tensor_copy(dt_blocks[32:64, G:P], dt_v[32:64, :])
                v.tensor_scalar(log_decay[:, :], dt_v[:, :], neg_a[:, 0:1], None, ALU.mult)
                v.drain()
                v.memset(log_decay[:, 0:1], -1e30).then_inc(log_decay_ready, 1)
                v.tensor_scalar(z_r, z_e, 1.0, None, ALU.add)
                v.drain()
                v.reciprocal(z_r, z_r)
                v.drain()
                v.tensor_tensor(z_r, z_r, bank[6][0:G, :], ALU.mult)
                v.wait_ge(conv_exp, done)
                v.tensor_scalar(xbc[:, :], xbc[:, :], 1.0, None, ALU.add)
                v.drain()
                v.reciprocal(xbc[:, :], xbc[:, :])
                v.drain()
                v.tensor_tensor(xbc[:, 0:DI], xbc[:, 0:DI], bank[0][:, :], ALU.mult)
                v.tensor_tensor(xbc[:, DI:CONV], xbc[:, DI:CONV], bank[1][:, 0:2 * NS], ALU.mult
                                ).then_inc(xbc_ready, 1)
                v.wait_ge(spread_psum, done)
                v.tensor_tensor_scan(prod, bank[5][:, :], delta[:, :, :].rearrange("p h t -> p (h t)"),
                                     0.0, ALU.mult, ALU.add)
                v.wait_ge(gram_psum, done)
                v.tensor_copy(gram[0:G, :], bank[7][0:G, 0:G])
                v.tensor_copy(gram[G:P, :], bank[7][G:P, G:P])
                v.drain()
                prod3 = prod.rearrange("p (h t) -> p h t", h=H)
                v.tensor_tensor(prod3, prod3, gram[:, :].unsqueeze(1).to_broadcast([P, H, G]), ALU.mult)
                v.drain()
                v.tensor_tensor(w_mix[0:G, :, 1:G], prod3[0:G, :, 0:G - 1],
                                bank[4][0:G, 256:256 + H].unsqueeze(2).to_broadcast([G, H, G - 1]), ALU.mult)
                v.tensor_tensor(w_mix[G:P, :, 0:G - 1], prod3[G:P, :, G - 2::-1],
                                bank[4][G:P, 256:256 + H].unsqueeze(2).to_broadcast([G, H, G - 1]), ALU.mult
                                ).then_inc(wmix_ready, 1)
                v.tensor_tensor(y1[:, :].rearrange("p (h c) -> p h c", h=H),
                                xbc[0:G, 0:DI].rearrange("p (h c) -> p h c", h=H),
                                bank[0][0:G, 0:H].unsqueeze(2).to_broadcast([G, H, HP]), ALU.mult)
                v.drain()
                v.wait_ge(y_psum, done)
                v.tensor_tensor(y1[:, :], y1[:, :], bank[5][0:G, :], ALU.add)
                v.drain()
                v.tensor_tensor(yg, y1[:, :], z_r, ALU.mult)
                v.drain()
                v.tensor_tensor_reduce(out=ysq, in0=yg, in1=yg, scale=1.0, scalar=0.0,
                                       op0=ALU.mult, op1=ALU.add, accum_out=ss[:, :]).then_inc(ss_ready, 1)
                v.wait_ge(rs_ready, done)
                v.tensor_scalar(yg, yg, rs[:, 1:2], None, ALU.mult).then_inc(yg_ready, 1)
                v.wait_ge(ot_psum, done)
                ot = bank[4][:, 0:4 * G].rearrange("p (m g) -> p m g", m=4)
                v.tensor_copy(ot_pair[0:G, :, 0:G], ot[0:G])
                v.tensor_copy(ot_pair[G:P, :, G:P], ot[G:P]).then_inc(ot_ready, 1)
                v.wait_ge(mix_psum, done)
                v.tensor_copy(mix[:, 2:4, :], bank[6][:, :].rearrange("p (m c) -> p m c", m=2)
                              ).then_inc(mix_ready, 1)

            over_batches(v, pair, mixer)
            with v.Fori(0, PAIRS) as i:
                for s in range(2):
                    finish_tile((B - 1) * TILES + 2 * i + s, s, i, (B - 1) * PAIRS + i)

        @block.scalar
        def _(act):
            def rstd(dst, mv, var_ready, count, ready):
                act.wait_ge(var_ready, count)
                nc.scalar.activation(dst[:, 0:1], mv[:, 1:2], ACT.Ln, bias=eps_col[:, 0:1])
                act.drain()
                nc.scalar.activation(dst[:, 1:2], dst[:, 0:1], ACT.Exp, scale=-0.5).then_inc(ready, 1)

            act.wait_ge(consts_ready, 1)
            with act.Fori(0, PAIRS) as i:
                for s in range(2):
                    rstd(rstd1, mv1, ln1_var_ready, 2 * i + s + 1, ln1_rstd_ready)
            act.wait_ge(a_log_capped, 1)
            nc.scalar.activation(neg_a[:, :], neg_a[:, :], ACT.Exp).then_inc(neg_a_ready, 1)

            def pair(b, i, finish, prepare, ahead):
                p = b * PAIRS + i
                for s in range(2):
                    n = 2 * p + s
                    if prepare:
                        rstd(rstd1, mv1, ln1_var_ready, n + TILES + 1, ln1_rstd_ready)
                    act.wait_ge(h_psum, n + 1)
                    nc.scalar.activation(h_t[:, :, :], bank[3][:, :].rearrange("p (m c) -> p m c", m=4), ACT.Copy
                                         ).then_inc(h_ready, 1)
                    rstd(rstd2, mv2, ln2_var_ready, n + 1, ln2_rstd_ready)
                    act.wait_ge(xn2t_psum, n + 1)
                    nc.scalar.activation(xn2_t[:, :, :], bank[4][:, C:2 * C].rearrange("p (m c) -> p m c", m=2),
                                         ACT.Copy).then_inc(xn2t_ready, 1)
                    act.wait_ge(shifted_ready, n + 1)
                    nc.scalar.activation(expo[:, :], expo[:, :], ACT.Exp).then_inc(exp_ready, 1)
                    act.wait_ge(swt_stored[s], 16 * (p + 1))
                    act.wait_ge(swt_psum, n + 1)
                    nc.scalar.activation(swt_out[:, s, :], bank[6][:, :], ACT.Copy).then_inc(swt_kept, 1)

            def mixer(b):
                done = b + 1
                act.wait_ge(sums_psum, done)
                nc.scalar.activation(tok_sum[:, 0, :], bank[0][:, :], ACT.Copy).then_inc(sums_copied, 1)
                act.wait_ge(ut_psum, done)
                nc.scalar.activation(u_t[:, :, :], bank[5][:, 0:4 * G].rearrange("p (m g) -> p m g", m=4), ACT.Copy
                                     ).then_inc(ut_ready, 1)
                act.wait_ge(zdt_psum, done)
                nc.scalar.activation(dt_y[0:32, :], bank[7][0:32, 0:G], ACT.Identity, bias=dt_b[0:32, 0:1])
                nc.scalar.activation(dt_y[32:64, :], bank[7][32:64, 0:G][:, ::-1], ACT.Identity,
                                     bias=dt_b[32:64, 0:1])
                act.drain()
                nc.scalar.activation(dt_a[:, :], dt_y[:, :], ACT.Abs)
                act.drain()
                nc.scalar.activation(dt_a[:, :], dt_a[:, :], ACT.Exp, scale=-1.0)
                nc.scalar.activation(z_e, bank[6][0:G, :], ACT.Exp, scale=-1.0)
                act.drain()
                nc.scalar.activation(dt_l[:, :], dt_a[:, :], ACT.Ln, bias=ones_col[0:G, 0:1]
                                     ).then_inc(softplus_parts, 1)
                act.wait_ge(log_decay_ready, done)
                nc.scalar.activation(decay[:, :], log_decay[:, :], ACT.Exp).then_inc(decay_ready, 1)
                act.wait_ge(conv_psum, done)
                nc.scalar.activation(xbc[:, 0:DI], bank[0][:, :], ACT.Exp, scale=-1.0)
                nc.scalar.activation(xbc[:, DI:CONV], bank[1][:, 0:2 * NS], ACT.Exp, scale=-1.0
                                     ).then_inc(conv_exp, 1)
                act.wait_ge(spread_psum, done)
                nc.scalar.activation(bc_t, bank[3][0:G, 0:2 * P], ACT.Copy)
                nc.scalar.activation(xs_t, bank[4][:, 0:4 * G].rearrange("p (m g) -> p m g", m=4), ACT.Copy
                                     ).then_inc(spread_copied, 1)
                act.wait_ge(ss_ready, done)
                nc.scalar.activation(rs[:, 0:1], ss[:, :], ACT.Ln, scale=1.0 / DI, bias=eps_col[0:G, 0:1])
                act.drain()
                nc.scalar.activation(rs[:, 1:2], rs[:, 0:1], ACT.Exp, scale=-0.5).then_inc(rs_ready, 1)
                act.wait_ge(ygt_psum, done)
                nc.scalar.activation(yg_t[:, :, :], bank[3][:, 0:4 * G].rearrange("p (m g) -> p m g", m=4), ACT.Copy
                                     ).then_inc(ygt_ready, 1)
                act.wait_ge(mix_psum, done)
                nc.scalar.activation(mix[:, 0:2, :], bank[5][:, :].rearrange("p (m c) -> p m c", m=2), ACT.Copy
                                     ).then_inc(mix_ready, 1)

            over_batches(act, pair, mixer)

        @block.tensor
        def _(pe):
            mm = nc.tensor.matmul

            def open_sums():
                for k in range(2):
                    mm(bank[k][:, :], zeros[0:1, 0:P], zeros[0:1, 0:1].to_broadcast([1, DI]), start=True, stop=False, skip_group_check=True)
                mm(bank[2][0:1, :], zeros[0:1, 0:1], zeros[0:1, 0:1].to_broadcast([1, DI]), start=True, stop=False, skip_group_check=True)

            def finish_tile(m, s, loads):
                pe.wait_ge(swcur_landed[s], 16 * loads)
                pe.wait_ge(out_ready, m + 1)
                for k in range(4):
                    last = mm(bank[7][:, 0:C], sw_cur[:, s, k * P:(k + 1) * P], mix[:, k, :],
                              start=(k == 0), stop=False)
                last.then_inc(swcur_free, 1)
                mm(bank[7][:, 0:C], ones[:, :], bout[:, :], start=False, stop=True).then_inc(final_psum, 1)

            pe.wait_ge(consts_ready, 1)
            pe.wait_ge(slices_landed, 16 * N_SLICE_LOADS)
            for k in range(2):
                for m in range(4):
                    last = mm(bank[3 + k][:, m * P:(m + 1) * P], w_x_raw[:, m, k * P:(k + 1) * P], slice_pair[:, :],
                              start=True, stop=True)
                last.then_inc(setup_psum, 1)
            for m in range(4):
                mm(bank[5][0:1, m * P:(m + 1) * P], bx_col[:, m:m + 1], slice_pair[:, :], start=True, stop=False)
                last = mm(bank[5][0:1, m * P:(m + 1) * P], ones[0:1, 0:1], b_slice2[:, :], start=False, stop=True)
            last.then_inc(setup_psum, 1)
            pe.wait_ge(dve_consts, 1)
            open_sums()
            pe.sem_inc(swcur_free, 2)
            pe.sem_inc(xn_free, 2)
            pe.wait_ge(setup_done, 1)
            pe.wait_ge(weights_landed, 16 * N_WEIGHTS)

            def pair(b, i, finish, prepare, ahead):
                p = b * PAIRS + i
                for s in range(2):
                    n = 2 * p + s
                    if finish:
                        finish_tile(n - TILES, s, p - PAIRS + 1)
                    pe.wait_ge(xn_landed[s], 16 * (p + 1))
                    for k in range(2):
                        last = nc.tensor.transpose(bank[3][:, k * P:(k + 1) * P], xn_t[:, s, k * P:(k + 1) * P],
                                                   ident[:, :])
                    last.then_inc(xn_free, 1)
                    pe.wait_ge(agg_ready, n + 1)
                    for k in range(2):
                        last = nc.tensor.transpose(bank[3][:, (2 + k) * P:(3 + k) * P], agg_f[:, k * P:(k + 1) * P],
                                                   ident[:, :])
                    last.then_inc(h_psum, 1)
                    pe.wait_ge(h_ready, n + 1)
                    for k in range(4):
                        mm(bank[4][:, 0:C], h_t[:, k, :], wg[:, k, :], start=(k == 0), stop=False)
                    mm(bank[4][:, 0:C], ones[:, :], wg_b[:, :], start=False, stop=True).then_inc(gnn_psum, 1)
                    pe.wait_ge(xn2_ready, n + 1)
                    for k in range(2):
                        last = nc.tensor.transpose(bank[4][:, C + k * P:C + (k + 1) * P], xn2[:, k * P:(k + 1) * P],
                                                   ident[:, :])
                    last.then_inc(xn2t_psum, 1)
                    pe.wait_ge(xn2t_ready, n + 1)
                    for k in range(2):
                        mm(bank[5][:, :], xn2_t[:, k, :], wlog[:, k, :], start=(k == 0), stop=False)
                    mm(bank[5][:, :], ones[:, :], blog[:, :], start=False, stop=True).then_inc(logits_psum, 1)
                    pe.wait_ge(swt_kept, n + 1)
                    pe.wait_ge(sw_ready, n + 1)
                    for k in range(4):
                        last = nc.tensor.transpose(bank[6][:, k * P:(k + 1) * P], sw[:, k * P:(k + 1) * P],
                                                   ident[:, :])
                    last.then_inc(swt_psum, 1)
                    for k in range(2):
                        mm(bank[k][:, :], xn2[:, k * P:(k + 1) * P], sw[:, :], start=False, stop=False,
                           skip_group_check=True)
                    mm(bank[2][0:1, :], ones_col[:, :], sw[:, :], start=False, stop=False, skip_group_check=True)

            def mixer(b):
                done = b + 1
                for k in range(2):
                    mm(bank[k][:, :], zeros[0:1, 0:P], zeros[0:1, 0:1].to_broadcast([1, DI]), start=False, stop=True, skip_group_check=True)
                mm(bank[2][0:1, :], zeros[0:1, 0:1], zeros[0:1, 0:1].to_broadcast([1, DI]), start=False, stop=True, skip_group_check=True
                   ).then_inc(sums_psum, 1)
                pe.wait_ge(swt_kept, TILES * done + 1)
                pe.wait_ge(sums_copied, 2 * done)
                for h in range(H):
                    cols = slice(h * HP, (h + 1) * HP)
                    for k in range(2):
                        mm(bank[3][0:G, cols], tok_sum[:, k, cols], wfx[:, k, cols], start=(k == 0), stop=False)
                    mm(bank[3][0:G, cols], snorm[0:1, cols], bfx[0:1, cols], start=False, stop=True)
                for h in range(H):
                    last = mm(bank[4][0:G, h:h + 1], snorm[0:1, h * G:(h + 1) * G], ones[0:1, 0:1],
                              start=True, stop=True)
                last.then_inc(slices_psum, 1)
                pe.wait_ge(u_ready, done)
                for k in range(4):
                    last = mm(bank[5][:, k * G:(k + 1) * G], u[:, k * P:(k + 1) * P], ident[0:G, 0:G],
                              start=True, stop=True)
                last.then_inc(ut_psum, 1)
                pe.wait_ge(ut_ready, done)
                for dst, c0, c1 in ((bank[3][0:G, :], DI, 2 * DI), (bank[4][0:G, 0:2 * NS], 2 * DI, DI + CONV)):
                    for k in range(4):
                        last = mm(dst, u_t[:, k, :], w_in[:, k, c0:c1], start=(k == 0), stop=(k == 3))
                last.then_inc(v_psum, 1)
                for k in range(4):
                    mm(bank[7][0:G, 0:G], w_dt[:, k, :], u_t[:, k, :], start=(k == 0), stop=(k == 3))
                for k in range(4):
                    last = mm(bank[6][0:G, :], u_t[:, k, :], w_in[:, k, 0:DI], start=(k == 0), stop=(k == 3))
                last.then_inc(zdt_psum, 1)
                pe.wait_ge(v3_ready, done)
                for dst, c0, c1 in ((bank[0][:, :], 0, DI), (bank[1][:, 0:2 * NS], DI, CONV)):
                    for k in range(K3):
                        mm(dst, shift[:, k, :], v3[:, k, c0:c1], start=(k == 0), stop=False)
                    last = mm(dst, ones[:, :], convb[:, c0:c1], start=False, stop=True)
                last.then_inc(conv_psum, 1)
                pe.wait_ge(decay_ready, done)
                for h in range(H):
                    mm(bank[5][:, h * G:(h + 1) * G], head_sel[:, h, :], decay[:, :], start=True, stop=True)
                mm(bank[4][:, 256:256 + H], dt_blocks[:, :], head_of_row[:, :], start=True, stop=True)
                pe.wait_ge(xbc_ready, done)
                for j in range(2):
                    mm(bank[3][0:G, j * P:(j + 1) * P], xbc[:, DI + j * NS:DI + (j + 1) * NS], ident[:, :],
                              start=True, stop=True)
                for k in range(4):
                    last = mm(bank[4][:, k * G:(k + 1) * G], xbc[0:G, k * P:(k + 1) * P], ident[0:G, 0:G],
                              start=True, stop=True)
                last.then_inc(spread_psum, 1)
                pe.wait_ge(spread_copied, done)
                for k in range(4):
                    mm(bank[0][0:G, 0:H], xs_t[:, k, :], fcd[:, k, :], start=(k == 0), stop=False)
                mm(bank[0][0:G, 0:H], ones[0:1, 0:G], dskip[:, :], start=False, stop=True)
                mm(bank[7][:, 0:P], bc_t[:, 0:P], bc_t[:, P:2 * P], start=True, stop=True).then_inc(gram_psum, 1)
                pe.wait_ge(wmix_ready, done)
                for h in range(H):
                    last = mm(bank[5][0:G, h * HP:(h + 1) * HP], w_mix[:, h, :], xbc[:, h * HP:(h + 1) * HP],
                              start=True, stop=True)
                last.then_inc(y_psum, 1)
                pe.wait_ge(yg_ready, done)
                for k in range(4):
                    last = mm(bank[3][:, k * G:(k + 1) * G], yg[:, k * P:(k + 1) * P], ident[0:G, 0:G],
                              start=True, stop=True)
                last.then_inc(ygt_psum, 1)
                pe.wait_ge(ygt_ready, done)
                for m in range(4):
                    for k in range(4):
                        last = mm(bank[4][:, m * G:(m + 1) * G], w_hyout[:, k, m * P:(m + 1) * P], yg_t[:, k, :],
                                  start=(k == 0), stop=(k == 3))
                last.then_inc(ot_psum, 1)
                pe.wait_ge(ot_ready, done)
                for m in range(4):
                    last = mm(bank[5 + m // 2][:, (m % 2) * C:(m % 2 + 1) * C], ot_pair[:, m, :], w_out[:, m, :],
                              start=True, stop=True)
                last.then_inc(mix_psum, 1)
                open_sums()
                pe.wait_ge(mix_ready, 2 * done)

            over_batches(pe, pair, mixer)
            with pe.Fori(0, PAIRS) as i:
                for s in range(2):
                    finish_tile((B - 1) * TILES + 2 * i + s, s, (B - 1) * PAIRS + i + 1)


def kernel(x, adj, L0_gnn_W, L0_gnn_b, L0_ffn_W_fx, L0_ffn_b_fx, L0_ffn_W_x, L0_ffn_b_x, L0_ffn_W_slice,
           L0_ffn_b_slice, L0_ffn_temperature, L0_ffn_hy_in_w, L0_ffn_hy_conv_w, L0_ffn_hy_conv_b,
           L0_ffn_hy_dt_bias, L0_ffn_hy_A_log, L0_ffn_hy_D, L0_ffn_hy_fcD_w, L0_ffn_hy_norm_w,
           L0_ffn_hy_out_w, L0_ffn_out_w, L0_ffn_out_b):
    import numpy as np
    import concourse.bacc as bacc
    from concourse.bass_utils import run_bass_kernel_spmd

    a = np.asarray
    arrays = {
        "x": a(x), "adj": a(adj), "gnn_w": a(L0_gnn_W), "gnn_b": a(L0_gnn_b).reshape(1, -1),
        "wfx_t": a(L0_ffn_W_fx).T, "b_fx": a(L0_ffn_b_fx).reshape(1, -1), "w_x": a(L0_ffn_W_x),
        "b_x": a(L0_ffn_b_x).reshape(4, 128).T, "wslice_t": a(L0_ffn_W_slice).T,
        "b_slice": a(L0_ffn_b_slice).reshape(1, -1), "temperature": a(L0_ffn_temperature).reshape(-1),
        "in_w_t": a(L0_ffn_hy_in_w).T, "conv_w": a(L0_ffn_hy_conv_w).reshape(-1),
        "conv_b": a(L0_ffn_hy_conv_b).reshape(1, -1), "dt_bias": a(L0_ffn_hy_dt_bias).reshape(-1, 1),
        "a_log": a(L0_ffn_hy_A_log).reshape(-1, 1), "d_skip": a(L0_ffn_hy_D).reshape(1, -1),
        "fcd_t": a(L0_ffn_hy_fcD_w).T, "norm_w": a(L0_ffn_hy_norm_w).reshape(4, 128).T,
        "hyout_t": a(L0_ffn_hy_out_w).T, "out_w_t": a(L0_ffn_out_w).T, "out_b": a(L0_ffn_out_b).reshape(1, -1),
    }
    nc = bacc.Bacc("TRN2", target_bir_lowering=False, num_devices=1)
    inputs, args = {}, {}
    for name, array in arrays.items():
        inputs[f"in_{name}"] = np.ascontiguousarray(array)
        args[name] = nc.dram_tensor(f"in_{name}", array.shape, mybir.dt.from_np(array.dtype),
                                    kind="ExternalInput").ap()
    args["out"] = nc.dram_tensor("out_x", (B, N, C), F32, kind="ExternalOutput").ap()
    adj_ffn(nc, **args)
    run = run_bass_kernel_spmd(nc, [inputs], core_ids=[0])
    return run.results[0]["out_x"]
```

```python
from contextlib import ExitStack

import concourse.bass as bass
from concourse import mybir

F32 = mybir.dt.float32
BF16 = mybir.dt.bfloat16
I32 = mybir.dt.int32
U32 = mybir.dt.uint32
ALU = mybir.AluOpType
ACT = mybir.ActivationFunctionType
AX_X = mybir.AxisListType.X

P = 128
B, N, C = 8, 2048, 256
H, HP, G = 8, 64, 64
DI = H * HP
NS = 64
CONV = DI + 2 * NS
K3 = 3
S = 25
TILES = N // P
PAIRS = TILES // 2
SEG = 8
NSEG = N // SEG
CAND = S + 1
TOP = 32
ROWS = N + 1
LN_EPS = 1e-5
BIG = 3.0e38
TOTAL = B * TILES
MIX_PAIRS = 5
LAG = TILES + 2 * MIX_PAIRS


def adj_ffn(nc, x, adj, gnn_w, gnn_b, wfx_t, b_fx, w_x, b_x, wslice_t, b_slice, temperature,
            in_w_t, conv_w, conv_b, dt_bias, a_log, d_skip, fcd_t, norm_w, hyout_t, out_w_t, out_b, out):
    x_rows = x.rearrange("b n c -> (b n) c")
    out_rows = out.rearrange("b n c -> (b n) c")
    adj_rows = adj.rearrange("b n m -> (b n) m")
    tables = [nc.dram_tensor(f"normed_table{j}", (ROWS, C), F32, kind="Internal").ap() for j in range(2)]
    x2_rows = nc.dram_tensor("x2_rows", (B * N, C), F32, kind="Internal").ap()
    turned = nc.dram_tensor("turned_weights", (B * N, DI), F32, kind="Internal").ap()

    with ExitStack() as ctx:
        def sb(name, shape, dt=F32):
            return ctx.enter_context(nc.sbuf_tensor("sb_" + name, shape, dt))

        def sem(name):
            return ctx.enter_context(nc.semaphore(name))

        bank = [ctx.enter_context(nc.psum_tensor(f"bank{i}", [P, 512], F32)) for i in range(8)]

        ident = sb("ident", [P, P])
        ones = sb("ones", [1, P])
        ones_col = sb("ones_col", [P, 1])
        eps_col = sb("eps_col", [P, 1])
        zeros = sb("zeros", [1, C])
        pack = sb("pack", [P, SEG, P], BF16)
        bit_mask = sb("bit_mask", [P, SEG], I32)
        bit_index = sb("bit_index", [P, SEG])
        seg_base = sb("seg_base", [P, NSEG])
        shift = sb("shift", [G, K3, P])
        head_sel = sb("head_sel", [G, H, P])
        head_of_row = sb("head_of_row", [G, H])
        delta = sb("delta", [P, H, G])

        wg = sb("gnn_w", [P, 4, C])
        wg_b = sb("gnn_b", [1, C])
        wfx = sb("wfx", [P, 2, DI])
        bfx = sb("bfx", [G, DI])
        wlog = sb("wlog", [P, 2, DI])
        blog = sb("blog", [1, DI])
        rtemp = sb("rtemp", [P, H])
        slice_pair = sb("slice_pair", [P, P])
        b_slice2 = sb("b_slice2", [1, P])
        bx_col = sb("bx_col", [P, 4])
        w_in = sb("w_in", [P, 4, 2 * DI + 2 * NS])
        w_dt = sb("w_dt", [P, 4, G])
        conv_bc = sb("conv_bc", [G, CONV * K3])
        convb = sb("convb", [1, CONV])
        dt_b = sb("dt_b", [G, 1])
        neg_a = sb("neg_a", [G, 1])
        dskip = sb("dskip", [1, H])
        fcd = sb("fcd", [P, 4, H])
        normw = sb("normw", [P, 4])
        w_hyout = sb("w_hyout", [P, 4, DI])
        w_out = sb("w_out", [P, 4, C])
        bout = sb("bout", [1, C])

        adj_t = sb("adj_t", [P, N], I32)
        keys = sb("keys", [P, NSEG])
        mask = sb("mask", [P, N], BF16)
        top_keys = sb("top_keys", [P, TOP])
        top_int = sb("top_int", [P, TOP], I32)
        top_base = sb("top_base", [P, TOP], I32)
        cand_bit = sb("cand_bit", [P, CAND, SEG], I32)
        cand = sb("cand", [P, CAND, SEG])
        first = sb("first", [P, TOP])
        indices = sb("indices", [P, 2, TOP], U32)
        floor = sb("floor", [P, 2])
        gathered = sb("gathered", [P, 2, S * C])
        agg = sb("agg", [P, C])
        agg_f = sb("agg_f", [P, C])
        x_t = sb("x_t", [P, 2, C])
        xn_t = sb("xn_t", [P, 2, C])
        h_t = sb("h_t", [P, 4, P])
        x2 = sb("x2", [P, 2, C])
        x2_back = sb("x2_back", [P, 2, C])
        stats2 = sb("stats2", [P, 6])
        mv2 = sb("mv2", [P, 2])
        rstd2 = sb("rstd2", [P, 4])
        xn2 = sb("xn2", [P, 2, C])
        xn2_t = sb("xn2_t", [P, 2, P])
        head_max = sb("head_max", [P, H])
        head_neg = sb("head_neg", [P, H])
        norm_sum = sb("norm_sum", [P, 4])
        head_sum = sb("head_sum", [P, H])
        head_rec = sb("head_rec", [P, H])
        expo = sb("expo", [P, DI])
        sw = sb("sw", [P, DI])
        swt_out = sb("swt_out", [P, 2, DI])
        sw_cur = sb("sw_cur", [P, 2, DI])
        out_t = sb("out_t", [P, 2, C])
        ln_x = sb("ln_x", [P, 2, C])
        ln_out = sb("ln_out", [P, 2, C])
        stats1 = sb("stats1", [P, 2, 6])
        mv1 = sb("mv1", [P, 2, 2])
        rstd1 = sb("rstd1", [P, 4])

        tok_sum = sb("tok_sum", [P, 2, DI])
        snorm = sb("snorm", [P, 4])
        den = sb("den", [G, H])
        rden = sb("rden", [G, H])
        u = sb("u", [G, DI])
        u_t = sb("u_t", [P, 4, G])
        v3 = sb("v3", [G, K3, CONV])
        dt_y = sb("dt_y", [G, G])
        dt_a = sb("dt_a", [G, G])
        dt_l = sb("dt_l", [G, G])
        dt_v = sb("dt_v", [G, G])
        dt_blocks = sb("dt_blocks", [G, P])
        log_decay = sb("log_decay", [G, G])
        decay = sb("decay", [G, G])
        xbc = sb("xbc", [P, CONV])
        gram = sb("gram", [P, G])
        w_mix = sb("w_mix", [P, H, G])
        z_e = sb("z_e", [G, DI])
        z_r = sb("z_r", [G, DI])
        prod = sb("prod", [P, DI])
        bc_t = sb("bc_t", [G, 2 * P])
        xs_t = sb("xs_t", [P, 4, G])
        y1 = u
        ss = sb("ss", [G, 1])
        rs = sb("rs", [G, 2])
        yg_t = u_t
        z_e, z_r, prod, bc_t, yg, ysq = (t[:, :] for t in (z_e, z_r, prod, bc_t, z_e, z_r))
        ot_pair = sb("ot_pair", [P, 4, P])
        mix = sb("mix", [P, 4, C])

        w_x_raw = mix[:, :, :]

        adj_landed = sem("adj_landed")
        x2_stored = [sem(f"x2_stored{s}") for s in range(2)]
        x2_landed = [sem(f"x2_landed{s}") for s in range(2)]
        swt_stored = [sem(f"swt_stored{s}") for s in range(2)]
        swcur_landed = [sem(f"swcur_landed{s}") for s in range(2)]
        x_landed = [sem(f"x_landed{s}") for s in range(2)]
        xn_landed = [sem(f"xn_landed{s}") for s in range(2)]
        lnx_landed = [sem(f"lnx_landed{s}") for s in range(2)]
        table_stored = [sem(f"table_stored{s}") for s in range(2)]
        zero_rows_stored = sem("zero_rows_stored")
        rows_gathered = [sem(f"rows_gathered{s}") for s in range(2)]
        out_stored = [sem(f"out_stored{s}") for s in range(2)]
        weights_landed = sem("weights_landed")
        slices_landed = sem("slices_landed")
        consts_ready = sem("consts_ready")
        const_step = sem("const_step")
        dve_consts = sem("dve_consts")
        setup_psum = sem("setup_psum")
        setup_done = sem("setup_done")
        a_log_capped = sem("a_log_capped")
        neg_a_ready = sem("neg_a_ready")
        adj_used = sem("adj_used")
        indices_ready = sem("indices_ready")
        gather_free = sem("gather_free")
        gathers_begun = sem("gathers_begun")
        agg_ready = sem("agg_ready")
        ln1_var_ready = sem("ln1_var_ready")
        ln1_rstd_ready = sem("ln1_rstd_ready")
        normed_ready = sem("normed_ready")
        h_psum = sem("h_psum")
        h_ready = sem("h_ready")
        gnn_psum = sem("gnn_psum")
        xn_free = sem("xn_free")
        x_free = sem("x_free")
        ln2_var_ready = sem("ln2_var_ready")
        ln2_rstd_ready = sem("ln2_rstd_ready")
        x2_ready = sem("x2_ready")
        xn2_ready = sem("xn2_ready")
        xn2t_psum = sem("xn2t_psum")
        xn2t_ready = sem("xn2t_ready")
        logits_psum = sem("logits_psum")
        max_ready = sem("max_ready")
        masked = sem("masked")
        mask_step = sem("mask_step")
        bits_psum = sem("bits_psum")
        keys_ready = sem("keys_ready")
        norm_psum = sem("norm_psum")
        norm_used = sem("norm_used")
        exp_ready = sem("exp_ready")
        sw_ready = sem("sw_ready")
        swt_psum = sem("swt_psum")
        swt_kept = sem("swt_kept")
        swcur_free = sem("swcur_free")
        final_psum = sem("final_psum")
        out_ready = sem("out_ready")
        sums_psum = sem("sums_psum")
        sums_copied = sem("sums_copied")
        slices_psum = sem("slices_psum")
        u_ready = sem("u_ready")
        ut_psum = sem("ut_psum")
        ut_ready = sem("ut_ready")
        v_psum = sem("v_psum")
        zdt_psum = sem("zdt_psum")
        z_used = sem("z_used")
        scanned = sem("scanned")
        xs_copied = sem("xs_copied")
        mix3_psum = sem("mix3_psum")
        mix_half = sem("mix_half")
        sums_opened = sem("sums_opened")
        v3_ready = sem("v3_ready")
        softplus_parts = sem("softplus_parts")
        log_decay_ready = sem("log_decay_ready")
        decay_ready = sem("decay_ready")
        conv_psum = sem("conv_psum")
        conv_exp = sem("conv_exp")
        xbc_ready = sem("xbc_ready")
        spread_psum = sem("spread_psum")
        spread_copied = sem("spread_copied")
        gram_psum = sem("gram_psum")
        wmix_ready = sem("wmix_ready")
        y_psum = sem("y_psum")
        ss_ready = sem("ss_ready")
        rs_ready = sem("rs_ready")
        yg_ready = sem("yg_ready")
        ygt_psum = sem("ygt_psum")
        ygt_ready = sem("ygt_ready")
        ot_psum = sem("ot_psum")
        ot_ready = sem("ot_ready")
        mix_psum = sem("mix_psum")
        mix_ready = sem("mix_ready")

        N_WEIGHTS = 20
        N_SLICE_LOADS = 7

        block = ctx.enter_context(nc.Block())

        def exists(m):
            return not isinstance(m, int) or 0 <= m < TOTAL

        def pairs(eng, b, start, pair, *flags):
            if start < PAIRS - 3:
                with eng.Fori(start, PAIRS - 2) as i:
                    pair(b, i, 1, *flags)
            else:
                pair(b, start, 1, *flags)
            pair(b, PAIRS - 2, 2, *flags)
            pair(b, PAIRS - 1, 0, *flags)

        def over_batches(eng, pair):
            pair(0, 0, 1, False, False)
            pairs(eng, 0, 1, pair, False, False)
            for i in range(MIX_PAIRS):
                pair(1, i, 1, False, True)
            pairs(eng, 1, MIX_PAIRS, pair, True, False)
            with eng.Fori(2, B - 1) as b:
                for i in range(MIX_PAIRS):
                    pair(b, i, 1, True, True)
                pairs(eng, b, MIX_PAIRS, pair, True, False)
            for i in range(PAIRS):
                pair(B - 1, i, 0, True, i < MIX_PAIRS)

        def over_batches_by_table(eng, pair):
            pair(0, 0, 1, False, 0)
            pairs(eng, 0, 1, pair, False, 0)
            with eng.Fori(0, MIX_PAIRS) as i:
                pair(1, i, 1, False, 1)
            pairs(eng, 1, MIX_PAIRS, pair, True, 1)
            with eng.Fori(0, (B - 4) // 2) as j:
                for own in range(2):
                    pairs(eng, 2 * j + 2 + own, 0, pair, True, own)
            pairs(eng, B - 2, 0, pair, True, 0)
            with eng.Fori(0, PAIRS - 3) as i:
                pair(B - 1, i, 0, True, 1)
            for i in range(PAIRS - 3, PAIRS):
                pair(B - 1, i, 0, True, 1)

        def to_normalise(p, s, prepare):
            if prepare == 2:
                return [(slot, p + PAIRS + s) for slot in range(2)]
            return [(s, p + PAIRS)] if prepare else []

        @block.sync
        def _(sp):
            for s in range(2):
                sp.dma_start(ln_x[:, s, :], x_rows[s * P:(s + 1) * P, :]).then_inc(lnx_landed[s], 16)
            sp.dma_start(adj_t[:, :], adj_rows[0:P, :]).then_inc(adj_landed, 16)

            with sp.Fori(0, PAIRS - 1) as i:
                for s in range(2):
                    m = 2 * i + s
                    sp.wait_ge(normed_ready, m + 1)
                    sp.dma_start(tables[0][bass.ds(m * P, P), :], ln_out[:, s, :]).then_inc(table_stored[s], 16)
                    sp.dma_start(ln_x[:, s, :], x_rows[bass.ds((m + 2) * P, P), :]).then_inc(lnx_landed[s], 16)
            for s in range(2):
                m = TILES - 2 + s
                sp.wait_ge(normed_ready, m + 1)
                sp.dma_start(tables[0][m * P:(m + 1) * P, :], ln_out[:, s, :]).then_inc(table_stored[s], 16)
            sp.dma_start(x_t[:, 0, :], x_rows[0:P, :]).then_inc(x_landed[0], 16)

            sp.wait_ge(dve_consts, 1)
            for j in range(2):
                sp.dma_start(tables[j][N:ROWS, :], zeros[:, :]).then_inc(zero_rows_stored, 16)
            sp.dma_start(slice_pair[0:G, 0:G], wslice_t).then_inc(slices_landed, 16)
            sp.dma_start(slice_pair[G:P, G:P], wslice_t).then_inc(slices_landed, 16)
            sp.dma_start(w_x_raw, w_x.rearrange("(m p) c -> p m c", p=P)).then_inc(slices_landed, 16)
            sp.dma_start(rtemp[:, :], temperature.partition_broadcast(P)).then_inc(slices_landed, 16)
            for j in range(2):
                sp.dma_start(b_slice2[0:1, j * G:(j + 1) * G], b_slice).then_inc(slices_landed, 16)
            sp.dma_start(bx_col[:, :], b_x).then_inc(slices_landed, 16)
            chunks = "(m p) c -> p m c"
            for dst, src in (
                (wg[:, :, :], gnn_w.rearrange(chunks, p=P)),
                (wg_b[:, :], gnn_b),
                (wfx[:, :, :], wfx_t.rearrange(chunks, p=P)),
                (bfx[:, :], b_fx.partition_broadcast(G)),
                (w_in[:, :, :], in_w_t[:, 0:DI + CONV].rearrange(chunks, p=P)),
                (w_dt[:, :, 0:H], in_w_t[:, DI + CONV:DI + CONV + H].rearrange(chunks, p=P)),
                (w_dt[:, :, 32:32 + H], in_w_t[:, DI + CONV + H:].rearrange(chunks, p=P)),
                (conv_bc[:, :], conv_w.partition_broadcast(G)),
                (convb[:, :], conv_b),
                (dt_b[0:H, :], dt_bias),
                (dt_b[32:32 + H, :], dt_bias),
                (neg_a[0:H, :], a_log),
                (neg_a[32:32 + H, :], a_log),
                (dskip[:, :], d_skip),
                (fcd[:, :, :], fcd_t.rearrange(chunks, p=P)),
                (normw[:, :], norm_w),
                (w_hyout[:, 0:2, :], hyout_t[0:2 * P].rearrange(chunks, p=P)),
                (w_hyout[:, 2:4, :], hyout_t[2 * P:].rearrange(chunks, p=P)),
                (w_out[:, :, :], out_w_t.rearrange(chunks, p=P)),
                (bout[:, :], out_b),
            ):
                sp.dma_start(dst, src).then_inc(weights_landed, 16)

            for m in range(1, 6):
                sp.wait_ge(adj_used, m)
                sp.dma_start(adj_t[:, :], adj_rows[m * P:(m + 1) * P, :]).then_inc(adj_landed, 16)

            def load_to_finish(m, s, loads):
                sp.wait_ge(swcur_free, m + 1)
                sp.wait_ge(swt_stored[s], 16 * loads + 16)
                sp.dma_start(sw_cur[:, s, :], turned[bass.ds(m * P, P), :]).then_inc(swcur_landed[s], 16)
                sp.wait_ge(out_ready, m + 1)
                sp.wait_ge(x2_stored[s], 16 * loads + 16)
                sp.dma_start(x2_back[:, s, :], x2_rows[bass.ds(m * P, P), :]).then_inc(x2_landed[s], 16)

            def store_finished(m, s):
                sp.wait_ge(out_ready, m + 3)
                sp.dma_start(out_rows[bass.ds(m * P, P), :], out_t[:, s, :]).then_inc(out_stored[s], 16)

            def pair(b, i, prepare, finish, own):
                p = b * PAIRS + i
                for s in range(2):
                    n = 2 * p + s
                    sp.wait_ge(xn_free, n + 1)
                    sp.wait_ge(table_stored[s], 16 * (p + 2))
                    sp.dma_start(xn_t[:, s, :], tables[own][bass.ds((2 * i + s) * P, P), :]).then_inc(xn_landed[s], 16)
                    if exists(n + 1):
                        sp.wait_ge(x_free, n + 1)
                        sp.dma_start(x_t[:, 1 - s, :], x_rows[bass.ds((n + 1) * P, P), :]
                                     ).then_inc(x_landed[1 - s], 16)
                    for slot, q in to_normalise(p, s, prepare):
                        sp.wait_ge(normed_ready, 2 * q + slot - 1)
                        sp.dma_start(ln_x[:, slot, :], x_rows[bass.ds((2 * q + slot) * P, P), :]
                                     ).then_inc(lnx_landed[slot], 16)
                    if finish:
                        load_to_finish(n - LAG, s, p - LAG // 2 + 1)
                    for slot, q in to_normalise(p, s, prepare):
                        row = (2 * i + s if prepare == 1 else 2 * (i + s) + slot) * P
                        sp.wait_ge(normed_ready, 2 * q + slot + 1)
                        sp.dma_start(tables[1 - own][bass.ds(row, P), :], ln_out[:, slot, :]
                                     ).then_inc(table_stored[slot], 16)
                    sp.wait_ge(x2_ready, n + 1)
                    sp.dma_start(x2_rows[bass.ds(n * P, P), :], x2[:, s, :]).then_inc(x2_stored[s], 16)
                    if finish:
                        store_finished(n - LAG, s)
                    if exists(n + 6):
                        sp.wait_ge(adj_used, n + 6)
                        sp.dma_start(adj_t[:, :], adj_rows[bass.ds((n + 6) * P, P), :]).then_inc(adj_landed, 16)

            over_batches_by_table(sp, pair)
            for m in range(TOTAL - LAG, TOTAL - TILES):
                load_to_finish(m, m % 2, m // 2 + 1)
                store_finished(m, m % 2)
            first = TOTAL - TILES
            for s in range(2):
                load_to_finish(first + s, s, first // 2 + 1)
            with sp.Fori(first // 2, TOTAL // 2 - 1) as q:
                for s in range(2):
                    load_to_finish(2 * q + 2 + s, s, q + 2)
                    store_finished(2 * q + s, s)
            for s in range(2):
                store_finished(TOTAL - 2 + s, s)
            for s in range(2):
                sp.wait_ge(out_stored[s], 16 * (TOTAL // 2 + 1))
                sp.wait_ge(table_stored[s], 16 * (TOTAL // 2 + 1))
                sp.wait_ge(swt_stored[s], 16 * (TOTAL // 2 + 1))
                sp.wait_ge(x2_stored[s], 16 * (TOTAL // 2 + 1))
            sp.wait_ge(zero_rows_stored, 32)

        @block.gpsimd
        def _(pool):
            steps = [0]

            def stepped(ins):
                steps[0] += 1
                ins.then_inc(const_step, 1)

            def wait_steps():
                pool.wait_ge(const_step, steps[0])

            stepped(pool.memset(ident[:, :], 0.0))
            stepped(pool.memset(shift[:, :, :], 0.0))
            stepped(pool.memset(head_sel[:, :, :], 0.0))
            stepped(pool.memset(head_of_row[:, :], 0.0))
            stepped(pool.memset(ones[:, :], 1.0))
            stepped(pool.memset(ones_col[:, :], 1.0))
            stepped(pool.memset(eps_col[:, :], LN_EPS))
            stepped(pool.memset(dt_blocks[:, :], 0.0))
            stepped(pool.memset(ot_pair[:, :, :], 0.0))
            stepped(pool.memset(w_mix[:, :, :], 0.0))
            stepped(pool.iota(seg_base[:, :], pattern=[[-256, NSEG]], base=256 * NSEG, channel_multiplier=0,
                              allow_small_or_imprecise_dtypes=True))
            stepped(pool.iota(bit_index[:, :], pattern=[[1, SEG]], base=0, channel_multiplier=0,
                              allow_small_or_imprecise_dtypes=True))
            stepped(pool.memset(pack[:, :, :], 0.0))
            for e in range(SEG):
                stepped(pool.memset(bit_mask[:, e:e + 1], 1 << (SEG - 1 - e)))
            wait_steps()

            def diagonal(view, base, pattern, fill=1.0):
                stepped(pool.affine_select(out=view, in_=view, compare_op=ALU.not_equal, fill=fill, base=base,
                                           pattern=pattern, channel_multiplier=1))

            diagonal(ident[:, :], 0, [[-1, P]])
            for e in range(SEG):
                diagonal(pack[:, e, :], 0, [[-1, P]], fill=float(1 << (SEG - 1 - e)))
            for k in range(K3):
                diagonal(shift[:, k, 0:G], 2 - k, [[-1, G]])
                diagonal(shift[:, k, G:P], -(G - 3) - k, [[1, G]])
            diagonal(head_sel[0:32, :, 0:G], 0, [[-1, H], [0, G]])
            diagonal(head_of_row[0:32, :], 0, [[-1, H]])
            wait_steps()
            diagonal(head_sel[32:64, :, G:P], 0, [[-1, H], [0, G]])
            diagonal(head_of_row[32:64, :], 0, [[-1, H]])
            wait_steps()
            for h in range(H):
                stepped(pool.tensor_tensor(delta[:, h, :], ident[:, 0:G], ident[:, G:P], ALU.add))
            wait_steps()
            pool.sem_inc(consts_ready, 1)
            pool.wait_ge(zero_rows_stored, 32)

            def pair(b, i, prepare, finish, own):
                p = b * PAIRS + i
                for s in range(2):
                    n = 2 * p + s
                    pool.wait_ge(table_stored[0], 16 * (PAIRS * (b + 1) + 1))
                    pool.wait_ge(table_stored[1], 16 * (PAIRS * (b + 1) + 1))
                    pool.wait_ge(gather_free, n + 1)
                    pool.wait_ge(indices_ready, n + 1)
                    pool.sem_inc(gathers_begun, 1)
                    for k in range(S):
                        pool.indirect_dma_start(
                            out=gathered[:, s, k * C:(k + 1) * C], out_offset=None, in_=tables[own],
                            in_offset=bass.IndirectOffsetOnAxis(ap=indices[:, s, k:k + 1], axis=0),
                        ).then_inc(rows_gathered[s], 16)

            over_batches_by_table(pool, pair)

        @block.vector
        def _(v):
            def ln1_stats(s, loads):
                v.wait_ge(lnx_landed[s], 16 * loads)
                v.bn_stats(stats1[:, s, :], ln_x[:, s, :])
                v.drain()
                v.bn_aggr(mv1[:, s, :], stats1[:, s, :]).then_inc(ln1_var_ready, 1)

            def make_keys(m):
                v.wait_ge(bits_psum, m + 1)
                v.scalar_tensor_tensor(out=keys[:, :], in0=bank[7][:, C:2 * C], scalar=0.0, in1=seg_base[:, :],
                                       op0=ALU.is_gt, op1=ALU.mult)
                v.drain()
                v.tensor_tensor(keys[:, :], keys[:, :], bank[7][:, C:2 * C], ALU.add).then_inc(keys_ready, 1)

            def top32(*jobs):
                for r in range(TOP // 8):
                    v.drain()
                    for best, values in jobs:
                        v.max(best[:, 8 * r:8 * r + 8], values)
                    if r < TOP // 8 - 1:
                        v.drain()
                        for best, values in jobs:
                            v.match_replace(values, best[:, 8 * r:8 * r + 8], values, 0.0)

            by_segment = (top_keys, keys[:, :])
            by_column = (first, cand[:, :, :].rearrange("p s e -> p (s e)"))

            def unpack_segments():
                v.drain()
                v.tensor_copy(top_int[:, :], top_keys[:, :])
                v.drain()
                v.tensor_scalar(top_base[:, :], top_int[:, :], 5, 0xFFF8, ALU.logical_shift_right, ALU.bitwise_and)
                v.tensor_tensor(cand_bit[:, :, :], top_int[:, 0:CAND].unsqueeze(2).to_broadcast([P, CAND, SEG]),
                                bit_mask[:, :].unsqueeze(1).to_broadcast([P, CAND, SEG]), ALU.bitwise_and)
                v.drain()
                v.tensor_tensor(cand[:, :, :], top_base[:, 0:CAND].unsqueeze(2).to_broadcast([P, CAND, SEG]),
                                bit_index[:, :].unsqueeze(1).to_broadcast([P, CAND, SEG]), ALU.subtract)
                v.drain()
                v.scalar_tensor_tensor(out=cand[:, :, :].rearrange("p s e -> p (s e)"),
                                       in0=cand_bit[:, :, :].rearrange("p s e -> p (s e)"), scalar=0.0,
                                       in1=cand[:, :, :].rearrange("p s e -> p (s e)"),
                                       op0=ALU.is_gt, op1=ALU.mult)

            def table_indices(s):
                v.tensor_scalar(indices[:, s, 0:S], first[:, 0:S], -1.0, float(N), ALU.mult, ALU.add
                                ).then_inc(indices_ready, 1)

            def maximum_floor(s):
                v.tensor_scalar(floor[:, s:s + 1], first[:, S:S + 1], 0.0, -BIG, ALU.is_gt, ALU.mult)

            v.memset(zeros[:, :], 0.0)
            v.memset(slice_pair[:, :], 0.0)
            v.memset(w_dt[:, :, :], 0.0)
            v.memset(dt_b[:, :], 0.0)
            v.memset(neg_a[:, :], 0.0)
            v.memset(norm_sum[:, :], 0.0)
            v.drain()
            v.sem_inc(dve_consts, 1)
            v.sem_inc(gather_free, 2)
            v.sem_inc(x_free, 1)
            v.sem_inc(swt_kept, 2)
            v.sem_inc(out_ready, 2)
            v.sem_inc(norm_used, 1)
            for s in range(2):
                v.sem_inc(table_stored[s], 16)
                v.sem_inc(swt_stored[s], 16)
                v.sem_inc(x2_stored[s], 16)
                v.sem_inc(out_stored[s], 16)
            v.wait_ge(consts_ready, 1)
            for m in range(4):
                make_keys(m)
                top32(by_segment)
                unpack_segments()
                if m < 3:
                    top32(by_column)
                if m < 2:
                    v.drain()
                    table_indices(m)
                    maximum_floor(m)
                if m == 0:
                    with v.Fori(0, PAIRS) as i:
                        for s in range(2):
                            ln1_stats(s, i + 1)

            v.wait_ge(slices_landed, 16 * N_SLICE_LOADS)
            v.tensor_scalar(rtemp[:, :], rtemp[:, :], 1e-6, None, ALU.max)
            v.drain()
            v.reciprocal(rtemp[:, :], rtemp[:, :])
            v.drain()
            for k in range(2):
                v.wait_ge(setup_psum, k + 1)
                v.tensor_tensor(wlog[:, k, :].rearrange("p (h g) -> p h g", h=H),
                                bank[3 + k][:, :].rearrange("p (h g) -> p h g", h=H),
                                rtemp[:, :].unsqueeze(2).to_broadcast([P, H, G]), ALU.mult)
            v.wait_ge(setup_psum, 3)
            v.tensor_tensor(blog[:, :].rearrange("p (h g) -> p h g", h=H),
                            bank[5][0:1, :].rearrange("p (h g) -> p h g", h=H),
                            rtemp[0:1, :].unsqueeze(2).to_broadcast([1, H, G]), ALU.mult)
            v.wait_ge(weights_landed, 16 * N_WEIGHTS)
            v.tensor_scalar(neg_a[:, :], neg_a[:, :], 88.0, None, ALU.min).then_inc(a_log_capped, 1)
            for k in range(4):
                v.tensor_scalar(w_hyout[:, k, :], w_hyout[:, k, :], normw[:, k:k + 1], None, ALU.mult)
            v.wait_ge(neg_a_ready, 1)
            v.tensor_scalar(neg_a[:, :], neg_a[:, :], -1.0, None, ALU.mult)
            v.drain()
            v.sem_inc(setup_done, 1)

            def finish_tile(m, s, q):
                v.wait_ge(x2_landed[s], 16 * (q + 1))
                v.wait_ge(out_stored[s], 16 * (q + 1))
                v.wait_ge(final_psum, m + 1)
                v.tensor_tensor(out_t[:, s, :], x2_back[:, s, :], bank[7][:, 0:C], ALU.add).then_inc(out_ready, 1)

            def head_maxima(m):
                v.wait_ge(logits_psum, m + 1)
                v.tensor_reduce(head_max[:, :], bank[5][:, :].rearrange("p (h g) -> p h g", h=H), AX_X, ALU.max)
                v.drain()
                v.tensor_scalar(head_neg[:, :], head_max[:, :], -1.0, None, ALU.mult).then_inc(max_ready, 1)

            def slice_weights(m):
                v.wait_ge(exp_ready, m + 1)
                v.reciprocal(head_rec[:, :], head_sum[:, :])
                v.drain()
                v.tensor_tensor(sw[:, :].rearrange("p (h g) -> p h g", h=H),
                                expo[:, :].rearrange("p (h g) -> p h g", h=H),
                                head_rec[:, :].unsqueeze(2).to_broadcast([P, H, G]), ALU.mult
                                ).then_inc(sw_ready, 1)

            def add_norm(m):
                v.wait_ge(norm_psum, m + 1)
                v.tensor_tensor(norm_sum[:, :], norm_sum[:, :], bank[6][:, 508:512], ALU.add).then_inc(norm_used, 1)

            def pair(b, i, prepare, finish, mixing):
                p = b * PAIRS + i
                for s in range(2):
                    n = 2 * p + s
                    v.wait_ge(rows_gathered[s], 16 * S * (p + 1))
                    if exists(n + 2):
                        table_indices(s)
                    v.tensor_reduce(agg[:, :], gathered[:, s, :].rearrange("p (k c) -> p c k", k=S), AX_X, ALU.max
                                    ).then_inc(gather_free, 1)
                    v.drain()
                    v.tensor_scalar(agg_f[:, :], agg[:, :], floor[:, s:s + 1], None, ALU.max).then_inc(agg_ready, 1)
                    if mixing:
                        mix_steps(b, i, s, 0)
                    if exists(n - 1):
                        head_maxima(n - 1)
                    for slot, q in to_normalise(p, s, prepare):
                        ln1_stats(slot, q + 1)
                    if exists(n + 4):
                        make_keys(n + 4)
                    if exists(n + 2):
                        maximum_floor(s)
                    if exists(n + 4):
                        top32(by_segment, by_column)
                    elif exists(n + 3):
                        top32(by_column)
                    if mixing:
                        mix_steps(b, i, s, 1)
                    if exists(n - 1):
                        slice_weights(n - 1)
                    v.wait_ge(x_landed[s], 16 * (p + 1))
                    v.wait_ge(x2_stored[s], 16 * (p + 1))
                    v.wait_ge(gnn_psum, n + 1)
                    v.scalar_tensor_tensor(out=x2[:, s, :], in0=bank[4][:, 0:C], scalar=0.0, in1=x_t[:, s, :],
                                           op0=ALU.max, op1=ALU.add).then_inc(x2_ready, 1)
                    v.drain()
                    v.bn_stats(stats2[:, :], x2[:, s, :]).then_inc(x_free, 1)
                    v.drain()
                    v.bn_aggr(mv2[:, :], stats2[:, :]).then_inc(ln2_var_ready, 1)
                    if exists(n + 4):
                        unpack_segments()
                    if finish and exists(n - LAG):
                        finish_tile(n - LAG, s, p - LAG // 2)
                    if exists(n - 1):
                        add_norm(n - 1)
                    if mixing:
                        mix_steps(b, i, s, 2)

            def copy_sums(done):
                v.drain()
                v.tensor_copy(snorm[:, :], norm_sum[:, :])
                v.drain()
                v.memset(norm_sum[:, :], 0.0)
                v.wait_ge(sums_psum, done)
                v.tensor_copy(tok_sum[:, 1, :], bank[1][:, :]).then_inc(sums_copied, 1)

            def slice_tokens(done):
                by_head = "p (h c) -> p h c"
                v.wait_ge(slices_psum, done)
                v.tensor_scalar(den[:, :], bank[6][0:G, 0:H], 1e-5, None, ALU.add)
                v.tensor_tensor(u[:, :].rearrange(by_head, h=H), bfx[:, :].rearrange(by_head, h=H),
                                bank[6][0:G, 0:H].unsqueeze(2).to_broadcast([G, H, HP]), ALU.mult)
                v.drain()
                v.reciprocal(rden[:, :], den[:, :])
                v.tensor_tensor(u[:, :], u[:, :], bank[2][0:G, :], ALU.add)
                v.drain()
                v.tensor_tensor(u[:, :].rearrange(by_head, h=H), u[:, :].rearrange(by_head, h=H),
                                rden[:, :].unsqueeze(2).to_broadcast([G, H, HP]), ALU.mult).then_inc(u_ready, 1)

            def conv_taps(done):
                v.wait_ge(v_psum, done)
                taps = conv_bc[:, :].rearrange("p (c k) -> p k c", k=K3)
                for k in range(K3):
                    v.tensor_tensor(v3[:, k, 0:DI], bank[2][0:G, :], taps[:, k, 0:DI], ALU.mult)
                    last = v.tensor_tensor(v3[:, k, DI:CONV], bank[6][0:G, 0:2 * NS], taps[:, k, DI:CONV], ALU.mult)
                last.then_inc(v3_ready, 1)

            def decays(done):
                v.wait_ge(softplus_parts, done)
                v.scalar_tensor_tensor(out=dt_v[:, :], in0=dt_y[:, :], scalar=0.0, in1=dt_l[:, :],
                                       op0=ALU.max, op1=ALU.add)
                v.tensor_scalar(z_r, z_e, 1.0, None, ALU.add)
                v.drain()
                v.tensor_copy(dt_blocks[0:32, 0:G], dt_v[0:32, :])
                v.tensor_copy(dt_blocks[32:64, G:P], dt_v[32:64, :])
                v.tensor_scalar(log_decay[:, :], dt_v[:, :], neg_a[:, 0:1], None, ALU.mult)
                v.reciprocal(z_r, z_r)
                v.drain()
                v.memset(log_decay[:, 0:1], -1e30).then_inc(log_decay_ready, 1)
                v.tensor_tensor(z_r, z_r, bank[2][0:G, :], ALU.mult).then_inc(z_used, 1)

            def conv_silu(done):
                v.wait_ge(conv_exp, done)
                v.tensor_scalar(xbc[:, :], xbc[:, :], 1.0, None, ALU.add)
                v.drain()
                v.reciprocal(xbc[:, :], xbc[:, :])
                v.drain()
                v.tensor_tensor(xbc[:, 0:DI], xbc[:, 0:DI], bank[2][:, :], ALU.mult)
                v.tensor_tensor(xbc[:, DI:CONV], xbc[:, DI:CONV], bank[6][:, 0:2 * NS], ALU.mult
                                ).then_inc(xbc_ready, 1)

            def scan_decays(done):
                v.wait_ge(spread_psum, done)
                v.tensor_tensor_scan(prod, bank[2][:, :], delta[:, :, :].rearrange("p h t -> p (h t)"),
                                     0.0, ALU.mult, ALU.add).then_inc(scanned, 1)

            def mixing_weights(done):
                prod3 = prod.rearrange("p (h t) -> p h t", h=H)
                dt_col = bank[6][:, 256:256 + H]
                v.wait_ge(gram_psum, done)
                v.tensor_copy(gram[0:G, :], bank[6][0:G, 264:264 + G])
                v.tensor_copy(gram[G:P, :], bank[6][G:P, 264 + G:264 + P])
                v.drain()
                v.tensor_tensor(prod3, prod3, gram[:, :].unsqueeze(1).to_broadcast([P, H, G]), ALU.mult)
                v.drain()
                v.tensor_tensor(w_mix[0:G, :, 1:G], prod3[0:G, :, 0:G - 1],
                                dt_col[0:G].unsqueeze(2).to_broadcast([G, H, G - 1]), ALU.mult)
                v.tensor_tensor(w_mix[G:P, :, 0:G - 1], prod3[G:P, :, G - 2::-1],
                                dt_col[G:P].unsqueeze(2).to_broadcast([G, H, G - 1]), ALU.mult
                                ).then_inc(wmix_ready, 1)

            def gate(done):
                v.wait_ge(y_psum, done)
                v.tensor_tensor(y1[:, :].rearrange("p (h c) -> p h c", h=H),
                                xbc[0:G, 0:DI].rearrange("p (h c) -> p h c", h=H),
                                bank[6][0:G, 400:400 + H].unsqueeze(2).to_broadcast([G, H, HP]), ALU.mult)
                v.drain()
                v.tensor_tensor(y1[:, :], y1[:, :], bank[2][0:G, :], ALU.add)
                v.drain()
                v.tensor_tensor(yg, y1[:, :], z_r, ALU.mult)
                v.drain()
                v.tensor_tensor_reduce(out=ysq, in0=yg, in1=yg, scale=1.0, scalar=0.0,
                                       op0=ALU.mult, op1=ALU.add, accum_out=ss[:, :]).then_inc(ss_ready, 1)

            def divide_by_root(done):
                v.wait_ge(rs_ready, done)
                v.tensor_scalar(yg, yg, rs[:, 1:2], None, ALU.mult).then_inc(yg_ready, 1)

            def pair_outputs(done):
                v.wait_ge(ot_psum, done)
                ot = bank[2][:, 0:4 * G].rearrange("p (m g) -> p m g", m=4)
                v.tensor_copy(ot_pair[0:G, :, 0:G], ot[0:G])
                v.tensor_copy(ot_pair[G:P, :, G:P], ot[G:P]).then_inc(ot_ready, 1)

            def keep_mix(done):
                v.wait_ge(mix_psum, done)
                v.tensor_copy(mix[:, 2, :], bank[6][:, 0:C])
                v.wait_ge(mix3_psum, done)
                v.tensor_copy(mix[:, 3, :], bank[2][:, 0:C]).then_inc(mix_ready, 1)

            steps = {(1, 0): (copy_sums,), (1, 2): (slice_tokens,), (2, 2): (conv_taps,), (4, 0): (decays,),
                     (5, 0): (conv_silu,), (5, 2): (scan_decays,), (6, 1): (mixing_weights,), (7, 0): (gate,),
                     (7, 1): (divide_by_root,), (8, 1): (pair_outputs,), (9, 2): (keep_mix,)}

            def mix_steps(b, i, s, point):
                for step in steps.get((2 * i + s, point), ()):
                    step(b)

            over_batches(v, pair)
            head_maxima(TOTAL - 1)
            slice_weights(TOTAL - 1)
            add_norm(TOTAL - 1)
            for i in range(MIX_PAIRS):
                for s in range(2):
                    mix_steps(B, i, s, 0)
                    mix_steps(B, i, s, 1)
                    finish_tile(TOTAL - LAG + 2 * i + s, s, (TOTAL - LAG) // 2 + i)
                    mix_steps(B, i, s, 2)
            with v.Fori((TOTAL - TILES) // 2, TOTAL // 2) as q:
                for s in range(2):
                    finish_tile(2 * q + s, s, q)

        @block.scalar
        def _(act):
            def normalise(dst, src, mv, part, ready):
                nc.scalar.activation(part[:, 0:1], mv[:, 1:2], ACT.Ln, bias=eps_col[:, 0:1])
                nc.scalar.activation(part[:, 2:3], mv[:, 0:1], ACT.Copy, scale=-1.0)
                act.drain()
                nc.scalar.activation(part[:, 1:2], part[:, 0:1], ACT.Exp, scale=-0.5)
                act.drain()
                nc.scalar.activation(part[:, 3:4], part[:, 2:3], ACT.Identity, scale=part[:, 1:2])
                act.drain()
                nc.scalar.activation(dst, src, ACT.Identity, scale=part[:, 1:2], bias=part[:, 3:4]
                                     ).then_inc(ready, 1)

            def normalise1(m, s, q):
                act.wait_ge(table_stored[s], 16 * (q + 1))
                act.wait_ge(ln1_var_ready, m + 1)
                normalise(ln_out[:, s, :], ln_x[:, s, :], mv1[:, s, :], rstd1, normed_ready)

            def make_mask(m):
                act.wait_ge(adj_landed, 16 * (m + 1))
                if not isinstance(m, int) or m > 0:
                    act.wait_ge(bits_psum, m)
                nc.scalar.activation(mask[:, :], adj_t[:, :], ACT.Sign).then_inc(adj_used, 1)
                act.drain()
                nc.scalar.activation(mask[:, :], mask[:, :], ACT.Square).then_inc(masked, 1)

            def exponentials(m):
                act.wait_ge(max_ready, m + 1)
                for h in range(H):
                    cols = slice(h * G, (h + 1) * G)
                    last = nc.scalar.activation(expo[:, cols], bank[5][:, cols], ACT.Exp, bias=head_neg[:, h:h + 1],
                                                accum_out=head_sum[:, h:h + 1])
                last.then_inc(exp_ready, 1)

            def keep_turned(m, s, q):
                act.wait_ge(swt_stored[s], 16 * (q + 1))
                act.wait_ge(swt_psum, m + 1)
                nc.scalar.activation(swt_out[:, s, :], bank[3][:, :], ACT.Copy).then_inc(swt_kept, 1)
                act.wait_ge(swt_kept, m + 3)
                act.dma_start(turned[bass.ds(m * P, P), :], swt_out[:, s, :]).then_inc(swt_stored[s], 16)

            act.preload_act_table_set("natural_log_exp_and_others")
            act.wait_ge(consts_ready, 1)
            make_mask(0)
            with act.Fori(0, PAIRS) as i:
                for s in range(2):
                    normalise1(2 * i + s, s, i)
            for m in range(1, 5):
                make_mask(m)
            act.wait_ge(a_log_capped, 1)
            nc.scalar.activation(neg_a[:, :], neg_a[:, :], ACT.Exp).then_inc(neg_a_ready, 1)

            def pair(b, i, prepare, finish, mixing):
                p = b * PAIRS + i
                for s in range(2):
                    n = 2 * p + s
                    if mixing:
                        mix_steps(b, i, s, 0)
                    if exists(n - 1):
                        exponentials(n - 1)
                    for slot, q in to_normalise(p, s, prepare):
                        normalise1(2 * q + slot, slot, q)
                    act.wait_ge(h_psum, n + 1)
                    nc.scalar.activation(h_t[:, :, :], bank[3][:, :].rearrange("p (m c) -> p m c", m=4), ACT.Copy
                                         ).then_inc(h_ready, 1)
                    if exists(n + 5):
                        make_mask(n + 5)
                    if mixing:
                        mix_steps(b, i, s, 1)
                    if exists(n - 1):
                        keep_turned(n - 1, 1 - s, p - 1 + s)
                    act.wait_ge(ln2_var_ready, n + 1)
                    normalise(xn2[:, s, :], x2[:, s, :], mv2, rstd2, xn2_ready)
                    act.wait_ge(xn2t_psum, n + 1)
                    nc.scalar.activation(xn2_t[:, :, :], bank[4][:, C:2 * C].rearrange("p (m c) -> p m c", m=2),
                                         ACT.Copy).then_inc(xn2t_ready, 1)
                    if mixing and (2 * i + s, 2) in steps:
                        act.wait_ge(norm_used, n + 1)
                        mix_steps(b, i, s, 2)

            def copy_sums(done):
                act.wait_ge(sums_psum, done)
                nc.scalar.activation(tok_sum[:, 0, :], bank[0][:, :], ACT.Copy).then_inc(sums_copied, 1)

            def copy_u(done):
                act.wait_ge(ut_psum, done)
                nc.scalar.activation(u_t[:, :, :], bank[6][:, 0:4 * G].rearrange("p (m g) -> p m g", m=4), ACT.Copy
                                     ).then_inc(ut_ready, 1)

            def softplus(done):
                act.wait_ge(zdt_psum, done)
                nc.scalar.activation(dt_y[0:32, :], bank[6][0:32, P:P + G], ACT.Identity, bias=dt_b[0:32, 0:1])
                nc.scalar.activation(dt_y[32:64, :], bank[6][32:64, P:P + G][:, ::-1], ACT.Identity,
                                     bias=dt_b[32:64, 0:1])
                act.drain()
                nc.scalar.activation(dt_a[:, :], dt_y[:, :], ACT.Abs)
                nc.scalar.activation(z_e, bank[2][0:G, :], ACT.Exp, scale=-1.0)
                act.drain()
                nc.scalar.activation(dt_a[:, :], dt_a[:, :], ACT.Exp, scale=-1.0)
                act.drain()
                nc.scalar.activation(dt_l[:, :], dt_a[:, :], ACT.Ln, bias=ones_col[0:G, 0:1]
                                     ).then_inc(softplus_parts, 1)

            def exp_decays(done):
                act.wait_ge(log_decay_ready, done)
                nc.scalar.activation(decay[:, :], log_decay[:, :], ACT.Exp).then_inc(decay_ready, 1)

            def conv_exps(done):
                act.wait_ge(conv_psum, done)
                nc.scalar.activation(xbc[:, 0:DI], bank[2][:, :], ACT.Exp, scale=-1.0)
                nc.scalar.activation(xbc[:, DI:CONV], bank[6][:, 0:2 * NS], ACT.Exp, scale=-1.0
                                     ).then_inc(conv_exp, 1)

            def copy_bc(done):
                act.wait_ge(spread_psum, done)
                nc.scalar.activation(bc_t, bank[6][0:G, 0:2 * P], ACT.Copy).then_inc(spread_copied, 1)

            def copy_xs(done):
                act.wait_ge(gram_psum, done)
                nc.scalar.activation(xs_t[:, :, :], bank[2][:, 0:4 * G].rearrange("p (m g) -> p m g", m=4), ACT.Copy
                                     ).then_inc(xs_copied, 1)

            def root_mean_square(done):
                act.wait_ge(ss_ready, done)
                nc.scalar.activation(rs[:, 0:1], ss[:, :], ACT.Ln, scale=1.0 / DI, bias=eps_col[0:G, 0:1])
                act.drain()
                nc.scalar.activation(rs[:, 1:2], rs[:, 0:1], ACT.Exp, scale=-0.5).then_inc(rs_ready, 1)

            def copy_yg(done):
                act.wait_ge(ygt_psum, done)
                nc.scalar.activation(yg_t[:, :, :], bank[6][:, 0:4 * G].rearrange("p (m g) -> p m g", m=4), ACT.Copy
                                     ).then_inc(ygt_ready, 1)

            def keep_mix(done):
                act.wait_ge(mix_psum, done)
                nc.scalar.activation(mix[:, 0:2, :], bank[2][:, :].rearrange("p (m c) -> p m c", m=2), ACT.Copy
                                     ).then_inc(mix_half, 1)

            steps = {(1, 0): (copy_sums,), (2, 0): (copy_u,), (3, 2): (softplus,), (4, 2): (exp_decays, conv_exps),
                     (5, 2): (copy_bc,), (6, 1): (copy_xs,), (7, 0): (root_mean_square,), (7, 2): (copy_yg,),
                     (9, 2): (keep_mix,)}

            def mix_steps(b, i, s, point):
                for step in steps.get((2 * i + s, point), ()):
                    step(b)

            over_batches(act, pair)
            exponentials(TOTAL - 1)
            keep_turned(TOTAL - 1, 1, TOTAL // 2 - 1)
            act.wait_ge(norm_used, TOTAL + 1)
            for at in sorted(steps):
                if keep_mix in steps[at]:
                    act.wait_ge(swcur_free, TOTAL - TILES + 2)
                for step in steps[at]:
                    step(B)

        @block.tensor
        def _(pe):
            mm = nc.tensor.matmul

            def open_sums():
                for k in range(2):
                    mm(bank[k][:, :], zeros[0:1, 0:P], zeros[0:1, 0:1].to_broadcast([1, DI]), start=True, stop=False,
                       skip_group_check=True)

            def turn(bank_cols, source, size=P):
                return mm(bank_cols, source, ident[0:size, 0:size], start=True, stop=True)

            def finish_tile(m, s, loads, mixes):
                pe.wait_ge(mix_ready, mixes)
                pe.wait_ge(swcur_landed[s], 16 * loads)
                for k in range(4):
                    last = mm(bank[7][:, 0:C], sw_cur[:, s, k * P:(k + 1) * P], mix[:, k, :],
                              start=(k == 0), stop=False)
                last.then_inc(swcur_free, 1)
                mm(bank[7][:, 0:C], ones[:, :], bout[:, :], start=False, stop=True).then_inc(final_psum, 1)

            def pack_bits(m):
                pe.wait_ge(masked, m + 1)
                if not isinstance(m, int) or m > 0:
                    pe.wait_ge(keys_ready, m)
                columns = mask[:, :].rearrange("p (g e) -> p e g", e=SEG)
                for e in range(SEG):
                    last = mm(bank[7][:, C:2 * C], pack[:, e, :], columns[:, e, :], start=(e == 0), stop=(e == SEG - 1))
                last.then_inc(bits_psum, 1)

            def add_slices(m, s):
                pe.wait_ge(sw_ready, m + 1)
                for k in range(4):
                    last = nc.tensor.transpose(bank[3][:, k * P:(k + 1) * P], sw[:, k * P:(k + 1) * P], ident[:, :])
                last.then_inc(swt_psum, 1)
                pe.wait_ge(norm_used, m + 1)
                for k in range(4):
                    last = mm(bank[6][:, 508 + k:509 + k], sw[:, k * P:(k + 1) * P], ones_col[:, :],
                              start=True, stop=True)
                last.then_inc(norm_psum, 1)
                for k in range(2):
                    mm(bank[k][:, :], xn2[:, s, k * P:(k + 1) * P], sw[:, :], start=False, stop=False,
                       skip_group_check=True)

            pe.wait_ge(consts_ready, 1)
            pack_bits(0)
            pe.wait_ge(slices_landed, 16 * N_SLICE_LOADS)
            for k in range(2):
                for m in range(4):
                    last = mm(bank[3 + k][:, m * P:(m + 1) * P], w_x_raw[:, m, k * P:(k + 1) * P], slice_pair[:, :],
                              start=True, stop=True)
                last.then_inc(setup_psum, 1)
            for m in range(4):
                mm(bank[5][0:1, m * P:(m + 1) * P], bx_col[:, m:m + 1], slice_pair[:, :], start=True, stop=False)
                last = mm(bank[5][0:1, m * P:(m + 1) * P], ones[0:1, 0:1], b_slice2[:, :], start=False, stop=True)
            last.then_inc(setup_psum, 1)
            for m in range(1, 5):
                pack_bits(m)
            pe.wait_ge(dve_consts, 1)
            open_sums()
            pe.sem_inc(swcur_free, 2)
            pe.sem_inc(xn_free, 2)
            pe.wait_ge(setup_done, 1)
            pe.wait_ge(weights_landed, 16 * N_WEIGHTS)

            def pair(b, i, prepare, finish, mixing):
                p = b * PAIRS + i
                for s in range(2):
                    n = 2 * p + s
                    pe.wait_ge(swt_kept, n + 1)
                    pe.wait_ge(xn_landed[s], 16 * (p + 1))
                    for k in range(2):
                        last = nc.tensor.transpose(bank[3][:, k * P:(k + 1) * P], xn_t[:, s, k * P:(k + 1) * P],
                                                   ident[:, :])
                    last.then_inc(xn_free, 1)
                    if mixing and (2 * i + s, 0) in steps:
                        pe.wait_ge(norm_used, n)
                        mix_steps(b, i, s, 0)
                    pe.wait_ge(agg_ready, n + 1)
                    for k in range(2):
                        last = nc.tensor.transpose(bank[3][:, (2 + k) * P:(3 + k) * P], agg_f[:, k * P:(k + 1) * P],
                                                   ident[:, :])
                    last.then_inc(h_psum, 1)
                    pe.wait_ge(h_ready, n + 1)
                    for k in range(4):
                        mm(bank[4][:, 0:C], h_t[:, k, :], wg[:, k, :], start=(k == 0), stop=False)
                    mm(bank[4][:, 0:C], ones[:, :], wg_b[:, :], start=False, stop=True).then_inc(gnn_psum, 1)
                    if finish:
                        pe.wait_ge(out_ready, n - LAG + 2)
                    if exists(n + 5):
                        pack_bits(n + 5)
                    else:
                        pe.wait_ge(keys_ready, TOTAL)
                    if finish:
                        finish_tile(n - LAG, s, p - LAG // 2 + 1, b - 1 if mixing else b)
                    if mixing:
                        mix_steps(b, i, s, 1)
                    if exists(n - 1):
                        add_slices(n - 1, 1 - s)
                    pe.wait_ge(xn2_ready, n + 1)
                    for k in range(2):
                        last = nc.tensor.transpose(bank[4][:, C + k * P:C + (k + 1) * P],
                                                   xn2[:, s, k * P:(k + 1) * P], ident[:, :])
                    last.then_inc(xn2t_psum, 1)
                    pe.wait_ge(xn2t_ready, n + 1)
                    for k in range(2):
                        mm(bank[5][:, :], xn2_t[:, k, :], wlog[:, k, :], start=(k == 0), stop=False)
                    mm(bank[5][:, :], ones[:, :], blog[:, :], start=False, stop=True).then_inc(logits_psum, 1)
                    if mixing and (2 * i + s, 2) in steps:
                        pe.wait_ge(norm_used, n + 1)
                        mix_steps(b, i, s, 2)

            def close_sums(done):
                for k in range(2):
                    last = mm(bank[k][:, :], zeros[0:1, 0:P], zeros[0:1, 0:1].to_broadcast([1, DI]), start=False,
                              stop=True, skip_group_check=True)
                last.then_inc(sums_psum, 1)

            def slice_tokens(done):
                pe.wait_ge(sums_copied, 2 * done)
                open_sums()
                for h in range(H):
                    cols = slice(h * HP, (h + 1) * HP)
                    for k in range(2):
                        mm(bank[2][0:G, cols], tok_sum[:, k, cols], wfx[:, k, cols], start=(k == 0), stop=(k == 1))
                for j in range(2):
                    last = mm(bank[6][0:G, 0:H].rearrange("p (m j) -> p j m", j=2)[:, j, :],
                              ident[:, j * G:(j + 1) * G], snorm[:, :], start=True, stop=True)
                last.then_inc(slices_psum, 1)

            def turn_tokens(done):
                pe.wait_ge(u_ready, done)
                for k in range(4):
                    last = turn(bank[6][:, k * G:(k + 1) * G], u[:, k * P:(k + 1) * P], G)
                last.then_inc(ut_psum, 1)

            def project_xbc(done):
                pe.wait_ge(ut_ready, done)
                for dst, c0, c1 in ((bank[2][0:G, :], DI, 2 * DI), (bank[6][0:G, 0:2 * NS], 2 * DI, DI + CONV)):
                    for k in range(4):
                        last = mm(dst, u_t[:, k, :], w_in[:, k, c0:c1], start=(k == 0), stop=(k == 3))
                last.then_inc(v_psum, 1)

            def project_gate(done):
                pe.wait_ge(v3_ready, done)
                for k in range(4):
                    mm(bank[6][0:G, P:P + G], w_dt[:, k, :], u_t[:, k, :], start=(k == 0), stop=(k == 3))
                for k in range(4):
                    last = mm(bank[2][0:G, :], u_t[:, k, :], w_in[:, k, 0:DI], start=(k == 0), stop=(k == 3))
                last.then_inc(zdt_psum, 1)

            def convolve(done):
                pe.wait_ge(z_used, done)
                for dst, c0, c1 in ((bank[2][:, :], 0, DI), (bank[6][:, 0:2 * NS], DI, CONV)):
                    for k in range(K3):
                        mm(dst, shift[:, k, :], v3[:, k, c0:c1], start=(k == 0), stop=False)
                    last = mm(dst, ones[:, :], convb[:, c0:c1], start=False, stop=True)
                last.then_inc(conv_psum, 1)

            def spread(done):
                pe.wait_ge(decay_ready, done)
                pe.wait_ge(xbc_ready, done)
                for h in range(H):
                    mm(bank[2][:, h * G:(h + 1) * G], head_sel[:, h, :], decay[:, :], start=True, stop=True)
                mm(bank[6][:, 256:256 + H], dt_blocks[:, :], head_of_row[:, :], start=True, stop=True)
                for j in range(2):
                    last = turn(bank[6][0:G, j * P:(j + 1) * P], xbc[:, DI + j * NS:DI + (j + 1) * NS])
                last.then_inc(spread_psum, 1)

            def correlate(done):
                pe.wait_ge(scanned, done)
                pe.wait_ge(spread_copied, done)
                for k in range(4):
                    turn(bank[2][:, k * G:(k + 1) * G], xbc[0:G, k * P:(k + 1) * P], G)
                mm(bank[6][:, 264:264 + P], bc_t[:, 0:P], bc_t[:, P:2 * P], start=True, stop=True
                   ).then_inc(gram_psum, 1)

            def outputs(done):
                pe.wait_ge(xs_copied, done)
                pe.wait_ge(wmix_ready, done)
                for k in range(4):
                    mm(bank[6][0:G, 400:400 + H], xs_t[:, k, :], fcd[:, k, :], start=(k == 0), stop=False)
                mm(bank[6][0:G, 400:400 + H], ones[0:1, 0:G], dskip[:, :], start=False, stop=True)
                for h in range(H):
                    last = mm(bank[2][0:G, h * HP:(h + 1) * HP], w_mix[:, h, :], xbc[:, h * HP:(h + 1) * HP],
                              start=True, stop=True)
                last.then_inc(y_psum, 1)

            def turn_outputs(done):
                pe.wait_ge(yg_ready, done)
                for k in range(4):
                    last = turn(bank[6][:, k * G:(k + 1) * G], yg[:, k * P:(k + 1) * P], G)
                last.then_inc(ygt_psum, 1)

            def project_out(done):
                pe.wait_ge(ygt_ready, done)
                for m in range(4):
                    for k in range(4):
                        last = mm(bank[2][:, m * G:(m + 1) * G], w_hyout[:, k, m * P:(m + 1) * P], yg_t[:, k, :],
                                  start=(k == 0), stop=(k == 3))
                last.then_inc(ot_psum, 1)

            def make_mix(done):
                pe.wait_ge(ot_ready, done)
                for m in range(3):
                    dst = bank[2][:, m * C:(m + 1) * C] if m < 2 else bank[6][:, 0:C]
                    last = mm(dst, ot_pair[:, m, :], w_out[:, m, :], start=True, stop=True)
                last.then_inc(mix_psum, 1)

            def end_mix(done):
                pe.wait_ge(mix_half, done)
                mm(bank[2][:, 0:C], ot_pair[:, 3, :], w_out[:, 3, :], start=True, stop=True).then_inc(mix3_psum, 1)

            steps = {(0, 2): (close_sums,), (1, 1): (slice_tokens,), (2, 0): (turn_tokens,), (2, 1): (project_xbc,),
                     (3, 0): (project_gate,), (4, 1): (convolve,), (5, 1): (spread,), (6, 0): (correlate,),
                     (6, 2): (outputs,), (7, 1): (turn_outputs,), (8, 0): (project_out,), (9, 0): (make_mix,),
                     (9, 2): (end_mix,)}

            def mix_steps(b, i, s, point):
                for step in steps.get((2 * i + s, point), ()):
                    step(b)

            over_batches(pe, pair)
            add_slices(TOTAL - 1, 1)
            pe.wait_ge(norm_used, TOTAL + 1)
            for i in range(MIX_PAIRS):
                for s in range(2):
                    mix_steps(B, i, s, 0)
                    mix_steps(B, i, s, 1)
                    pe.wait_ge(out_ready, TOTAL - LAG + 2 * i + s + 2)
                    finish_tile(TOTAL - LAG + 2 * i + s, s, (TOTAL - LAG) // 2 + i + 1, B - 1)
                    mix_steps(B, i, s, 2)
            with pe.Fori((TOTAL - TILES) // 2, TOTAL // 2) as q:
                for s in range(2):
                    pe.wait_ge(out_ready, 2 * q + s + 2)
                    finish_tile(2 * q + s, s, q + 1, B)


def kernel(x, adj, L0_gnn_W, L0_gnn_b, L0_ffn_W_fx, L0_ffn_b_fx, L0_ffn_W_x, L0_ffn_b_x, L0_ffn_W_slice,
           L0_ffn_b_slice, L0_ffn_temperature, L0_ffn_hy_in_w, L0_ffn_hy_conv_w, L0_ffn_hy_conv_b,
           L0_ffn_hy_dt_bias, L0_ffn_hy_A_log, L0_ffn_hy_D, L0_ffn_hy_fcD_w, L0_ffn_hy_norm_w,
           L0_ffn_hy_out_w, L0_ffn_out_w, L0_ffn_out_b):
    import numpy as np
    import concourse.bacc as bacc
    from concourse.bass_utils import run_bass_kernel_spmd

    a = np.asarray
    arrays = {
        "x": a(x), "adj": a(adj), "gnn_w": a(L0_gnn_W), "gnn_b": a(L0_gnn_b).reshape(1, -1),
        "wfx_t": a(L0_ffn_W_fx).T, "b_fx": a(L0_ffn_b_fx), "w_x": a(L0_ffn_W_x),
        "b_x": a(L0_ffn_b_x).reshape(4, 128).T, "wslice_t": a(L0_ffn_W_slice).T,
        "b_slice": a(L0_ffn_b_slice).reshape(1, -1), "temperature": a(L0_ffn_temperature).reshape(-1),
        "in_w_t": a(L0_ffn_hy_in_w).T, "conv_w": a(L0_ffn_hy_conv_w).reshape(-1),
        "conv_b": a(L0_ffn_hy_conv_b).reshape(1, -1), "dt_bias": a(L0_ffn_hy_dt_bias).reshape(-1, 1),
        "a_log": a(L0_ffn_hy_A_log).reshape(-1, 1), "d_skip": a(L0_ffn_hy_D).reshape(1, -1),
        "fcd_t": a(L0_ffn_hy_fcD_w).T, "norm_w": a(L0_ffn_hy_norm_w).reshape(4, 128).T,
        "hyout_t": a(L0_ffn_hy_out_w).T, "out_w_t": a(L0_ffn_out_w).T, "out_b": a(L0_ffn_out_b).reshape(1, -1),
    }
    nc = bacc.Bacc("TRN2", target_bir_lowering=False, num_devices=1)
    inputs, args = {}, {}
    for name, array in arrays.items():
        inputs[f"in_{name}"] = np.ascontiguousarray(array)
        args[name] = nc.dram_tensor(f"in_{name}", array.shape, mybir.dt.from_np(array.dtype),
                                    kind="ExternalInput").ap()
    args["out"] = nc.dram_tensor("out_x", (B, N, C), F32, kind="ExternalOutput").ap()
    adj_ffn(nc, **args)
    run = run_bass_kernel_spmd(nc, [inputs], core_ids=[0])
    return run.results[0]["out_x"]
```

```python
from contextlib import ExitStack

import concourse.bass as bass
from concourse import mybir

F32 = mybir.dt.float32
BF16 = mybir.dt.bfloat16
I32 = mybir.dt.int32
U32 = mybir.dt.uint32
ALU = mybir.AluOpType
ACT = mybir.ActivationFunctionType
AX_X = mybir.AxisListType.X

P = 128
B, N, C = 8, 2048, 256
H, HP, G = 8, 64, 64
DI = H * HP
NS = 64
CONV = DI + 2 * NS
K3 = 3
S = 25
TILES = N // P
PAIRS = TILES // 2
SEG = 8
NSEG = N // SEG
CAND = S + 1
TOP = 32
ROWS = N + 1
LN_EPS = 1e-5
BIG = 3.0e38
TOTAL = B * TILES
MIX_PAIRS = 5
LAG = TILES + 2 * MIX_PAIRS
CHUNK = 4
CATCH_UP = TOTAL - 4
LEFT = CATCH_UP - LAG + 2 * (TOTAL - CATCH_UP)


def adj_ffn(nc, x, adj, gnn_w, gnn_b, wfx_t, b_fx, w_x, b_x, wslice_t, b_slice, temperature,
            in_w_t, conv_w, conv_b, dt_bias, a_log, d_skip, fcd_t, norm_w, hyout_t, out_w_t, out_b, out):
    x_rows = x.rearrange("b n c -> (b n) c")
    out_rows = out.rearrange("b n c -> (b n) c")
    adj_rows = adj.rearrange("b n m -> (b n) m")
    tables = [nc.dram_tensor(f"normed_table{j}", (ROWS, C), F32, kind="Internal").ap() for j in range(2)]
    x2_rows = nc.dram_tensor("x2_rows", (B * N, C), F32, kind="Internal").ap()
    turned = nc.dram_tensor("turned_weights", (B * N, DI), F32, kind="Internal").ap()

    with ExitStack() as ctx:
        def sb(name, shape, dt=F32):
            return ctx.enter_context(nc.sbuf_tensor("sb_" + name, shape, dt))

        def sem(name):
            return ctx.enter_context(nc.semaphore(name))

        bank = [ctx.enter_context(nc.psum_tensor(f"bank{i}", [P, 512], F32)) for i in range(8)]

        ident = sb("ident", [P, P])
        ones = sb("ones", [1, P])
        ones_col = sb("ones_col", [P, 1])
        eps_col = sb("eps_col", [P, 1])
        zeros = sb("zeros", [1, C])
        pack = sb("pack", [P, SEG, P], BF16)
        bit_mask = sb("bit_mask", [P, SEG], I32)
        bit_index = sb("bit_index", [P, SEG])
        seg_base = sb("seg_base", [P, NSEG])
        shift = sb("shift", [G, K3, P])
        head_sel = sb("head_sel", [G, H, P])
        head_of_row = sb("head_of_row", [G, H])
        delta = sb("delta", [P, H, G])

        wg = sb("gnn_w", [P, 4, C])
        wg_b = sb("gnn_b", [1, C])
        wfx = sb("wfx", [P, 2, DI])
        bfx = sb("bfx", [G, DI])
        wlog = sb("wlog", [P, 2, DI])
        blog = sb("blog", [1, DI])
        rtemp = sb("rtemp", [P, H])
        slice_pair = sb("slice_pair", [P, P])
        b_slice2 = sb("b_slice2", [1, P])
        bx_col = sb("bx_col", [P, 4])
        w_in = sb("w_in", [P, 4, 2 * DI + 2 * NS])
        w_dt = sb("w_dt", [P, 4, G])
        conv_bc = sb("conv_bc", [G, CONV * K3])
        convb = sb("convb", [1, CONV])
        dt_b = sb("dt_b", [G, 1])
        neg_a = sb("neg_a", [G, 1])
        dskip = sb("dskip", [1, H])
        fcd = sb("fcd", [P, 4, H])
        normw = sb("normw", [P, 4])
        w_hyout = sb("w_hyout", [P, 4, DI])
        w_out = sb("w_out", [P, 4, C])
        bout = sb("bout", [1, C])

        adj_t = sb("adj_t", [P, N], I32)
        keys = sb("keys", [P, NSEG])
        mask = sb("mask", [P, N], BF16)
        top_keys = sb("top_keys", [P, TOP])
        top_int = sb("top_int", [P, TOP], I32)
        top_base = sb("top_base", [P, TOP], I32)
        cand_bit = sb("cand_bit", [P, CAND, SEG], I32)
        cand = sb("cand", [P, CAND, SEG])
        first = sb("first", [P, TOP])
        indices = sb("indices", [P, 2, TOP], U32)
        floor = sb("floor", [P, 2])
        gathered = sb("gathered", [P, 2, S * C])
        agg = sb("agg", [P, C])
        agg_f = sb("agg_f", [P, C])
        x_t = sb("x_t", [P, 2, C])
        xn_t = sb("xn_t", [P, 2, C])
        h_t = sb("h_t", [P, 4, P])
        x2 = sb("x2", [P, 2, C])
        x2_back = sb("x2_back", [P, 2, C])
        stats2 = sb("stats2", [P, 6])
        mv2 = sb("mv2", [P, 2])
        rstd2 = sb("rstd2", [P, 4])
        xn2 = sb("xn2", [P, 2, C])
        xn2_t = sb("xn2_t", [P, 2, P])
        head_max = sb("head_max", [P, H])
        head_neg = sb("head_neg", [P, H])
        norm_sum = sb("norm_sum", [P, 4])
        head_sum = sb("head_sum", [P, H])
        head_rec = sb("head_rec", [P, H])
        expo = sb("expo", [P, DI])
        sw = sb("sw", [P, DI])
        swt_out = sb("swt_out", [P, 2, DI])
        sw_cur = sb("sw_cur", [P, 2, DI])
        out_t = sb("out_t", [P, 2, C])
        ln_x = sb("ln_x", [P, 2, C])
        ln_out = sb("ln_out", [P, 2, C])
        stats1 = sb("stats1", [P, 2, 6])
        mv1 = sb("mv1", [P, 2, 2])
        rstd1 = sb("rstd1", [P, 4])

        tok_sum = sb("tok_sum", [P, 2, DI])
        snorm = sb("snorm", [P, 4])
        den = sb("den", [G, H])
        rden = sb("rden", [G, H])
        u = sb("u", [G, DI])
        u_t = sb("u_t", [P, 4, G])
        v3 = sb("v3", [G, K3, CONV])
        dt_y = sb("dt_y", [G, G])
        dt_a = sb("dt_a", [G, G])
        dt_l = sb("dt_l", [G, G])
        dt_v = sb("dt_v", [G, G])
        dt_blocks = sb("dt_blocks", [G, P])
        log_decay = sb("log_decay", [G, G])
        decay = sb("decay", [G, G])
        xbc = sb("xbc", [P, CONV])
        gram = sb("gram", [P, G])
        w_mix = sb("w_mix", [P, H, G])
        z_e = sb("z_e", [G, DI])
        z_r = sb("z_r", [G, DI])
        prod = sb("prod", [P, DI])
        bc_t = sb("bc_t", [G, 2 * P])
        xs_t = sb("xs_t", [P, 4, G])
        y1 = u
        ss = sb("ss", [G, 1])
        rs = sb("rs", [G, 2])
        yg_t = u_t
        z_e, z_r, prod, bc_t, yg, ysq = (t[:, :] for t in (z_e, z_r, prod, bc_t, z_e, z_r))
        ot_pair = sb("ot_pair", [P, 4, P])
        mix = sb("mix", [P, 4, C])

        w_x_raw = mix[:, :, :]

        first_x = gathered[:, 0, 0:TILES * C].rearrange("p (m c) -> p m c", m=TILES)
        first_stats = gathered[:, 1, 0:TILES * 6].rearrange("p (m c) -> p m c", m=TILES)
        first_mv = gathered[:, 1, TILES * 6:TILES * 8].rearrange("p (m c) -> p m c", m=TILES)
        first_rstd = gathered[:, 1, TILES * 8:TILES * 9]

        gathered_flat = gathered[:, :, :].rearrange("p s c -> p (s c)")
        last_sw = gathered_flat[:, 0:TILES * DI].rearrange("p (m c) -> p m c", m=TILES)
        last_x2 = gathered_flat[:, TILES * DI:TILES * (DI + C)].rearrange("p (m c) -> p m c", m=TILES)
        out_bias = gathered_flat[:, TILES * (DI + C):TILES * (DI + C) + C]

        out_bias_landed = sem("out_bias_landed")
        last_landed = [sem(f"last_landed{k}") for k in range(TILES // CHUNK)]
        last_stored = sem("last_stored")
        first_x_landed = [sem(f"first_x_landed{k}") for k in range(TILES // CHUNK)]
        first_table_stored = sem("first_table_stored")
        adj_landed = sem("adj_landed")
        x2_stored = [sem(f"x2_stored{s}") for s in range(2)]
        x2_landed = [sem(f"x2_landed{s}") for s in range(2)]
        swt_stored = [sem(f"swt_stored{s}") for s in range(2)]
        swcur_landed = [sem(f"swcur_landed{s}") for s in range(2)]
        x_landed = [sem(f"x_landed{s}") for s in range(2)]
        xn_landed = [sem(f"xn_landed{s}") for s in range(2)]
        lnx_landed = [sem(f"lnx_landed{s}") for s in range(2)]
        table_stored = [sem(f"table_stored{s}") for s in range(2)]
        zero_rows_stored = sem("zero_rows_stored")
        rows_gathered = [sem(f"rows_gathered{s}") for s in range(2)]
        out_stored = [sem(f"out_stored{s}") for s in range(2)]
        weights_landed = sem("weights_landed")
        slices_landed = sem("slices_landed")
        first_var_ready = sem("first_var_ready")
        first_rstd_ready = sem("first_rstd_ready")
        first_normed = sem("first_normed")
        consts_ready = sem("consts_ready")
        const_step = sem("const_step")
        dve_consts = sem("dve_consts")
        setup_psum = sem("setup_psum")
        setup_done = sem("setup_done")
        a_log_capped = sem("a_log_capped")
        neg_a_ready = sem("neg_a_ready")
        adj_used = sem("adj_used")
        indices_ready = sem("indices_ready")
        gather_free = sem("gather_free")
        gathers_begun = sem("gathers_begun")
        agg_ready = sem("agg_ready")
        ln1_var_ready = sem("ln1_var_ready")
        normed_ready = sem("normed_ready")
        h_psum = sem("h_psum")
        h_ready = sem("h_ready")
        gnn_psum = sem("gnn_psum")
        xn_free = sem("xn_free")
        x_free = sem("x_free")
        ln2_var_ready = sem("ln2_var_ready")
        x2_ready = sem("x2_ready")
        xn2_ready = sem("xn2_ready")
        xn2t_psum = sem("xn2t_psum")
        xn2t_ready = sem("xn2t_ready")
        logits_psum = sem("logits_psum")
        max_ready = sem("max_ready")
        masked = sem("masked")
        bits_psum = sem("bits_psum")
        keys_ready = sem("keys_ready")
        norm_psum = sem("norm_psum")
        norm_used = sem("norm_used")
        exp_ready = sem("exp_ready")
        sw_ready = sem("sw_ready")
        swt_psum = sem("swt_psum")
        swt_kept = sem("swt_kept")
        swcur_free = sem("swcur_free")
        final_psum = sem("final_psum")
        out_ready = sem("out_ready")
        sums_psum = sem("sums_psum")
        sums_copied = sem("sums_copied")
        slices_psum = sem("slices_psum")
        u_ready = sem("u_ready")
        ut_psum = sem("ut_psum")
        ut_ready = sem("ut_ready")
        v_psum = sem("v_psum")
        zdt_psum = sem("zdt_psum")
        z_used = sem("z_used")
        scanned = sem("scanned")
        xs_copied = sem("xs_copied")
        mix3_psum = sem("mix3_psum")
        mix_half = sem("mix_half")
        v3_ready = sem("v3_ready")
        softplus_parts = sem("softplus_parts")
        log_decay_ready = sem("log_decay_ready")
        decay_ready = sem("decay_ready")
        conv_psum = sem("conv_psum")
        conv_exp = sem("conv_exp")
        xbc_ready = sem("xbc_ready")
        spread_psum = sem("spread_psum")
        spread_copied = sem("spread_copied")
        gram_psum = sem("gram_psum")
        wmix_ready = sem("wmix_ready")
        y_psum = sem("y_psum")
        ss_ready = sem("ss_ready")
        rs_ready = sem("rs_ready")
        yg_ready = sem("yg_ready")
        ygt_psum = sem("ygt_psum")
        ygt_ready = sem("ygt_ready")
        ot_psum = sem("ot_psum")
        ot_ready = sem("ot_ready")
        mix_psum = sem("mix_psum")
        mix_ready = sem("mix_ready")

        N_WEIGHTS = 20
        N_SLICE_LOADS = 7

        block = ctx.enter_context(nc.Block())

        def exists(m):
            return not isinstance(m, int) or 0 <= m < TOTAL

        def pairs(eng, b, start, pair, *flags):
            if start < PAIRS - 3:
                with eng.Fori(start, PAIRS - 2) as i:
                    pair(b, i, 1, *flags)
            else:
                pair(b, start, 1, *flags)
            pair(b, PAIRS - 2, 2, *flags)
            pair(b, PAIRS - 1, 0, *flags)

        def over_batches(eng, pair):
            pair(0, 0, 1, False, False)
            pairs(eng, 0, 1, pair, False, False)
            for i in range(MIX_PAIRS):
                pair(1, i, 1, False, True)
            pairs(eng, 1, MIX_PAIRS, pair, True, False)
            with eng.Fori(2, B - 1) as b:
                for i in range(MIX_PAIRS):
                    pair(b, i, 1, True, True)
                pairs(eng, b, MIX_PAIRS, pair, True, False)
            for i in range(PAIRS):
                pair(B - 1, i, 0, True, i < MIX_PAIRS)

        def over_batches_by_table(eng, pair):
            pair(0, 0, 1, False, 0)
            pairs(eng, 0, 1, pair, False, 0)
            with eng.Fori(0, MIX_PAIRS) as i:
                pair(1, i, 1, False, 1)
            pairs(eng, 1, MIX_PAIRS, pair, True, 1)
            with eng.Fori(0, (B - 4) // 2) as j:
                for own in range(2):
                    pairs(eng, 2 * j + 2 + own, 0, pair, True, own)
            pairs(eng, B - 2, 0, pair, True, 0)
            with eng.Fori(0, PAIRS - 3) as i:
                pair(B - 1, i, 0, True, 1)
            for i in range(PAIRS - 3, PAIRS):
                pair(B - 1, i, 0, True, 1)

        def to_finish(n, p, s):
            if isinstance(n, int) and n >= CATCH_UP:
                start = CATCH_UP - LAG + 2 * (n - CATCH_UP)
                return [(m, m % 2, m // 2) for m in (start, start + 1)]
            return [(n - LAG, s, p - LAG // 2)]

        LAST_BANKS = (7, 5, 4, 3)

        left_made = {(0, 2): (LEFT,), (2, 1): (LEFT + 1,), (3, 0): (LEFT + 2, LEFT + 3), (4, 1): (LEFT + 4,),
                     (6, 2): (LEFT + 5,)}
        left_added = {(1, 0): (LEFT,), (2, 2): (LEFT + 1, LEFT + 2), (4, 0): (LEFT + 3,), (5, 0): (LEFT + 4,),
                      (7, 1): (LEFT + 5,)}

        def to_normalise(p, s, prepare):
            if prepare == 2:
                return [(slot, p + PAIRS + s) for slot in range(2)]
            return [(s, p + PAIRS)] if prepare else []

        @block.sync
        def _(sp):
            for k in range(TILES // CHUNK):
                rows = slice(k * CHUNK * P, (k + 1) * CHUNK * P)
                sp.dma_start(first_x[:, k * CHUNK:(k + 1) * CHUNK, :], x_rows[rows, :].rearrange("(m p) c -> p m c", p=P)
                             ).then_inc(first_x_landed[k], 16)
            sp.dma_start(adj_t[:, :], adj_rows[0:P, :]).then_inc(adj_landed, 16)
            sp.wait_ge(dve_consts, 1)
            for j in range(2):
                sp.dma_start(tables[j][N:ROWS, :], zeros[:, :]).then_inc(zero_rows_stored, 16)
            sp.dma_start(x_t[:, 0, :], x_rows[0:P, :]).then_inc(x_landed[0], 16)

            def load_adjacency(m):
                sp.wait_ge(adj_used, m)
                sp.dma_start(adj_t[:, :], adj_rows[m * P:(m + 1) * P, :]).then_inc(adj_landed, 16)

            load_adjacency(1)
            for k in range(TILES // CHUNK):
                rows = slice(k * CHUNK * P, (k + 1) * CHUNK * P)
                sp.wait_ge(first_normed, k + 1)
                sp.dma_start(tables[0][rows, :].rearrange("(m p) c -> p m c", p=P), first_x[:, k * CHUNK:(k + 1) * CHUNK, :]
                             ).then_inc(first_table_stored, 16)
            load_adjacency(2)

            sp.dma_start(slice_pair[0:G, 0:G], wslice_t).then_inc(slices_landed, 16)
            sp.dma_start(slice_pair[G:P, G:P], wslice_t).then_inc(slices_landed, 16)
            sp.dma_start(w_x_raw, w_x.rearrange("(m p) c -> p m c", p=P)).then_inc(slices_landed, 16)
            sp.dma_start(rtemp[:, :], temperature.partition_broadcast(P)).then_inc(slices_landed, 16)
            for j in range(2):
                sp.dma_start(b_slice2[0:1, j * G:(j + 1) * G], b_slice).then_inc(slices_landed, 16)
            sp.dma_start(bx_col[:, :], b_x).then_inc(slices_landed, 16)
            chunks = "(m p) c -> p m c"
            for dst, src in (
                (wg[:, :, :], gnn_w.rearrange(chunks, p=P)),
                (wg_b[:, :], gnn_b),
                (wfx[:, :, :], wfx_t.rearrange(chunks, p=P)),
                (bfx[:, :], b_fx.partition_broadcast(G)),
                (w_in[:, :, :], in_w_t[:, 0:DI + CONV].rearrange(chunks, p=P)),
                (w_dt[:, :, 0:H], in_w_t[:, DI + CONV:DI + CONV + H].rearrange(chunks, p=P)),
                (w_dt[:, :, 32:32 + H], in_w_t[:, DI + CONV + H:].rearrange(chunks, p=P)),
                (conv_bc[:, :], conv_w.partition_broadcast(G)),
                (convb[:, :], conv_b),
                (dt_b[0:H, :], dt_bias),
                (dt_b[32:32 + H, :], dt_bias),
                (neg_a[0:H, :], a_log),
                (neg_a[32:32 + H, :], a_log),
                (dskip[:, :], d_skip),
                (fcd[:, :, :], fcd_t.rearrange(chunks, p=P)),
                (normw[:, :], norm_w),
                (w_hyout[:, 0:2, :], hyout_t[0:2 * P].rearrange(chunks, p=P)),
                (w_hyout[:, 2:4, :], hyout_t[2 * P:].rearrange(chunks, p=P)),
                (w_out[:, :, :], out_w_t.rearrange(chunks, p=P)),
                (bout[:, :], out_b),
            ):
                sp.dma_start(dst, src).then_inc(weights_landed, 16)

            for m in range(3, 6):
                load_adjacency(m)
            sp.wait_ge(first_table_stored, 16 * TILES // CHUNK)

            def load_to_finish(m, s, loads):
                sp.wait_ge(swcur_free, m + 1)
                sp.wait_ge(swt_stored[s], 16 * loads + 16)
                sp.dma_start(sw_cur[:, s, :], turned[bass.ds(m * P, P), :]).then_inc(swcur_landed[s], 16)
                sp.wait_ge(out_ready, m + 1)
                sp.wait_ge(x2_stored[s], 16 * loads + 16)
                sp.dma_start(x2_back[:, s, :], x2_rows[bass.ds(m * P, P), :]).then_inc(x2_landed[s], 16)

            def store_finished(m, s):
                sp.wait_ge(out_ready, m + 3)
                sp.dma_start(out_rows[bass.ds(m * P, P), :], out_t[:, s, :]).then_inc(out_stored[s], 16)

            def pair(b, i, prepare, finish, own):
                p = b * PAIRS + i
                for s in range(2):
                    n = 2 * p + s
                    sp.wait_ge(xn_free, n + 1)
                    sp.wait_ge(table_stored[s], 16 * (p + 2))
                    sp.dma_start(xn_t[:, s, :], tables[own][bass.ds((2 * i + s) * P, P), :]).then_inc(xn_landed[s], 16)
                    if exists(n + 1):
                        sp.wait_ge(x_free, n + 1)
                        sp.dma_start(x_t[:, 1 - s, :], x_rows[bass.ds((n + 1) * P, P), :]
                                     ).then_inc(x_landed[1 - s], 16)
                    for slot, q in to_normalise(p, s, prepare):
                        sp.wait_ge(normed_ready, 2 * q + slot - 1)
                        sp.dma_start(ln_x[:, slot, :], x_rows[bass.ds((2 * q + slot) * P, P), :]
                                     ).then_inc(lnx_landed[slot], 16)
                    ending = to_finish(n, p, s) if finish else []
                    for m, slot, q in ending:
                        load_to_finish(m, slot, q + 1)
                    for slot, q in to_normalise(p, s, prepare):
                        row = (2 * i + s if prepare == 1 else 2 * (i + s) + slot) * P
                        sp.wait_ge(normed_ready, 2 * q + slot + 1)
                        sp.dma_start(tables[1 - own][bass.ds(row, P), :], ln_out[:, slot, :]
                                     ).then_inc(table_stored[slot], 16)
                    sp.wait_ge(x2_ready, n + 1)
                    sp.dma_start(x2_rows[bass.ds(n * P, P), :], x2[:, s, :]).then_inc(x2_stored[s], 16)
                    for m, slot, q in ending:
                        store_finished(m, slot)
                    if exists(n + 6):
                        sp.wait_ge(adj_used, n + 6)
                        sp.dma_start(adj_t[:, :], adj_rows[bass.ds((n + 6) * P, P), :]).then_inc(adj_landed, 16)

            over_batches_by_table(sp, pair)
            sp.wait_ge(gather_free, TOTAL + 2)
            sp.dma_start(out_bias, out_b[0, :].partition_broadcast(P)).then_inc(out_bias_landed, 16)
            for m in range(LEFT, LEFT + 2):
                load_to_finish(m, m % 2, m // 2 + 1)
            for m in range(LEFT, TOTAL - TILES):
                if m + 2 < TOTAL - TILES:
                    load_to_finish(m + 2, m % 2, m // 2 + 2)
                store_finished(m, m % 2)
                if m == LEFT:
                    for s in range(2):
                        sp.wait_ge(swt_stored[s], 16 * (TOTAL // 2 + 1))
                        sp.wait_ge(x2_stored[s], 16 * (TOTAL // 2 + 1))
                k = m - LEFT
                if k < TILES // CHUNK:
                    rows = slice((TOTAL - TILES + k * CHUNK) * P, (TOTAL - TILES + (k + 1) * CHUNK) * P)
                    for dst, src in ((last_sw, turned), (last_x2, x2_rows)):
                        sp.dma_start(dst[:, k * CHUNK:(k + 1) * CHUNK, :], src[rows, :].rearrange("(m p) c -> p m c", p=P)
                                     ).then_inc(last_landed[k], 16)
            for q in range(PAIRS):
                m = TOTAL - TILES + 2 * q
                sp.wait_ge(out_ready, m + 4)
                sp.dma_start(out_rows[m * P:(m + 2) * P, :].rearrange("(m p) c -> p m c", p=P),
                             last_x2[:, 2 * q:2 * q + 2, :]).then_inc(last_stored, 16)
            sp.wait_ge(last_stored, 16 * PAIRS)
            for s in range(2):
                sp.wait_ge(out_stored[s], 16 * ((TOTAL - TILES) // 2 + 1))
                sp.wait_ge(table_stored[s], 16 * (TOTAL // 2 + 1))
            sp.wait_ge(zero_rows_stored, 32)

        @block.gpsimd
        def _(pool):
            steps = [0]

            def stepped(ins):
                steps[0] += 1
                ins.then_inc(const_step, 1)

            def wait_steps():
                pool.wait_ge(const_step, steps[0])

            stepped(pool.memset(ident[:, :], 0.0))
            stepped(pool.memset(shift[:, :, :], 0.0))
            stepped(pool.memset(head_sel[:, :, :], 0.0))
            stepped(pool.memset(head_of_row[:, :], 0.0))
            stepped(pool.memset(ones[:, :], 1.0))
            stepped(pool.memset(ones_col[:, :], 1.0))
            stepped(pool.memset(eps_col[:, :], LN_EPS))
            stepped(pool.memset(dt_blocks[:, :], 0.0))
            stepped(pool.memset(ot_pair[:, :, :], 0.0))
            stepped(pool.memset(w_mix[:, :, :], 0.0))
            stepped(pool.iota(seg_base[:, :], pattern=[[-256, NSEG]], base=256 * NSEG, channel_multiplier=0,
                              allow_small_or_imprecise_dtypes=True))
            stepped(pool.iota(bit_index[:, :], pattern=[[1, SEG]], base=0, channel_multiplier=0,
                              allow_small_or_imprecise_dtypes=True))
            stepped(pool.memset(pack[:, :, :], 0.0))
            for e in range(SEG):
                stepped(pool.memset(bit_mask[:, e:e + 1], 1 << (SEG - 1 - e)))
            wait_steps()

            def diagonal(view, base, pattern, fill=1.0):
                stepped(pool.affine_select(out=view, in_=view, compare_op=ALU.not_equal, fill=fill, base=base,
                                           pattern=pattern, channel_multiplier=1))

            diagonal(ident[:, :], 0, [[-1, P]])
            for e in range(SEG):
                diagonal(pack[:, e, :], 0, [[-1, P]], fill=float(1 << (SEG - 1 - e)))
            for k in range(K3):
                diagonal(shift[:, k, 0:G], 2 - k, [[-1, G]])
                diagonal(shift[:, k, G:P], -(G - 3) - k, [[1, G]])
            diagonal(head_sel[0:32, :, 0:G], 0, [[-1, H], [0, G]])
            diagonal(head_of_row[0:32, :], 0, [[-1, H]])
            wait_steps()
            diagonal(head_sel[32:64, :, G:P], 0, [[-1, H], [0, G]])
            diagonal(head_of_row[32:64, :], 0, [[-1, H]])
            wait_steps()
            for h in range(H):
                stepped(pool.tensor_tensor(delta[:, h, :], ident[:, 0:G], ident[:, G:P], ALU.add))
            wait_steps()
            pool.sem_inc(consts_ready, 1)
            pool.wait_ge(zero_rows_stored, 32)
            pool.wait_ge(first_table_stored, 16 * TILES // CHUNK)

            def pair(b, i, prepare, finish, own):
                p = b * PAIRS + i
                for s in range(2):
                    n = 2 * p + s
                    pool.wait_ge(table_stored[0], 16 * (PAIRS * (b + 1) + 1))
                    pool.wait_ge(table_stored[1], 16 * (PAIRS * (b + 1) + 1))
                    pool.wait_ge(gather_free, n + 1)
                    pool.wait_ge(indices_ready, n + 1)
                    pool.sem_inc(gathers_begun, 1)
                    for k in range(S):
                        pool.indirect_dma_start(
                            out=gathered[:, s, k * C:(k + 1) * C], out_offset=None, in_=tables[own],
                            in_offset=bass.IndirectOffsetOnAxis(ap=indices[:, s, k:k + 1], axis=0),
                        ).then_inc(rows_gathered[s], 16)

            over_batches_by_table(pool, pair)

        @block.vector
        def _(v):
            def ln1_stats(s, loads):
                v.wait_ge(lnx_landed[s], 16 * loads)
                v.bn_stats(stats1[:, s, :], ln_x[:, s, :])
                v.drain()
                v.bn_aggr(mv1[:, s, :], stats1[:, s, :]).then_inc(ln1_var_ready, 1)

            def make_keys(m):
                v.wait_ge(bits_psum, m + 1)
                v.scalar_tensor_tensor(out=keys[:, :], in0=bank[7][:, C:2 * C], scalar=0.0, in1=seg_base[:, :],
                                       op0=ALU.is_gt, op1=ALU.mult)
                v.drain()
                v.tensor_tensor(keys[:, :], keys[:, :], bank[7][:, C:2 * C], ALU.add).then_inc(keys_ready, 1)

            def top32(*jobs):
                for r in range(TOP // 8):
                    v.drain()
                    for best, values in jobs:
                        v.max(best[:, 8 * r:8 * r + 8], values)
                    if r < TOP // 8 - 1:
                        v.drain()
                        for best, values in jobs:
                            v.match_replace(values, best[:, 8 * r:8 * r + 8], values, 0.0)

            by_segment = (top_keys, keys[:, :])
            by_column = (first, cand[:, :, :].rearrange("p s e -> p (s e)"))

            def unpack_segments():
                v.drain()
                v.tensor_copy(top_int[:, :], top_keys[:, :])
                v.drain()
                v.tensor_scalar(top_base[:, :], top_int[:, :], 5, 0xFFF8, ALU.logical_shift_right, ALU.bitwise_and)
                v.tensor_tensor(cand_bit[:, :, :], top_int[:, 0:CAND].unsqueeze(2).to_broadcast([P, CAND, SEG]),
                                bit_mask[:, :].unsqueeze(1).to_broadcast([P, CAND, SEG]), ALU.bitwise_and)
                v.drain()
                v.tensor_tensor(cand[:, :, :], top_base[:, 0:CAND].unsqueeze(2).to_broadcast([P, CAND, SEG]),
                                bit_index[:, :].unsqueeze(1).to_broadcast([P, CAND, SEG]), ALU.subtract)
                v.drain()
                v.scalar_tensor_tensor(out=cand[:, :, :].rearrange("p s e -> p (s e)"),
                                       in0=cand_bit[:, :, :].rearrange("p s e -> p (s e)"), scalar=0.0,
                                       in1=cand[:, :, :].rearrange("p s e -> p (s e)"),
                                       op0=ALU.is_gt, op1=ALU.mult)

            def table_indices(s):
                v.tensor_scalar(indices[:, s, 0:S], first[:, 0:S], -1.0, float(N), ALU.mult, ALU.add
                                ).then_inc(indices_ready, 1)

            def maximum_floor(s):
                v.tensor_scalar(floor[:, s:s + 1], first[:, S:S + 1], 0.0, -BIG, ALU.is_gt, ALU.mult)

            v.memset(zeros[:, :], 0.0)
            v.memset(slice_pair[:, :], 0.0)
            v.memset(w_dt[:, :, :], 0.0)
            v.memset(dt_b[:, :], 0.0)
            v.memset(neg_a[:, :], 0.0)
            v.memset(norm_sum[:, :], 0.0)
            v.drain()
            v.sem_inc(dve_consts, 1)
            v.sem_inc(gather_free, 2)
            v.sem_inc(x_free, 1)
            v.sem_inc(swt_kept, 2)
            v.sem_inc(out_ready, 2)
            v.sem_inc(norm_used, 1)
            for s in range(2):
                v.sem_inc(table_stored[s], 16)
                v.sem_inc(table_stored[s], 16 * PAIRS)
                v.sem_inc(lnx_landed[s], 16 * PAIRS)
                v.sem_inc(swt_stored[s], 16)
                v.sem_inc(x2_stored[s], 16)
                v.sem_inc(out_stored[s], 16)
            v.sem_inc(ln1_var_ready, TILES)
            v.sem_inc(normed_ready, TILES)

            for m in range(TILES):
                if m % CHUNK == 0:
                    v.wait_ge(first_x_landed[m // CHUNK], 16)
                v.bn_stats(first_stats[:, m, :], first_x[:, m, :])
            v.drain()
            for m in range(TILES):
                last = v.bn_aggr(first_mv[:, m, :], first_stats[:, m, :])
            last.then_inc(first_var_ready, 1)
            v.wait_ge(first_rstd_ready, 1)
            for m in range(TILES):
                last = v.tensor_scalar(first_x[:, m, :], first_x[:, m, :], first_mv[:, m, 0:1], first_rstd[:, m:m + 1],
                                       ALU.subtract, ALU.mult)
                if m % CHUNK == CHUNK - 1:
                    last.then_inc(first_normed, 1)

            v.wait_ge(consts_ready, 1)
            for m in range(4):
                make_keys(m)
                top32(by_segment)
                unpack_segments()
                if m < 3:
                    top32(by_column)
                if m < 2:
                    v.drain()
                    table_indices(m)
                    maximum_floor(m)

            v.wait_ge(slices_landed, 16 * N_SLICE_LOADS)
            v.tensor_scalar(rtemp[:, :], rtemp[:, :], 1e-6, None, ALU.max)
            v.drain()
            v.reciprocal(rtemp[:, :], rtemp[:, :])
            v.drain()
            for k in range(2):
                v.wait_ge(setup_psum, k + 1)
                v.tensor_tensor(wlog[:, k, :].rearrange("p (h g) -> p h g", h=H),
                                bank[3 + k][:, :].rearrange("p (h g) -> p h g", h=H),
                                rtemp[:, :].unsqueeze(2).to_broadcast([P, H, G]), ALU.mult)
            v.wait_ge(setup_psum, 3)
            v.tensor_tensor(blog[:, :].rearrange("p (h g) -> p h g", h=H),
                            bank[5][0:1, :].rearrange("p (h g) -> p h g", h=H),
                            rtemp[0:1, :].unsqueeze(2).to_broadcast([1, H, G]), ALU.mult)
            v.wait_ge(weights_landed, 16 * N_WEIGHTS)
            v.tensor_scalar(neg_a[:, :], neg_a[:, :], 88.0, None, ALU.min).then_inc(a_log_capped, 1)
            for k in range(4):
                v.tensor_scalar(w_hyout[:, k, :], w_hyout[:, k, :], normw[:, k:k + 1], None, ALU.mult)
            v.wait_ge(neg_a_ready, 1)
            v.tensor_scalar(neg_a[:, :], neg_a[:, :], -1.0, None, ALU.mult)
            v.drain()
            v.sem_inc(setup_done, 1)

            def finish_tile(m, s, q):
                v.wait_ge(x2_landed[s], 16 * (q + 1))
                v.wait_ge(out_stored[s], 16 * (q + 1))
                v.wait_ge(final_psum, m + 1)
                v.tensor_tensor(out_t[:, s, :], x2_back[:, s, :], bank[7][:, 0:C], ALU.add).then_inc(out_ready, 1)

            def head_maxima(m):
                v.wait_ge(logits_psum, m + 1)
                v.tensor_reduce(head_max[:, :], bank[5][:, :].rearrange("p (h g) -> p h g", h=H), AX_X, ALU.max)
                v.drain()
                v.tensor_scalar(head_neg[:, :], head_max[:, :], -1.0, None, ALU.mult).then_inc(max_ready, 1)

            def slice_weights(m):
                v.wait_ge(exp_ready, m + 1)
                v.reciprocal(head_rec[:, :], head_sum[:, :])
                v.drain()
                v.tensor_tensor(sw[:, :].rearrange("p (h g) -> p h g", h=H),
                                expo[:, :].rearrange("p (h g) -> p h g", h=H),
                                head_rec[:, :].unsqueeze(2).to_broadcast([P, H, G]), ALU.mult
                                ).then_inc(sw_ready, 1)

            def add_norm(m):
                v.wait_ge(norm_psum, m + 1)
                v.tensor_tensor(norm_sum[:, :], norm_sum[:, :], bank[6][:, 508:512], ALU.add).then_inc(norm_used, 1)

            def pair(b, i, prepare, finish, mixing):
                p = b * PAIRS + i
                for s in range(2):
                    n = 2 * p + s
                    v.wait_ge(rows_gathered[s], 16 * S * (p + 1))
                    if exists(n + 2):
                        table_indices(s)
                    v.tensor_reduce(agg[:, :], gathered[:, s, :].rearrange("p (k c) -> p c k", k=S), AX_X, ALU.max
                                    ).then_inc(gather_free, 1)
                    v.drain()
                    v.tensor_scalar(agg_f[:, :], agg[:, :], floor[:, s:s + 1], None, ALU.max).then_inc(agg_ready, 1)
                    ending = to_finish(n, p, s) if finish else []
                    for m, slot, q in ending[:-1]:
                        finish_tile(m, slot, q)
                    if mixing:
                        mix_steps(b, i, s, 0)
                    if exists(n - 1):
                        head_maxima(n - 1)
                    for slot, q in to_normalise(p, s, prepare):
                        ln1_stats(slot, q + 1)
                    if exists(n + 4):
                        make_keys(n + 4)
                    if exists(n + 2):
                        maximum_floor(s)
                    if exists(n + 4):
                        top32(by_segment, by_column)
                    elif exists(n + 3):
                        top32(by_column)
                    if mixing:
                        mix_steps(b, i, s, 1)
                    if exists(n - 1):
                        slice_weights(n - 1)
                    v.wait_ge(x_landed[s], 16 * (p + 1))
                    v.wait_ge(x2_stored[s], 16 * (p + 1))
                    v.wait_ge(gnn_psum, n + 1)
                    v.scalar_tensor_tensor(out=x2[:, s, :], in0=bank[4][:, 0:C], scalar=0.0, in1=x_t[:, s, :],
                                           op0=ALU.max, op1=ALU.add).then_inc(x2_ready, 1)
                    v.drain()
                    v.bn_stats(stats2[:, :], x2[:, s, :]).then_inc(x_free, 1)
                    v.drain()
                    v.bn_aggr(mv2[:, :], stats2[:, :]).then_inc(ln2_var_ready, 1)
                    if exists(n + 4):
                        unpack_segments()
                    for m, slot, q in ending[-1:]:
                        finish_tile(m, slot, q)
                    if exists(n - 1):
                        add_norm(n - 1)
                    if mixing:
                        mix_steps(b, i, s, 2)

            def copy_sums(done):
                v.drain()
                v.tensor_copy(snorm[:, :], norm_sum[:, :])
                v.drain()
                v.memset(norm_sum[:, :], 0.0)
                v.wait_ge(sums_psum, done)
                v.tensor_copy(tok_sum[:, 1, :], bank[1][:, :]).then_inc(sums_copied, 1)

            def slice_tokens(done):
                by_head = "p (h c) -> p h c"
                v.wait_ge(slices_psum, done)
                v.tensor_scalar(den[:, :], bank[6][0:G, 0:H], 1e-5, None, ALU.add)
                v.tensor_tensor(u[:, :].rearrange(by_head, h=H), bfx[:, :].rearrange(by_head, h=H),
                                bank[6][0:G, 0:H].unsqueeze(2).to_broadcast([G, H, HP]), ALU.mult)
                v.drain()
                v.reciprocal(rden[:, :], den[:, :])
                v.tensor_tensor(u[:, :], u[:, :], bank[2][0:G, :], ALU.add)
                v.drain()
                v.tensor_tensor(u[:, :].rearrange(by_head, h=H), u[:, :].rearrange(by_head, h=H),
                                rden[:, :].unsqueeze(2).to_broadcast([G, H, HP]), ALU.mult).then_inc(u_ready, 1)

            def conv_taps(done):
                v.wait_ge(v_psum, done)
                taps = conv_bc[:, :].rearrange("p (c k) -> p k c", k=K3)
                for k in range(K3):
                    v.tensor_tensor(v3[:, k, 0:DI], bank[2][0:G, :], taps[:, k, 0:DI], ALU.mult)
                    last = v.tensor_tensor(v3[:, k, DI:CONV], bank[6][0:G, 0:2 * NS], taps[:, k, DI:CONV], ALU.mult)
                last.then_inc(v3_ready, 1)

            def decays(done):
                v.wait_ge(softplus_parts, done)
                v.scalar_tensor_tensor(out=dt_v[:, :], in0=dt_y[:, :], scalar=0.0, in1=dt_l[:, :],
                                       op0=ALU.max, op1=ALU.add)
                v.tensor_scalar(z_e, z_e, 1.0, None, ALU.add)
                v.drain()
                v.tensor_copy(dt_blocks[0:32, 0:G], dt_v[0:32, :])
                v.tensor_copy(dt_blocks[32:64, G:P], dt_v[32:64, :])
                v.tensor_scalar(log_decay[:, :], dt_v[:, :], neg_a[:, 0:1], None, ALU.mult)
                v.drain()
                v.memset(log_decay[:, 0:1], -1e30).then_inc(log_decay_ready, 1)
                v.reciprocal(z_e, z_e)
                v.drain()
                v.tensor_tensor(z_r, z_r, z_e, ALU.mult)

            def conv_silu(done):
                v.wait_ge(conv_exp, done)
                for part, conv in ((slice(DI, CONV), bank[6][:, 0:2 * NS]), (slice(0, DI), prod)):
                    v.tensor_scalar(xbc[:, part], xbc[:, part], 1.0, None, ALU.add)
                    v.drain()
                    v.reciprocal(xbc[:, part], xbc[:, part])
                    v.drain()
                    last = v.tensor_tensor(xbc[:, part], xbc[:, part], conv, ALU.mult)
                    if part.start == DI:
                        last.then_inc(xbc_ready, 1)
                v.drain()

            def scan_decays(done):
                v.wait_ge(spread_psum, done)
                v.tensor_tensor_scan(prod, bank[2][:, :], delta[:, :, :].rearrange("p h t -> p (h t)"),
                                     0.0, ALU.mult, ALU.add).then_inc(scanned, 1)

            def mixing_weights(done):
                prod3 = prod.rearrange("p (h t) -> p h t", h=H)
                dt_col = bank[6][:, 256:256 + H]
                v.wait_ge(gram_psum, done)
                v.tensor_copy(gram[0:G, :], bank[6][0:G, 264:264 + G])
                v.tensor_copy(gram[G:P, :], bank[6][G:P, 264 + G:264 + P])
                v.drain()
                v.tensor_tensor(prod3, prod3, gram[:, :].unsqueeze(1).to_broadcast([P, H, G]), ALU.mult)
                v.drain()
                v.tensor_tensor(w_mix[0:G, :, 1:G], prod3[0:G, :, 0:G - 1],
                                dt_col[0:G].unsqueeze(2).to_broadcast([G, H, G - 1]), ALU.mult)
                v.tensor_tensor(w_mix[G:P, :, 0:G - 1], prod3[G:P, :, G - 2::-1],
                                dt_col[G:P].unsqueeze(2).to_broadcast([G, H, G - 1]), ALU.mult
                                ).then_inc(wmix_ready, 1)

            def gate(done):
                v.wait_ge(y_psum, done)
                v.tensor_tensor(y1[:, :].rearrange("p (h c) -> p h c", h=H),
                                xbc[0:G, 0:DI].rearrange("p (h c) -> p h c", h=H),
                                bank[6][0:G, 400:400 + H].unsqueeze(2).to_broadcast([G, H, HP]), ALU.mult)
                v.drain()
                v.tensor_tensor(y1[:, :], y1[:, :], bank[2][0:G, :], ALU.add)
                v.drain()
                v.tensor_tensor(yg, y1[:, :], z_r, ALU.mult)
                v.drain()
                v.tensor_tensor_reduce(out=ysq, in0=yg, in1=yg, scale=1.0, scalar=0.0,
                                       op0=ALU.mult, op1=ALU.add, accum_out=ss[:, :]).then_inc(ss_ready, 1)

            def divide_by_root(done):
                v.wait_ge(rs_ready, done)
                v.tensor_scalar(yg, yg, rs[:, 1:2], None, ALU.mult).then_inc(yg_ready, 1)

            def pair_outputs(done):
                v.wait_ge(ot_psum, done)
                ot = bank[2][:, 0:4 * G].rearrange("p (m g) -> p m g", m=4)
                v.tensor_copy(ot_pair[0:G, :, 0:G], ot[0:G])
                v.tensor_copy(ot_pair[G:P, :, G:P], ot[G:P]).then_inc(ot_ready, 1)

            def keep_mix(done):
                v.wait_ge(mix_psum, done)
                v.tensor_copy(mix[:, 2, :], bank[6][:, 0:C])
                v.wait_ge(mix3_psum, done)
                v.tensor_copy(mix[:, 3, :], bank[2][:, 0:C]).then_inc(mix_ready, 1)

            steps = {(1, 0): (copy_sums,), (1, 2): (slice_tokens,), (2, 2): (conv_taps,), (4, 0): (decays,),
                     (5, 0): (conv_silu,), (5, 2): (scan_decays,), (6, 1): (mixing_weights,), (7, 0): (gate,),
                     (7, 1): (divide_by_root,), (8, 1): (pair_outputs,), (9, 2): (keep_mix,)}

            def mix_steps(b, i, s, point):
                for step in steps.get((2 * i + s, point), ()):
                    step(b)

            over_batches(v, pair)
            head_maxima(TOTAL - 1)
            slice_weights(TOTAL - 1)
            add_norm(TOTAL - 1)
            for at in sorted(steps):
                for step in steps[at]:
                    step(B)
                for m in left_added.get(at, ()):
                    finish_tile(m, m % 2, m // 2)
                if divide_by_root in steps[at]:
                    v.wait_ge(out_bias_landed, 16)
                    for k in range(TILES // CHUNK):
                        v.wait_ge(last_landed[k], 32)
                        chunk = last_x2[:, k * CHUNK:(k + 1) * CHUNK, :]
                        v.tensor_tensor(chunk, chunk, out_bias.unsqueeze(1).to_broadcast([P, CHUNK, C]), ALU.add)
            v.drain()
            for j in range(TILES):
                v.wait_ge(final_psum, TOTAL - TILES + j + 1)
                v.tensor_tensor(last_x2[:, j, :], last_x2[:, j, :], bank[LAST_BANKS[j % 4]][:, 0:C], ALU.add
                                ).then_inc(out_ready, 1)

        @block.scalar
        def _(act):
            def normalise(dst, src, mv, part, ready):
                nc.scalar.activation(part[:, 0:1], mv[:, 1:2], ACT.Ln, bias=eps_col[:, 0:1])
                nc.scalar.activation(part[:, 2:3], mv[:, 0:1], ACT.Copy, scale=-1.0)
                act.drain()
                nc.scalar.activation(part[:, 1:2], part[:, 0:1], ACT.Exp, scale=-0.5)
                act.drain()
                nc.scalar.activation(part[:, 3:4], part[:, 2:3], ACT.Identity, scale=part[:, 1:2])
                act.drain()
                nc.scalar.activation(dst, src, ACT.Identity, scale=part[:, 1:2], bias=part[:, 3:4]
                                     ).then_inc(ready, 1)

            def normalise1(m, s, q):
                act.wait_ge(table_stored[s], 16 * (q + 1))
                act.wait_ge(ln1_var_ready, m + 1)
                normalise(ln_out[:, s, :], ln_x[:, s, :], mv1[:, s, :], rstd1, normed_ready)

            def make_mask(m):
                act.wait_ge(adj_landed, 16 * (m + 1))
                if not isinstance(m, int) or m > 0:
                    act.wait_ge(bits_psum, m)
                nc.scalar.activation(mask[:, :], adj_t[:, :], ACT.Sign).then_inc(adj_used, 1)
                act.drain()
                nc.scalar.activation(mask[:, :], mask[:, :], ACT.Square).then_inc(masked, 1)

            def exponentials(m):
                act.wait_ge(max_ready, m + 1)
                for h in range(H):
                    cols = slice(h * G, (h + 1) * G)
                    last = nc.scalar.activation(expo[:, cols], bank[5][:, cols], ACT.Exp, bias=head_neg[:, h:h + 1],
                                                accum_out=head_sum[:, h:h + 1])
                last.then_inc(exp_ready, 1)

            def keep_turned(m, s, q):
                act.wait_ge(swt_stored[s], 16 * (q + 1))
                act.wait_ge(swt_psum, m + 1)
                nc.scalar.activation(swt_out[:, s, :], bank[3][:, :], ACT.Copy).then_inc(swt_kept, 1)
                act.wait_ge(swt_kept, m + 3)
                act.dma_start(turned[bass.ds(m * P, P), :], swt_out[:, s, :]).then_inc(swt_stored[s], 16)

            act.preload_act_table_set("natural_log_exp_and_others")
            act.wait_ge(consts_ready, 1)
            act.wait_ge(first_var_ready, 1)
            nc.scalar.activation(first_rstd, first_mv[:, :, 1], ACT.Ln, bias=eps_col[:, 0:1])
            act.drain()
            nc.scalar.activation(first_rstd, first_rstd, ACT.Exp, scale=-0.5).then_inc(first_rstd_ready, 1)
            for m in range(5):
                make_mask(m)
            act.wait_ge(a_log_capped, 1)
            nc.scalar.activation(neg_a[:, :], neg_a[:, :], ACT.Exp).then_inc(neg_a_ready, 1)

            def pair(b, i, prepare, finish, mixing):
                p = b * PAIRS + i
                for s in range(2):
                    n = 2 * p + s
                    if mixing:
                        mix_steps(b, i, s, 0)
                    if exists(n - 1):
                        exponentials(n - 1)
                    for slot, q in to_normalise(p, s, prepare):
                        normalise1(2 * q + slot, slot, q)
                    act.wait_ge(h_psum, n + 1)
                    nc.scalar.activation(h_t[:, :, :], bank[3][:, :].rearrange("p (m c) -> p m c", m=4), ACT.Copy
                                         ).then_inc(h_ready, 1)
                    if exists(n + 5):
                        make_mask(n + 5)
                    if mixing:
                        mix_steps(b, i, s, 1)
                    if exists(n - 1):
                        keep_turned(n - 1, 1 - s, p - 1 + s)
                    act.wait_ge(ln2_var_ready, n + 1)
                    normalise(xn2[:, s, :], x2[:, s, :], mv2, rstd2, xn2_ready)
                    act.wait_ge(xn2t_psum, n + 1)
                    nc.scalar.activation(xn2_t[:, :, :], bank[4][:, C:2 * C].rearrange("p (m c) -> p m c", m=2),
                                         ACT.Copy).then_inc(xn2t_ready, 1)
                    if mixing and (2 * i + s, 2) in steps:
                        act.wait_ge(norm_used, n + 1)
                        mix_steps(b, i, s, 2)

            def copy_sums(done):
                act.wait_ge(sums_psum, done)
                nc.scalar.activation(tok_sum[:, 0, :], bank[0][:, :], ACT.Copy).then_inc(sums_copied, 1)

            def copy_u(done):
                act.wait_ge(ut_psum, done)
                nc.scalar.activation(u_t[:, :, :], bank[6][:, 0:4 * G].rearrange("p (m g) -> p m g", m=4), ACT.Copy
                                     ).then_inc(ut_ready, 1)

            def softplus(done):
                act.wait_ge(zdt_psum, done)
                nc.scalar.activation(dt_y[0:32, :], bank[6][0:32, P:P + G], ACT.Identity, bias=dt_b[0:32, 0:1])
                nc.scalar.activation(dt_y[32:64, :], bank[6][32:64, P:P + G][:, ::-1], ACT.Identity,
                                     bias=dt_b[32:64, 0:1])
                act.drain()
                nc.scalar.activation(dt_a[:, :], dt_y[:, :], ACT.Abs)
                nc.scalar.activation(z_e, bank[2][0:G, :], ACT.Exp, scale=-1.0)
                nc.scalar.activation(z_r, bank[2][0:G, :], ACT.Copy).then_inc(z_used, 1)
                act.drain()
                nc.scalar.activation(dt_a[:, :], dt_a[:, :], ACT.Exp, scale=-1.0)
                act.drain()
                nc.scalar.activation(dt_l[:, :], dt_a[:, :], ACT.Ln, bias=ones_col[0:G, 0:1]
                                     ).then_inc(softplus_parts, 1)

            def exp_decays(done):
                act.wait_ge(log_decay_ready, done)
                nc.scalar.activation(decay[:, :], log_decay[:, :], ACT.Exp).then_inc(decay_ready, 1)

            def conv_exps(done):
                act.wait_ge(conv_psum, done)
                nc.scalar.activation(xbc[:, 0:DI], bank[2][:, :], ACT.Exp, scale=-1.0)
                nc.scalar.activation(xbc[:, DI:CONV], bank[6][:, 0:2 * NS], ACT.Exp, scale=-1.0)
                nc.scalar.activation(prod, bank[2][:, :], ACT.Copy).then_inc(conv_exp, 1)

            def copy_bc(done):
                act.wait_ge(spread_psum, done)
                nc.scalar.activation(bc_t, bank[6][0:G, 0:2 * P], ACT.Copy).then_inc(spread_copied, 1)

            def copy_xs(done):
                act.wait_ge(gram_psum, done)
                nc.scalar.activation(xs_t[:, :, :], bank[2][:, 0:4 * G].rearrange("p (m g) -> p m g", m=4), ACT.Copy
                                     ).then_inc(xs_copied, 1)

            def root_mean_square(done):
                act.wait_ge(ss_ready, done)
                nc.scalar.activation(rs[:, 0:1], ss[:, :], ACT.Ln, scale=1.0 / DI, bias=eps_col[0:G, 0:1])
                act.drain()
                nc.scalar.activation(rs[:, 1:2], rs[:, 0:1], ACT.Exp, scale=-0.5).then_inc(rs_ready, 1)

            def copy_yg(done):
                act.wait_ge(ygt_psum, done)
                nc.scalar.activation(yg_t[:, :, :], bank[6][:, 0:4 * G].rearrange("p (m g) -> p m g", m=4), ACT.Copy
                                     ).then_inc(ygt_ready, 1)

            def keep_mix(done):
                act.wait_ge(mix_psum, done)
                nc.scalar.activation(mix[:, 0:2, :], bank[2][:, :].rearrange("p (m c) -> p m c", m=2), ACT.Copy
                                     ).then_inc(mix_half, 1)

            steps = {(1, 0): (copy_sums,), (2, 0): (copy_u,), (3, 2): (softplus,), (4, 2): (exp_decays, conv_exps),
                     (5, 2): (copy_bc,), (6, 1): (copy_xs,), (7, 0): (root_mean_square,), (7, 2): (copy_yg,),
                     (9, 2): (keep_mix,)}

            def mix_steps(b, i, s, point):
                for step in steps.get((2 * i + s, point), ()):
                    step(b)

            over_batches(act, pair)
            exponentials(TOTAL - 1)
            keep_turned(TOTAL - 1, 1, TOTAL // 2 - 1)
            act.wait_ge(norm_used, TOTAL + 1)
            for at in sorted(steps):
                if keep_mix in steps[at]:
                    act.wait_ge(swcur_free, TOTAL - TILES + 2)
                for step in steps[at]:
                    step(B)

        @block.tensor
        def _(pe):
            mm = nc.tensor.matmul

            def open_sums():
                for k in range(2):
                    mm(bank[k][:, :], zeros[0:1, 0:P], zeros[0:1, 0:1].to_broadcast([1, DI]), start=True, stop=False,
                       skip_group_check=True)

            def turn(bank_cols, source, size=P):
                return mm(bank_cols, source, ident[0:size, 0:size], start=True, stop=True)

            def finish_tile(m, s, loads, mixes):
                pe.wait_ge(mix_ready, mixes)
                pe.wait_ge(swcur_landed[s], 16 * loads)
                for k in range(4):
                    last = mm(bank[7][:, 0:C], sw_cur[:, s, k * P:(k + 1) * P], mix[:, k, :],
                              start=(k == 0), stop=False)
                last.then_inc(swcur_free, 1)
                mm(bank[7][:, 0:C], ones[:, :], bout[:, :], start=False, stop=True).then_inc(final_psum, 1)

            def pack_bits(m):
                pe.wait_ge(masked, m + 1)
                if not isinstance(m, int) or m > 0:
                    pe.wait_ge(keys_ready, m)
                columns = mask[:, :].rearrange("p (g e) -> p e g", e=SEG)
                for e in range(SEG):
                    last = mm(bank[7][:, C:2 * C], pack[:, e, :], columns[:, e, :], start=(e == 0), stop=(e == SEG - 1))
                last.then_inc(bits_psum, 1)

            def add_slices(m, s):
                pe.wait_ge(sw_ready, m + 1)
                for k in range(4):
                    last = nc.tensor.transpose(bank[3][:, k * P:(k + 1) * P], sw[:, k * P:(k + 1) * P], ident[:, :])
                last.then_inc(swt_psum, 1)
                pe.wait_ge(norm_used, m + 1)
                for k in range(4):
                    last = mm(bank[6][:, 508 + k:509 + k], sw[:, k * P:(k + 1) * P], ones_col[:, :],
                              start=True, stop=True)
                last.then_inc(norm_psum, 1)
                for k in range(2):
                    mm(bank[k][:, :], xn2[:, s, k * P:(k + 1) * P], sw[:, :], start=False, stop=False,
                       skip_group_check=True)

            pe.wait_ge(consts_ready, 1)
            pack_bits(0)
            pack_bits(1)
            pe.wait_ge(slices_landed, 16 * N_SLICE_LOADS)
            for k in range(2):
                for m in range(4):
                    last = mm(bank[3 + k][:, m * P:(m + 1) * P], w_x_raw[:, m, k * P:(k + 1) * P], slice_pair[:, :],
                              start=True, stop=True)
                last.then_inc(setup_psum, 1)
            for m in range(4):
                mm(bank[5][0:1, m * P:(m + 1) * P], bx_col[:, m:m + 1], slice_pair[:, :], start=True, stop=False)
                last = mm(bank[5][0:1, m * P:(m + 1) * P], ones[0:1, 0:1], b_slice2[:, :], start=False, stop=True)
            last.then_inc(setup_psum, 1)
            for m in range(2, 5):
                pack_bits(m)
            pe.wait_ge(dve_consts, 1)
            open_sums()
            pe.sem_inc(swcur_free, 2)
            pe.sem_inc(xn_free, 2)
            pe.wait_ge(setup_done, 1)
            pe.wait_ge(weights_landed, 16 * N_WEIGHTS)

            def pair(b, i, prepare, finish, mixing):
                p = b * PAIRS + i
                for s in range(2):
                    n = 2 * p + s
                    pe.wait_ge(swt_kept, n + 1)
                    pe.wait_ge(xn_landed[s], 16 * (p + 1))
                    for k in range(2):
                        last = nc.tensor.transpose(bank[3][:, k * P:(k + 1) * P], xn_t[:, s, k * P:(k + 1) * P],
                                                   ident[:, :])
                    last.then_inc(xn_free, 1)
                    ending = to_finish(n, p, s) if finish else []
                    for m, slot, q in ending[:-1]:
                        pe.wait_ge(keys_ready, TOTAL)
                        pe.wait_ge(out_ready, m + 2)
                        finish_tile(m, slot, q + 1, b)
                    if mixing and (2 * i + s, 0) in steps:
                        pe.wait_ge(norm_used, n)
                        mix_steps(b, i, s, 0)
                    pe.wait_ge(agg_ready, n + 1)
                    for k in range(2):
                        last = nc.tensor.transpose(bank[3][:, (2 + k) * P:(3 + k) * P], agg_f[:, k * P:(k + 1) * P],
                                                   ident[:, :])
                    last.then_inc(h_psum, 1)
                    pe.wait_ge(h_ready, n + 1)
                    for k in range(4):
                        mm(bank[4][:, 0:C], h_t[:, k, :], wg[:, k, :], start=(k == 0), stop=False)
                    mm(bank[4][:, 0:C], ones[:, :], wg_b[:, :], start=False, stop=True).then_inc(gnn_psum, 1)
                    if finish:
                        pe.wait_ge(out_ready, ending[-1][0] + 2)
                    if exists(n + 5):
                        pack_bits(n + 5)
                    else:
                        pe.wait_ge(keys_ready, TOTAL)
                    for m, slot, q in ending[-1:]:
                        finish_tile(m, slot, q + 1, b - 1 if mixing else b)
                    if mixing:
                        mix_steps(b, i, s, 1)
                    if exists(n - 1):
                        add_slices(n - 1, 1 - s)
                    pe.wait_ge(xn2_ready, n + 1)
                    for k in range(2):
                        last = nc.tensor.transpose(bank[4][:, C + k * P:C + (k + 1) * P],
                                                   xn2[:, s, k * P:(k + 1) * P], ident[:, :])
                    last.then_inc(xn2t_psum, 1)
                    pe.wait_ge(xn2t_ready, n + 1)
                    for k in range(2):
                        mm(bank[5][:, :], xn2_t[:, k, :], wlog[:, k, :], start=(k == 0), stop=False)
                    mm(bank[5][:, :], ones[:, :], blog[:, :], start=False, stop=True).then_inc(logits_psum, 1)
                    if mixing and (2 * i + s, 2) in steps:
                        pe.wait_ge(norm_used, n + 1)
                        mix_steps(b, i, s, 2)

            def close_sums(done):
                for k in range(2):
                    last = mm(bank[k][:, :], zeros[0:1, 0:P], zeros[0:1, 0:1].to_broadcast([1, DI]), start=False,
                              stop=True, skip_group_check=True)
                last.then_inc(sums_psum, 1)

            def slice_tokens(done):
                pe.wait_ge(sums_copied, 2 * done)
                if not isinstance(done, int) or done < B:
                    open_sums()
                for h in range(H):
                    cols = slice(h * HP, (h + 1) * HP)
                    for k in range(2):
                        mm(bank[2][0:G, cols], tok_sum[:, k, cols], wfx[:, k, cols], start=(k == 0), stop=(k == 1))
                for j in range(2):
                    last = mm(bank[6][0:G, 0:H].rearrange("p (m j) -> p j m", j=2)[:, j, :],
                              ident[:, j * G:(j + 1) * G], snorm[:, :], start=True, stop=True)
                last.then_inc(slices_psum, 1)

            def turn_tokens(done):
                pe.wait_ge(u_ready, done)
                for k in range(4):
                    last = turn(bank[6][:, k * G:(k + 1) * G], u[:, k * P:(k + 1) * P], G)
                last.then_inc(ut_psum, 1)

            def project_xbc(done):
                pe.wait_ge(ut_ready, done)
                for dst, c0, c1 in ((bank[2][0:G, :], DI, 2 * DI), (bank[6][0:G, 0:2 * NS], 2 * DI, DI + CONV)):
                    for k in range(4):
                        last = mm(dst, u_t[:, k, :], w_in[:, k, c0:c1], start=(k == 0), stop=(k == 3))
                last.then_inc(v_psum, 1)

            def project_gate(done):
                pe.wait_ge(v3_ready, done)
                for k in range(4):
                    mm(bank[6][0:G, P:P + G], w_dt[:, k, :], u_t[:, k, :], start=(k == 0), stop=(k == 3))
                for k in range(4):
                    last = mm(bank[2][0:G, :], u_t[:, k, :], w_in[:, k, 0:DI], start=(k == 0), stop=(k == 3))
                last.then_inc(zdt_psum, 1)

            def convolve(done):
                pe.wait_ge(z_used, done)
                for dst, c0, c1 in ((bank[2][:, :], 0, DI), (bank[6][:, 0:2 * NS], DI, CONV)):
                    for k in range(K3):
                        mm(dst, shift[:, k, :], v3[:, k, c0:c1], start=(k == 0), stop=False)
                    last = mm(dst, ones[:, :], convb[:, c0:c1], start=False, stop=True)
                last.then_inc(conv_psum, 1)

            def spread(done):
                pe.wait_ge(decay_ready, done)
                pe.wait_ge(xbc_ready, done)
                for h in range(H):
                    mm(bank[2][:, h * G:(h + 1) * G], head_sel[:, h, :], decay[:, :], start=True, stop=True)
                mm(bank[6][:, 256:256 + H], dt_blocks[:, :], head_of_row[:, :], start=True, stop=True)
                for j in range(2):
                    last = turn(bank[6][0:G, j * P:(j + 1) * P], xbc[:, DI + j * NS:DI + (j + 1) * NS])
                last.then_inc(spread_psum, 1)

            def correlate(done):
                pe.wait_ge(scanned, done)
                pe.wait_ge(spread_copied, done)
                for k in range(4):
                    turn(bank[2][:, k * G:(k + 1) * G], xbc[0:G, k * P:(k + 1) * P], G)
                mm(bank[6][:, 264:264 + P], bc_t[:, 0:P], bc_t[:, P:2 * P], start=True, stop=True
                   ).then_inc(gram_psum, 1)

            def outputs(done):
                pe.wait_ge(xs_copied, done)
                pe.wait_ge(wmix_ready, done)
                for k in range(4):
                    mm(bank[6][0:G, 400:400 + H], xs_t[:, k, :], fcd[:, k, :], start=(k == 0), stop=False)
                mm(bank[6][0:G, 400:400 + H], ones[0:1, 0:G], dskip[:, :], start=False, stop=True)
                for h in range(H):
                    last = mm(bank[2][0:G, h * HP:(h + 1) * HP], w_mix[:, h, :], xbc[:, h * HP:(h + 1) * HP],
                              start=True, stop=True)
                last.then_inc(y_psum, 1)

            def turn_outputs(done):
                pe.wait_ge(yg_ready, done)
                for k in range(4):
                    last = turn(bank[6][:, k * G:(k + 1) * G], yg[:, k * P:(k + 1) * P], G)
                last.then_inc(ygt_psum, 1)

            def project_out(done):
                pe.wait_ge(ygt_ready, done)
                for m in range(4):
                    for k in range(4):
                        last = mm(bank[2][:, m * G:(m + 1) * G], w_hyout[:, k, m * P:(m + 1) * P], yg_t[:, k, :],
                                  start=(k == 0), stop=(k == 3))
                last.then_inc(ot_psum, 1)

            def make_mix(done):
                pe.wait_ge(ot_ready, done)
                for m in range(3):
                    dst = bank[2][:, m * C:(m + 1) * C] if m < 2 else bank[6][:, 0:C]
                    last = mm(dst, ot_pair[:, m, :], w_out[:, m, :], start=True, stop=True)
                last.then_inc(mix_psum, 1)

            def end_mix(done):
                pe.wait_ge(mix_half, done)
                mm(bank[2][:, 0:C], ot_pair[:, 3, :], w_out[:, 3, :], start=True, stop=True).then_inc(mix3_psum, 1)

            steps = {(0, 2): (close_sums,), (1, 1): (slice_tokens,), (2, 0): (turn_tokens,), (2, 1): (project_xbc,),
                     (3, 0): (project_gate,), (4, 1): (convolve,), (5, 1): (spread,), (6, 0): (correlate,),
                     (6, 2): (outputs,), (7, 1): (turn_outputs,), (8, 0): (project_out,), (9, 0): (make_mix,),
                     (9, 2): (end_mix,)}

            def mix_steps(b, i, s, point):
                for step in steps.get((2 * i + s, point), ()):
                    step(b)

            over_batches(pe, pair)
            add_slices(TOTAL - 1, 1)
            pe.wait_ge(norm_used, TOTAL + 1)
            for at in sorted(steps):
                for step in steps[at]:
                    step(B)
                for m in left_made.get(at, ()):
                    pe.wait_ge(out_ready, m + 2)
                    finish_tile(m, m % 2, m // 2 + 1, B - 1)
            pe.wait_ge(mix_ready, B)
            pe.wait_ge(swt_kept, TOTAL + 2)
            for j in range(TILES):
                if j % CHUNK == 0:
                    pe.wait_ge(last_landed[j // CHUNK], 32)
                pe.wait_ge(out_ready, max(TOTAL - TILES + j - 4 + 3, TOTAL - TILES + 2))
                for k in range(4):
                    last = mm(bank[LAST_BANKS[j % 4]][:, 0:C], last_sw[:, j, k * P:(k + 1) * P], mix[:, k, :],
                              start=(k == 0), stop=(k == 3))
                last.then_inc(final_psum, 1)


def kernel(x, adj, L0_gnn_W, L0_gnn_b, L0_ffn_W_fx, L0_ffn_b_fx, L0_ffn_W_x, L0_ffn_b_x, L0_ffn_W_slice,
           L0_ffn_b_slice, L0_ffn_temperature, L0_ffn_hy_in_w, L0_ffn_hy_conv_w, L0_ffn_hy_conv_b,
           L0_ffn_hy_dt_bias, L0_ffn_hy_A_log, L0_ffn_hy_D, L0_ffn_hy_fcD_w, L0_ffn_hy_norm_w,
           L0_ffn_hy_out_w, L0_ffn_out_w, L0_ffn_out_b):
    import numpy as np
    import concourse.bacc as bacc
    from concourse.bass_utils import run_bass_kernel_spmd

    a = np.asarray
    arrays = {
        "x": a(x), "adj": a(adj), "gnn_w": a(L0_gnn_W), "gnn_b": a(L0_gnn_b).reshape(1, -1),
        "wfx_t": a(L0_ffn_W_fx).T, "b_fx": a(L0_ffn_b_fx), "w_x": a(L0_ffn_W_x),
        "b_x": a(L0_ffn_b_x).reshape(4, 128).T, "wslice_t": a(L0_ffn_W_slice).T,
        "b_slice": a(L0_ffn_b_slice).reshape(1, -1), "temperature": a(L0_ffn_temperature).reshape(-1),
        "in_w_t": a(L0_ffn_hy_in_w).T, "conv_w": a(L0_ffn_hy_conv_w).reshape(-1),
        "conv_b": a(L0_ffn_hy_conv_b).reshape(1, -1), "dt_bias": a(L0_ffn_hy_dt_bias).reshape(-1, 1),
        "a_log": a(L0_ffn_hy_A_log).reshape(-1, 1), "d_skip": a(L0_ffn_hy_D).reshape(1, -1),
        "fcd_t": a(L0_ffn_hy_fcD_w).T, "norm_w": a(L0_ffn_hy_norm_w).reshape(4, 128).T,
        "hyout_t": a(L0_ffn_hy_out_w).T, "out_w_t": a(L0_ffn_out_w).T, "out_b": a(L0_ffn_out_b).reshape(1, -1),
    }
    nc = bacc.Bacc("TRN2", target_bir_lowering=False, num_devices=1)
    inputs, args = {}, {}
    for name, array in arrays.items():
        inputs[f"in_{name}"] = np.ascontiguousarray(array)
        args[name] = nc.dram_tensor(f"in_{name}", array.shape, mybir.dt.from_np(array.dtype),
                                    kind="ExternalInput").ap()
    args["out"] = nc.dram_tensor("out_x", (B, N, C), F32, kind="ExternalOutput").ap()
    adj_ffn(nc, **args)
    run = run_bass_kernel_spmd(nc, [inputs], core_ids=[0])
    return run.results[0]["out_x"]
```
